# Optimizing a Trainium2 kernel written in Bass

```python
import numpy as np
import jax
import jax.numpy as jnp

def _softmax(x, axis=-1):
    return jax.nn.softmax(x, axis=axis)

def _gelu(x):
    return jax.nn.gelu(x, approximate=True)

def _silu(x):
    return jax.nn.silu(x)

def _sigmoid(x):
    return jax.nn.sigmoid(x)

def _layernorm(x, axis=-1, eps=1e-05):
    m = jnp.mean(x, axis=axis, keepdims=True)
    v = jnp.var(x, axis=axis, keepdims=True)
    return (x - m) / jnp.sqrt(v + eps)

def _scatter_add(tgt, idx, src, axis=0):
    return tgt.at[idx].add(src)

def _segment_sum(src, seg, n):
    return jax.ops.segment_sum(src, seg, n)
kernel_name = 'mk_gps_d1_gnn_r8_e59178'

def setup_inputs(seed: int=0):
    np.random.seed(seed)
    _w = jnp.asarray

    def _rec_inputs():
        import jax
        import jax.numpy as jnp
        _gk = jax.random.key(seed)
        x = -0.0003713 + 1 * jax.random.normal(jax.random.fold_in(_gk, 1), (6250, 256), jnp.float32)
        _s = jax.random.randint(jax.random.fold_in(_gk, 2), (100000,), 0, 6250, jnp.int32)
        _d = jax.random.randint(jax.random.fold_in(_gk, 3), (100000,), 0, 6250, jnp.int32)
        _loop = jnp.arange(6250, dtype=jnp.int32)
        src = jnp.concatenate([_s, _d, _loop])
        dst = jnp.concatenate([_d, _s, _loop])
        _o = jnp.argsort(dst, stable=True)
        src = src[_o]
        dst = dst[_o]
        return (x, src, dst)
    x, src, dst = _rec_inputs()

    def _L0_gnn_setup():
        import jax, jax.numpy as jnp
        import numpy as np
        N = 6250
        E = 100000
        D = 256
        SMALL = 25
        key = jax.random.key(seed)
        k1, k2, k3, k4, k5 = jax.random.split(key, 5)
        x = jax.random.normal(k1, (N, D), jnp.float32)
        src = jax.random.randint(k2, (E,), 0, N)
        dst = jax.random.randint(k3, (E,), 0, N)
        Wq = jax.random.normal(k4, (D, SMALL), jnp.float32) / np.float32(np.sqrt(D))
        bq = jnp.zeros((SMALL,), jnp.float32)
        Wk = jax.random.normal(k5, (D, SMALL), jnp.float32) / np.float32(np.sqrt(D))
        bk = jnp.zeros((SMALL,), jnp.float32)
        return {'x': x, 'src': src, 'dst': dst, 'Wq': Wq, 'bq': bq, 'Wk': Wk, 'bk': bk}
    _L0_gnn_all = _L0_gnn_setup()
    _L0_gnn_in = {k: v for k, v in _L0_gnn_all.items() if k in ('Wq', 'bq', 'Wk', 'bk')}
    del _L0_gnn_all

    def _L0_mix_setup():
        import jax, jax.numpy as jnp
        import numpy as np
        D_MODEL = 256
        NHEAD = 8
        D_HEAD = D_MODEL // NHEAD
        DIM_FF = 1024
        B, L = (4, 2048)
        LN_EPS = 1e-05

        def _layernorm(x, g, b):
            mu = jnp.mean(x, axis=-1, keepdims=True)
            var = jnp.mean((x - mu) ** 2, axis=-1, keepdims=True)
            return (x - mu) * jax.lax.rsqrt(var + LN_EPS) * g + b

        def _phi(x):
            return jnp.where(x > 0, x + 1.0, jnp.exp(x))
        key = jax.random.key(seed)
        ks = jax.random.split(key, 16)
        s_in = 1.0 / np.sqrt(D_MODEL)
        s_ff = 1.0 / np.sqrt(DIM_FF)
        inp = {'x': jax.random.normal(ks[0], (B, L, D_MODEL), dtype=jnp.float32), 'Wq': jax.random.normal(ks[1], (D_MODEL, D_MODEL), dtype=jnp.float32) * s_in, 'bq': jnp.zeros((D_MODEL,), jnp.float32), 'Wk': jax.random.normal(ks[2], (D_MODEL, D_MODEL), dtype=jnp.float32) * s_in, 'bk': jnp.zeros((D_MODEL,), jnp.float32), 'Wv': jax.random.normal(ks[3], (D_MODEL, D_MODEL), dtype=jnp.float32) * s_in, 'bv': jnp.zeros((D_MODEL,), jnp.float32), 'Wo': jax.random.normal(ks[4], (D_MODEL, D_MODEL), dtype=jnp.float32) * s_in, 'bo': jnp.zeros((D_MODEL,), jnp.float32), 'W1': jax.random.normal(ks[5], (D_MODEL, DIM_FF), dtype=jnp.float32) * s_in, 'b1': jnp.zeros((DIM_FF,), jnp.float32), 'W2': jax.random.normal(ks[6], (DIM_FF, D_MODEL), dtype=jnp.float32) * s_ff, 'b2': jnp.zeros((D_MODEL,), jnp.float32), 'ln1_g': jnp.ones((D_MODEL,), jnp.float32), 'ln1_b': jnp.zeros((D_MODEL,), jnp.float32), 'ln2_g': jnp.ones((D_MODEL,), jnp.float32), 'ln2_b': jnp.zeros((D_MODEL,), jnp.float32)}
        return inp
    _L0_mix_all = _L0_mix_setup()
    _L0_mix_in = {k: v for k, v in _L0_mix_all.items() if k in ('Wq', 'bq', 'Wk', 'bk', 'Wv', 'bv', 'Wo', 'bo', 'W1', 'b1', 'W2', 'b2', 'ln1_g', 'ln1_b', 'ln2_g', 'ln2_b')}
    del _L0_mix_all

    def _L0_ffn_setup():
        import jax, jax.numpy as jnp
        import numpy as np
        NUM_EXPERTS = 8
        TOP_K = 2
        B, S, D = (8, 1024, 256)

        def _moe(tokens, router_w, w1, b1, w2, b2):
            N = tokens.shape[0]
            E = router_w.shape[0]
            logits = tokens.astype(jnp.float32) @ router_w.astype(jnp.float32).T
            probs = jax.nn.softmax(logits, axis=-1)
            rw, re = jax.lax.top_k(probs, TOP_K)
            if TOP_K > 1:
                rw = rw / jnp.maximum(rw.sum(-1, keepdims=True), 1e-12)
            rw = rw.astype(tokens.dtype)
            combine = jnp.zeros((N, E), tokens.dtype).at[jnp.arange(N)[:, None], re].set(rw)
            out = tokens
            for e in range(E):
                h = jax.nn.gelu(tokens @ w1[e] + b1[e], approximate=False)
                y = h @ w2[e] + b2[e]
                out = out + combine[:, e:e + 1] * y
            return out
        key = jax.random.key(seed)
        ks = jax.random.split(key, 4)
        scale = 1.0 / np.sqrt(D).astype(np.float32)
        return {'input_embeddings': jax.random.normal(ks[0], (B, S, D), jnp.float32), 'router_w': jax.random.normal(ks[1], (NUM_EXPERTS, D), jnp.float32) * scale, 'w1': jax.random.normal(ks[2], (NUM_EXPERTS, D, D), jnp.float32) * scale, 'b1': jnp.zeros((NUM_EXPERTS, D), jnp.float32), 'w2': jax.random.normal(ks[3], (NUM_EXPERTS, D, D), jnp.float32) * scale, 'b2': jnp.zeros((NUM_EXPERTS, D), jnp.float32)}
    _L0_ffn_all = _L0_ffn_setup()
    _L0_ffn_in = {k: v for k, v in _L0_ffn_all.items() if k in ('router_w', 'w1', 'b1', 'w2', 'b2')}
    del _L0_ffn_all
    return {'x': x, 'src': src, 'dst': dst, 'L0_gnn_Wq': _L0_gnn_in['Wq'], 'L0_gnn_bq': _L0_gnn_in['bq'], 'L0_gnn_Wk': _L0_gnn_in['Wk'], 'L0_gnn_bk': _L0_gnn_in['bk'], 'L0_mix_Wq': _L0_mix_in['Wq'], 'L0_mix_bq': _L0_mix_in['bq'], 'L0_mix_Wk': _L0_mix_in['Wk'], 'L0_mix_bk': _L0_mix_in['bk'], 'L0_mix_Wv': _L0_mix_in['Wv'], 'L0_mix_bv': _L0_mix_in['bv'], 'L0_mix_Wo': _L0_mix_in['Wo'], 'L0_mix_bo': _L0_mix_in['bo'], 'L0_mix_W1': _L0_mix_in['W1'], 'L0_mix_b1': _L0_mix_in['b1'], 'L0_mix_W2': _L0_mix_in['W2'], 'L0_mix_b2': _L0_mix_in['b2'], 'L0_mix_ln1_g': _L0_mix_in['ln1_g'], 'L0_mix_ln1_b': _L0_mix_in['ln1_b'], 'L0_mix_ln2_g': _L0_mix_in['ln2_g'], 'L0_mix_ln2_b': _L0_mix_in['ln2_b'], 'L0_ffn_router_w': _L0_ffn_in['router_w'], 'L0_ffn_w1': _L0_ffn_in['w1'], 'L0_ffn_b1': _L0_ffn_in['b1'], 'L0_ffn_w2': _L0_ffn_in['w2'], 'L0_ffn_b2': _L0_ffn_in['b2']}

def reference(x, src, dst, L0_gnn_Wq, L0_gnn_bq, L0_gnn_Wk, L0_gnn_bk, L0_mix_Wq, L0_mix_bq, L0_mix_Wk, L0_mix_bk, L0_mix_Wv, L0_mix_bv, L0_mix_Wo, L0_mix_bo, L0_mix_W1, L0_mix_b1, L0_mix_W2, L0_mix_b2, L0_mix_ln1_g, L0_mix_ln1_b, L0_mix_ln2_g, L0_mix_ln2_b, L0_ffn_router_w, L0_ffn_w1, L0_ffn_b1, L0_ffn_w2, L0_ffn_b2):
    import jax
    import jax.numpy as jnp

    def _L0_gnn_ref(x, src, dst, Wq, bq, Wk, bk):
        import jax, jax.numpy as jnp
        import numpy as np
        N = 6250
        E = 100000
        D = 256
        SMALL = 25
        d_k = np.float32(np.sqrt(SMALL))
        q = jnp.tanh(x @ Wq + bq)
        k = x @ Wk + bk
        loop = jnp.arange(N, dtype=src.dtype)
        s = jnp.concatenate([src, loop])
        d = jnp.concatenate([dst, loop])
        w = jnp.sum(q[s] * k[d], axis=1) / d_k
        wmax = jax.ops.segment_max(w, d, num_segments=N)
        ew = jnp.exp(w - wmax[d])
        denom = jax.ops.segment_sum(ew, d, num_segments=N)
        alpha = ew / denom[d]
        out = jax.ops.segment_sum(alpha[:, None] * x[s], d, num_segments=N)
        return out

    def _L0_mix_ref(x, Wq, bq, Wk, bk, Wv, bv, Wo, bo, W1, b1, W2, b2, ln1_g, ln1_b, ln2_g, ln2_b):
        import jax, jax.numpy as jnp
        import numpy as np
        D_MODEL = 256
        NHEAD = 8
        D_HEAD = D_MODEL // NHEAD
        DIM_FF = 1024
        B, L = (4, 2048)
        LN_EPS = 1e-05

        def _layernorm(x, g, b):
            mu = jnp.mean(x, axis=-1, keepdims=True)
            var = jnp.mean((x - mu) ** 2, axis=-1, keepdims=True)
            return (x - mu) * jax.lax.rsqrt(var + LN_EPS) * g + b

        def _phi(x):
            return jnp.where(x > 0, x + 1.0, jnp.exp(x))
        Bq, Lq, _ = x.shape
        q = (x @ Wq + bq).reshape(Bq, Lq, NHEAD, D_HEAD)
        k = (x @ Wk + bk).reshape(Bq, Lq, NHEAD, D_HEAD)
        v = (x @ Wv + bv).reshape(Bq, Lq, NHEAD, D_HEAD)
        q_phi = _phi(q)
        k_phi = _phi(k)
        kv = jnp.einsum('blhd,blhe->bhde', k_phi, v)
        k_sum = k_phi.sum(axis=1)
        z = 1.0 / (jnp.einsum('blhd,bhd->blh', q_phi, k_sum) + 1e-06)
        out = jnp.einsum('blhd,bhde,blh->blhe', q_phi, kv, z)
        out = out.reshape(Bq, Lq, D_MODEL) @ Wo + bo
        x = _layernorm(x + out, ln1_g, ln1_b)
        ff = jax.nn.relu(x @ W1 + b1) @ W2 + b2
        x = _layernorm(x + ff, ln2_g, ln2_b)
        return x

    def _L0_ffn_ref(input_embeddings, router_w, w1, b1, w2, b2):
        import jax, jax.numpy as jnp
        import numpy as np
        NUM_EXPERTS = 8
        TOP_K = 2
        B, S, D = (8, 1024, 256)

        def _moe(tokens, router_w, w1, b1, w2, b2):
            N = tokens.shape[0]
            E = router_w.shape[0]
            logits = tokens.astype(jnp.float32) @ router_w.astype(jnp.float32).T
            probs = jax.nn.softmax(logits, axis=-1)
            rw, re = jax.lax.top_k(probs, TOP_K)
            if TOP_K > 1:
                rw = rw / jnp.maximum(rw.sum(-1, keepdims=True), 1e-12)
            rw = rw.astype(tokens.dtype)
            combine = jnp.zeros((N, E), tokens.dtype).at[jnp.arange(N)[:, None], re].set(rw)
            out = tokens
            for e in range(E):
                h = jax.nn.gelu(tokens @ w1[e] + b1[e], approximate=False)
                y = h @ w2[e] + b2[e]
                out = out + combine[:, e:e + 1] * y
            return out
        b, s, d = input_embeddings.shape
        tokens = input_embeddings.reshape(b * s, d)
        return _moe(tokens, router_w, w1, b1, w2, b2).reshape(b, s, d)
    xn = _layernorm(x, axis=-1)
    x = x + _L0_gnn_ref(xn, src, dst, L0_gnn_Wq, L0_gnn_bq, L0_gnn_Wk, L0_gnn_bk) + _L0_mix_ref(xn[None], L0_mix_Wq, L0_mix_bq, L0_mix_Wk, L0_mix_bk, L0_mix_Wv, L0_mix_bv, L0_mix_Wo, L0_mix_bo, L0_mix_W1, L0_mix_b1, L0_mix_W2, L0_mix_b2, L0_mix_ln1_g, L0_mix_ln1_b, L0_mix_ln2_g, L0_mix_ln2_b)[0]
    x = x + _L0_ffn_ref(_layernorm(x, axis=-1)[None], L0_ffn_router_w, L0_ffn_w1, L0_ffn_b1, L0_ffn_w2, L0_ffn_b2)[0]
    return x

_drawn_inputs = setup_inputs


def setup_inputs(seed=0):
    import zlib

    import numpy as np

    out = dict(_drawn_inputs(seed))
    spreads = {'L0_gnn_bq': (0.0, 0.8),
     'L0_gnn_bk': (0.0, 0.589),
     'L0_mix_bq': (0.0, 0.8),
     'L0_mix_bk': (0.0, 0.8),
     'L0_mix_bv': (0.0, 0.1),
     'L0_mix_bo': (0.0, 0.1),
     'L0_mix_b1': (0.0, 0.1),
     'L0_mix_b2': (0.0, 0.1),
     'L0_mix_ln1_g': (1.0, 0.2),
     'L0_mix_ln1_b': (0.0, 0.1),
     'L0_mix_ln2_g': (1.0, 0.2),
     'L0_mix_ln2_b': (0.0, 0.1),
     'L0_ffn_b1': (0.0, 0.478),
     'L0_ffn_b2': (0.0, 0.323)}
    factors = {'L0_mix_Wq': 8.0, 'L0_mix_Wk': 6.074, 'L0_mix_Wv': 4.792}
    for name, (base, spread) in spreads.items():
        noise = np.random.default_rng([zlib.crc32(name.encode()), seed]).standard_normal(out[name].shape)
        drawn = base * np.exp(spread * noise) if base else spread * noise
        out[name] = jnp.asarray(drawn.astype(out[name].dtype))
    for name, factor in factors.items():
        out[name] = (out[name] * factor).astype(out[name].dtype)
    return out
```

```python
from contextlib import ExitStack

import numpy as np

import concourse.bass as bass
from concourse import mybir

F32 = mybir.dt.float32
BF16 = mybir.dt.bfloat16
I32 = mybir.dt.int32
U32 = mybir.dt.uint32
ALU = mybir.AluOpType
ACT = mybir.ActivationFunctionType
AX = mybir.AxisListType

P = 128
NODES, D = 6250, 256
NB = (NODES + P - 1) // P
NPAD = NB * P
LAST = NODES - (NB - 1) * P
EDGES = 206250
TPP = 13
NT = TPP * P
CH = 36
GT = 6
NG = CH // GT
PT = 4
NP = CH // PT
RING = 3
SM = 25
ROW = 288
C1, CQ, CW = D, D + 1, D + 1 + SM
AGG = D + 1
HEADS, HD = 8, 32
FF = 1024
FC = FF // P
EXP = 8
EPS = 1e-5
D_CHAIN = 70
BIG = float(2.0 ** 100)
FAR = 1 << 14

R_BK, R_BV, R_BO, R_G1, R_B1, R_G2, R_B2, R_F2 = [D * i for i in range(8)]
R_BQK = 8 * D
R_END = R_BQK + 2 * SM
V_BQ, V_FB1, V_EB1 = 0, 2, 2 + FC
V_END = V_EB1 + 2 * EXP


def at(signal, step, n=None):
    _, per = signal
    return step * per + (per if n is None else n)


def chain_of(eng, signal, step, fence=None):
    semaphore, per = signal
    count = [0]

    def tick(ins):
        count[0] += 1
        ins.then_inc(semaphore, 1)
        return count[0]

    def wait(n=None):
        eng.wait_ge(semaphore, at(signal, step, count[0] if n is None else n))

    def link(ins, hold=False):
        tick(ins)
        wait()
        if hold:
            fence()

    def close():
        assert count[0] == per, (count[0], per)

    return tick, wait, link, close


def graph_block(nc, xpad, src_t, dst_t, dst_n, rowvec, colvec, wqk, wq, wkv, wo, w1, w2, rw, ew1, ew2, eb2, out):
    ctx = ExitStack()
    with ctx:
        def sb(name, shape, dt=F32):
            return ctx.enter_context(nc.sbuf_tensor(name, shape, dt))

        def ps(name, shape, dt=F32):
            return ctx.enter_context(nc.psum_tensor(name, shape, dt))

        def sem(name):
            return ctx.enter_context(nc.semaphore(name))

        def sig(name, per=1):
            return sem(name), per

        table = nc.dram_tensor("node_table", (NPAD, ROW), F32).ap()
        knode = nc.dram_tensor("node_keys", (NPAD, 3 * SM), BF16).ap()
        tile_rng = nc.dram_tensor("tile_range", (2, NT), F32).ap()
        blk_rng = nc.dram_tensor("block_range", (2, P), I32).ap()

        rows = sb("gathered_rows", [P, 2, CH, ROW])
        flat = rows[:, :, :, :].rearrange("p a b c -> p (a b c)")
        xall = flat[:, 0:NB * D].rearrange("p (b d) -> p b d", d=D)
        o = NB * D
        t_max, t_min, t_idx, t_tmp = [flat[:, o + i * NT:o + (i + 1) * NT] for i in range(4)]
        farm = sb("far_mask", [P, CH, P], BF16)
        onehot = sb("onehot_t", [P, CH, P], BF16)
        wgt = sb("weights", [P, RING * PT, P])
        mx = sb("max_partial", [P, GT, P])
        mxr = sb("max_rows", [P, P])
        prod = sb("score_products", [P, GT, 3 * SM])
        score = sb("scores", [P, CH])
        ebias = sb("exp_bias", [P, CH])
        src_i = sb("src_idx", [P, 2, CH], I32)
        dst_i = sb("dst_idx", [P, 2, CH], I32)
        dloc = sb("dst_local", [P, CH])
        base = sb("block_base", [P, 1])
        kcur = sb("block_keys", [P, 2, 3 * SM], BF16)
        own = sb("own_rows", [P, 2, ROW])
        acc = sb("aggregate", [P, 2, AGG])
        shift2 = sb("shift_parts", [P, 2], BF16)
        sm = sb("softmax_cols", [P, 8])
        iota_b = sb("iota_b", [P, P], BF16)
        identf = sb("ident_f", [P, P])
        identb = sb("ident_b", [P, P], BF16)
        zero = acc[:, :, :].rearrange("p a b -> p (a b)")[:, 0:2 * (P + 1)]
        ctl = sb("control", [1, 2 * P], I32)
        cols = sb("range_cols", [P, 8])
        coli = sb("range_cols_i", [P, 2], I32)
        chunk_steps = sb("chunk_steps", [P, 48])
        s_wqk = sb("w_graph_qk", [P, 2, 2 * SM])
        s_wq = sb("w_mix_q", [P, 2, D])
        s_wkv = sb("w_mix_kv", [P, 2, 2 * D])
        s_wo = sb("w_mix_o", [P, 2, D])
        s_w1 = sb("w_ff1", [P, 2, FF])
        s_w2 = sb("w_ff2", [P, FC, D])
        s_rw = sb("w_router", [P, 2, EXP])
        s_e1 = sb("w_expert1", [P, EXP, 2, D])
        s_e2 = sb("w_expert2", [P, EXP, 2, D])
        s_eb2 = sb("b_expert2", [EXP, D])
        rv = sb("row_vectors", [P, R_END])
        cv = sb("col_vectors", [P, V_END])
        bq1 = sb("bq_plus_1", [P, 2])
        o += 4 * NT
        st = flat[:, o:o + 6 * NB].rearrange("p (b s) -> p b s", s=6)
        lnm = flat[:, o + 6 * NB:o + 12 * NB].rearrange("p (s b) -> p s b", s=6)
        nrow = flat[:, o + 12 * NB:o + 12 * NB + 2 * ROW].rearrange("p (a c) -> p a c", a=2)
        krow = sb("node_key_parts", [P, 2, 3 * SM], BF16)
        wflat = wgt[:, :, :].rearrange("p a b -> p (a b)")
        kb, km, kphi = [wflat[:, i * 2 * D:(i + 1) * 2 * D].rearrange("p (a b) -> p a b", a=2) for i in range(3)]
        vaug = mx[:, :, :].rearrange("p a b -> p (a b)")[:, 0:4 * (P + 1)].rearrange("p (a b c) -> p a b c", a=2, b=2)
        dn = onehot[:, 0:2 * TPP, :].rearrange("p a b -> p (a b)").bitcast(I32).rearrange("p (a b) -> p a b", b=P)
        iota_i = farm[:, 0:2 * TPP, :].rearrange("p a b -> p (a b)").bitcast(I32)
        qkb = sb("qk_biased", [P, 2, 2 * SM])
        kf = sb("k_fifth", [P, SM])
        kr = sb("k_rest", [P, 2, SM])
        qkp = sb("qk_product", [P, SM])
        kvm = sb("kv_blocks", [P, 2, P + 4])
        xd = sb("block_x", [P, 2, 2, D])
        xt = sb("xn_t", [P, 2, P])
        qm = sb("q_min", [P, 2, P])
        qphi = sb("q_phi", [P, 2, P])
        den = sb("attn_den", [P, 2, HEADS])
        att = sb("attn", [P, D])
        y1 = sb("y1", [P, D])
        x1 = sb("x1", [P, D])
        hff = sb("h_ff", [P, FC, P])
        xt0 = hff[:, 0:4, :].rearrange("p a b -> p (a b)").rearrange("p (a b) -> p a b", a=2)
        xr = sb("x_res", [P, D])
        xm = sb("x_moe", [P, D])
        hex_ = hff[:, :, :].rearrange("p (a b c) n -> p a b c n", a=2, b=2)
        res = sb("result", [P, 2, D])
        lns = sb("ln_small", [P, 3, 12])
        rt = sb("router", [P, 4, EXP])
        rts = sb("router_small", [P, 8])
        ridx = sb("router_idx", [P, 8], U32)
        ct = sb("combine_t", [EXP, P])
        iota8 = sb("iota8", [P, EXP])
        rl = sb("inv_sum", [P, 1])

        b_t = [ps(f"bank_t{i}", [P, GT, P], BF16) for i in range(2)]
        b_s = ps("bank_scores", [P, 512])
        b_m = ps("bank_max", [P, 512])
        b_a = ps("bank_agg", [P, 512])
        b_d = [ps(f"bank_d{i}", [P, 512]) for i in range(3)]
        tr_ps = [b_s, b_m]
        kv_ps = [b_d[0], b_d[1]]
        qk_ps = [b_d[2][:, 0:2 * SM], b_d[2][:, 64:64 + 2 * SM]]
        kva_ps = b_a[:, 0:2 * (P + 1)].rearrange("p (c n) -> p c n", c=2)

        s_wload, s_xload, s_dn = sem("weights_loaded"), sem("x_loaded"), sem("dst_tiles_loaded")
        s_const = sem("constants_ready")
        s_pool = sem("pool_constants_ready")
        s_rng_w, s_rng_r, s_trng = sem("tile_range_stored"), sem("tile_range_loaded"), sem("tile_range_ready")
        s_blk, s_blk_w, s_ctl = sem("block_range_ready"), sem("block_range_stored"), sem("control_loaded")
        s_set = sem("dve_setup_chain")
        s_kvz, s_kvm = sem("kv_zeroed"), sem("kv_blocks_ready")
        f_xn, f_tr, f_xt, f_kv = sig("f_xn_ready"), sig("f_transposed"), sig("f_xt_ready"), sig("f_kv_ready")
        f_km, f_ke, f_kphi, f_acc = sig("f_kmin_ready"), sig("f_kexp_ready"), sig("f_kphi_ready"), sig("f_kv_added")
        f_qkb, f_q, f_row = sig("f_qk_biased"), sig("f_q_ready"), sig("f_row_ready")
        f_st = [sem("f_rows_stored0"), sem("f_rows_stored1")]
        f_chain = sig("f_dve_chain", 7)

        def graph_signals(tag):
            return {
                "idx": [sem(f"{tag}_edges_loaded{i}") for i in range(2)],
                "key": [sem(f"{tag}_block_loaded{i}") for i in range(2)],
                "gat": [[sem(f"{tag}_rows_gathered{i}_{g}") for g in range(NG)] for i in range(2)],
                "far": sig(f"{tag}_far_mask_ready", NG),
                "tr": sig(f"{tag}_mask_transposed", NG),
                "oh": sig(f"{tag}_onehot_ready", NG),
                "ke": sig(f"{tag}_keys_spread", NG),
                "ku": sig(f"{tag}_keys_used", NG),
                "mx": sig(f"{tag}_max_rows_ready"),
                "mt": sig(f"{tag}_max_transposed"),
                "sh": sig(f"{tag}_shift_ready"),
                "me": sig(f"{tag}_shift_spread"),
                "eb": sig(f"{tag}_exp_bias_ready"),
                "es": sig(f"{tag}_old_scale_ready"),
                "w": sig(f"{tag}_weights_ready", NP),
                "wu": sig(f"{tag}_weights_used", NP),
                "agg": sig(f"{tag}_aggregate_ready"),
                "chain": sig(f"{tag}_dve_chain", 3 * NG + 8),
            }

        M = graph_signals("m")
        V = graph_signals("v")
        v_meet = sem("v_engines_meet")
        s_fence = sem("wait_carried")

        d_x = [sem("d_x_loaded0"), sem("d_x_loaded1")]
        d_out = [sem("d_out_stored0"), sem("d_out_stored1")]
        (d_t1, d_xt, d_q, d_qm, d_qe, d_qphi, d_at, d_att, d_t2, d_attT, d_o, d_x1, d_t3, d_x1T) = [
            sig("d_" + n) for n in ("xn_transposed", "xn_t_ready", "q_ready", "qmin_ready", "qexp_ready", "qphi_ready",
                                    "attn_ready", "attn_normed", "attn_transposed", "attn_t_ready", "wo_ready",
                                    "x1_ready", "x1_transposed", "x1_t_ready")]
        d_f1, d_h, d_f2, d_xm, d_t4, d_xmT = [
            sig("d_" + n, k) for n, k in (("ff1_ready", 2), ("relu_ready", 2), ("ff2_ready", 1), ("xm_ready", 1),
                                          ("xm_transposed", 1), ("xm_t_ready", 1))]
        d_lg, d_nm, d_re, d_cb, d_ct, d_ctT, d_cb2 = [
            sig("d_" + n) for n in ("logits_ready", "logit_max_ready", "router_exp_ready", "combine_ready",
                                    "combine_transposed", "combine_t_ready", "combine_b2_ready")]
        d_eh, d_eg, d_ey, d_eu = [sig("d_" + n, EXP // 2) for n in ("expert_h_ready", "expert_gelu_ready",
                                                                   "expert_y_ready", "expert_y_used")]
        d_done = sig("d_block_done")
        d_chain = sig("d_dve_chain", D_CHAIN)
        b_sig = sig("block_base_moved")

        def fence(eng):
            eng.sem_inc(s_fence, 1)

        def loop_steps(eng, first, step, last):
            first(0, 0, 0)
            with eng.Fori(0, (NB - 1) // 2) as i:
                step(i * 2 + 1, 1, i)
                step(i * 2 + 2, 0, i + 1)
            last(NB, 1, (NB - 1) // 2)

        def further_chunks(eng, block, body, counter):
            more = eng.value_load(ctl[0:1, bass.ds(block + P, 1)], min_val=0, max_val=NT // CH)
            with eng.If(more > 0):
                with eng.Fori(0, more) as c:
                    k = eng.snap(counter, min_val=0, max_val=NB * NT // CH)
                    eng.drain().then_inc(v_meet, 1)
                    eng.wait_ge(v_meet, k * 10 + 5)
                    fence(eng)
                    body(k, c)
                    eng.drain().then_inc(v_meet, 1)
                    eng.wait_ge(v_meet, k * 10 + 10)
                    fence(eng)
                    eng.reg_add(counter, counter, 1)

        block = ctx.enter_context(nc.Block())

        @block.sync
        def _(sp):
            sp.dma_start(dn[:, :, :], dst_n).then_inc(s_dn, 16)
            sp.dma_start(xall, xpad.rearrange("(b p) d -> p b d", p=P)).then_inc(s_xload, 16)
            sp.wait_ge(s_trng, 2)
            sp.dma_start(tile_rng[0].rearrange("(p c) -> p c", p=P), t_tmp[:, 0:TPP]).then_inc(s_rng_w, 16)
            sp.dma_start(tile_rng[1].rearrange("(p c) -> p c", p=P), t_tmp[:, TPP:2 * TPP]).then_inc(s_rng_w, 16)
            sp.wait_ge(s_rng_w, 32)
            sp.dma_start(t_max, tile_rng[0:1, :].broadcast_to([P, NT])).then_inc(s_rng_r, 16)
            sp.dma_start(t_min, tile_rng[1:2, :].broadcast_to([P, NT])).then_inc(s_rng_r, 16)
            sp.wait_ge(s_blk, 1)
            sp.dma_start(blk_rng[0], coli[:, 0]).then_inc(s_blk_w, 16)
            sp.dma_start(blk_rng[1], coli[:, 1]).then_inc(s_blk_w, 16)
            sp.wait_ge(s_blk_w, 32)
            sp.dma_start(ctl[0:1, :], blk_rng.rearrange("a b -> (a b)").unsqueeze(0)).then_inc(s_ctl, 16)

            def store_rows(b, par, h):
                sp.wait_ge(f_row[0], at(f_row, b))
                fence(sp)
                sp.dma_start(table[bass.ds(b * P, P), :], nrow[:, par, :]).then_inc(f_st[par], 16)
                sp.dma_start(knode[bass.ds(b * P, P), :], krow[:, par, :]).then_inc(f_st[par], 16)

            loop_steps(sp, store_rows, store_rows, lambda *a: None)
            sp.wait_ge(f_st[0], 32 * ((NB + 1) // 2))
            sp.wait_ge(f_st[1], 32 * (NB // 2))
            sp.wait_ge(s_ctl, 16)
            counter = sp.alloc_register("v_count_sp")
            sp.reg_mov(counter, 0)

            def load_edges(s, par, G, extra=0):
                lo = sp.value_load(ctl[0:1, bass.ds(s, 1)], min_val=0, max_val=EDGES // P)
                tile = nc.s_assert_within(lo + extra, 0, NT - CH, skip_runtime_bounds_check_because=(
                    "a chunk starts at one of its block's tiles, before the padding"))
                sp.dma_start(src_i[:, par, :], src_t[:, bass.ds(tile, CH)]).then_inc(G["idx"][par], 16)
                sp.dma_start(dst_i[:, par, :], dst_t[:, bass.ds(tile, CH)]).then_inc(G["idx"][par], 16)

            def load(s, par, h, first=False):
                if not first:
                    sp.wait_ge(M["wu"][0], at(M["wu"], s - 2))
                    fence(sp)
                    sp.wait_ge(M["agg"][0], at(M["agg"], s - 2))
                    fence(sp)
                load_edges(s, par, M)
                sp.dma_start(kcur[:, par, :], knode[bass.ds(s * P, P), :]).then_inc(M["key"][par], 16)
                sp.dma_start(own[:, par, :], table[bass.ds(s * P, P), :]).then_inc(M["key"][par], 16)

            def load_x(b, par):
                sp.dma_start(xd[:, par, 0, :], xpad[bass.ds(b * P, P), :]).then_inc(d_x[par], 16)
                sp.dma_start(xd[:, par, 1, :], table[bass.ds(b * P, P), 0:D]).then_inc(d_x[par], 16)

            def more(s, par):
                def body(k, c):
                    load_edges(s, par, V, (c + 1) * CH)
                further_chunks(sp, s, body, counter)

            def store(b, par):
                sp.wait_ge(d_done[0], at(d_done, b))
                fence(sp)
                sp.dma_start(out[bass.ds(b * P, P), :], res[:, par, :]).then_inc(d_out[par], 16)

            def step(s, par, h, ahead=True, nxt=True):
                more(s, par)
                if ahead:
                    load(s + 2, par, h + 1)
                store(s - 1, 1 - par)
                if nxt:
                    load_x(s + 1, 1 - par)

            load(0, 0, 0, True)
            load(1, 1, 0, True)
            load_x(0, 0)
            load_x(1, 1)
            more(0, 0)
            load(2, 0, 1)
            with sp.Fori(0, (NB - 3) // 2) as i:
                step(i * 2 + 1, 1, i)
                step(i * 2 + 2, 0, i + 1)
            step(NB - 2, 1, 0, ahead=False)
            step(NB - 1, 0, 0, ahead=False, nxt=False)
            store(NB - 1, 0)
            sp.wait_ge(d_out[0], 16 * ((NB + 1) // 2))
            sp.wait_ge(d_out[1], 16 * (NB // 2))

        @block.gpsimd
        def _(pool):
            nc.gpsimd.iota(iota_i[:, :], pattern=[[1, NT]], base=0, channel_multiplier=0).then_inc(s_pool, 1)
            nc.gpsimd.iota(coli[:, 0:1], pattern=[[0, 1]], base=0, channel_multiplier=P).then_inc(s_pool, 1)
            nc.gpsimd.memset(identf[:, :], 0.0).then_inc(s_pool, 1)
            pool.wait_ge(s_pool, 3)
            nc.gpsimd.affine_select(out=identf[:, :], in_=identf[:, :], compare_op=ALU.not_equal, fill=1.0, base=0,
                                    pattern=[[-1, P]], channel_multiplier=1).then_inc(s_pool, 1)
            counter = pool.alloc_register("v_count_pool")
            pool.reg_mov(counter, 0)
            pool.wait_ge(s_ctl, 16)
            pool.wait_ge(f_st[0], 32 * ((NB + 1) // 2))
            pool.wait_ge(f_st[1], 32 * (NB // 2))
            pool.wait_ge(s_blk, 1)

            def gather_chunk(par, G):
                for g in range(NG):
                    for j in range(g * GT, (g + 1) * GT):
                        nc.gpsimd.indirect_dma_start(
                            out=rows[:, par, j, :], out_offset=None, in_=table,
                            in_offset=bass.IndirectOffsetOnAxis(ap=src_i[:, par, j:j + 1], axis=0),
                        ).then_inc(G["gat"][par][g], 16)

            def gather(s, par, h, first=False):
                pool.wait_ge(M["idx"][par], h * 32 + 32)
                if not first:
                    pool.wait_ge(M["wu"][0], at(M["wu"], s - 2))
                fence(pool)
                gather_chunk(par, M)

            def more(s, par, vh):
                def body(k, c):
                    pool.wait_ge(V["idx"][par], pool.snap(vh[par], min_val=0, max_val=1 << 20) * 32 + 32)
                    fence(pool)
                    gather_chunk(par, V)
                    pool.reg_add(vh[par], vh[par], 1)
                further_chunks(pool, s, body, counter)

            vh = [pool.alloc_register(f"v_half_pool{i}") for i in range(2)]
            pool.reg_mov(vh[0], 0)
            pool.reg_mov(vh[1], 0)
            gather(0, 0, 0, True)
            gather(1, 1, 0, True)
            with pool.Fori(0, (NB - 3) // 2) as i:
                more(i * 2, 0, vh)
                gather(i * 2 + 2, 0, i + 1)
                more(i * 2 + 1, 1, vh)
                gather(i * 2 + 3, 1, i + 1)
            more(NB - 3, 0, vh)
            gather(NB - 1, 0, (NB - 1) // 2)
            more(NB - 2, 1, vh)
            more(NB - 1, 0, vh)

        @block.scalar
        def _(act):
            for dst, src in ((s_wqk, wqk), (s_wkv, wkv), (rv, rowvec.broadcast_to([P, R_END])), (cv, colvec),
                             (s_wq, wq), (s_wo, wo), (s_w1, w1), (s_w2, w2), (s_rw, rw), (s_e1, ew1), (s_e2, ew2),
                             (s_eb2, eb2)):
                full = tuple(slice(None) for _ in dst.shape)
                act.dma_start(dst[full], src).then_inc(s_wload, 16)

            def f_evac(b, par, h):
                act.wait_ge(f_tr[0], at(f_tr, b))
                nc.scalar.activation(xt0[:, par, :], tr_ps[par][:, 0:2 * P], ACT.Copy).then_inc(f_xt[0], 1)

            def f_phi(b, par):
                act.wait_ge(f_qkb[0], at(f_qkb, b))
                nc.scalar.activation(nrow[:, par, CQ:CQ + SM], qkb[:, par, 0:SM], ACT.Tanh).then_inc(f_q[0], 1)
                act.wait_ge(f_km[0], at(f_km, b))
                nc.scalar.activation(km[:, par, :], km[:, par, :], ACT.Exp).then_inc(f_ke[0], 1)

            def f_step(b, par, h):
                f_evac(b, par, h)
                f_phi(b - 1, 1 - par)

            loop_steps(act, f_evac, f_step, lambda b, par, h: f_phi(b - 1, 1 - par))

            counter = act.alloc_register("v_count_act")
            act.reg_mov(counter, 0)
            act.wait_ge(s_ctl, 16)

            def onehots(s, G):
                for g in range(NG):
                    act.wait_ge(G["tr"][0], at(G["tr"], s, g + 1))
                    nc.scalar.activation(onehot[:, g * GT:(g + 1) * GT, :], b_t[g % 2][:, :, :], ACT.Identity,
                                         bias=1.0, scale=1.0 / BIG).then_inc(G["oh"][0], 1)

            def weights(s, G, q):
                if q == 0:
                    act.wait_ge(G["eb"][0], at(G["eb"], s))
                    nc.scalar.activation(sm[:, 5:6], sm[:, 4:5], ACT.Exp).then_inc(G["es"][0], 1)
                if q >= RING:
                    act.wait_ge(G["wu"][0], at(G["wu"], s, q - RING + 1))
                for j in range(q * PT, (q + 1) * PT):
                    ins = nc.scalar.activation(wgt[:, j % (RING * PT), :], farm[:, j, :], ACT.Exp, bias=ebias[:, j:j + 1])
                ins.then_inc(G["w"][0], 1)

            def evac(b, dst, src, ready, done):
                act.wait_ge(ready[0], at(ready, b))
                nc.scalar.activation(dst, src, ACT.Copy).then_inc(done[0], 1)

            flat2 = lambda t: t[:, :, :].rearrange("p a b -> p (a b)")

            def dense_parts(b):
                def p_xt():
                    evac(b, flat2(xt), b_d[0][:, 0:D], d_t1, d_xt)

                def p_phi():
                    act.wait_ge(d_qm[0], at(d_qm, b))
                    nc.scalar.activation(flat2(qm), flat2(qm), ACT.Exp).then_inc(d_qe[0], 1)

                def p_att():
                    evac(b, flat2(xt), b_d[0][:, 0:D], d_t2, d_attT)

                def p_x1():
                    evac(b, flat2(xt), b_d[0][:, 0:D], d_t3, d_x1T)

                def p_relu():
                    for m in range(FC):
                        if m % 4 == 0:
                            act.wait_ge(d_f1[0], at(d_f1, b, m // 4 + 1))
                        ins = nc.scalar.activation(hff[:, m, :], b_d[1 + m // 4][:, m % 4 * P:(m % 4 + 1) * P], ACT.Relu,
                                                   bias=cv[:, V_FB1 + m:V_FB1 + m + 1])
                        if m % 4 == 3:
                            ins.then_inc(d_h[0], 1)

                def p_xm():
                    evac(b, flat2(xt), b_d[0][:, 0:D], d_t4, d_xmT)

                def p_router():
                    act.wait_ge(d_nm[0], at(d_nm, b))
                    nc.scalar.activation(rt[:, 0, :], b_d[0][:, 0:EXP], ACT.Exp, bias=rts[:, 0:1],
                                         accum_out=rts[:, 1:2]).then_inc(d_re[0], 1)

                def p_moe():
                    for p in range(EXP // 2):
                        act.wait_ge(d_eh[0], at(d_eh, b, p + 1))
                        for e in range(2):
                            for m in range(2):
                                c = V_EB1 + (2 * p + e) * 2 + m
                                ins = nc.scalar.activation(hex_[:, p % 2, e, m, :],
                                                           b_d[1 + p % 2][:, (2 * e + m) * P:(2 * e + m + 1) * P],
                                                           ACT.Gelu, bias=cv[:, c:c + 1])
                        ins.then_inc(d_eg[0], 1)
                        if p == 1:
                            evac(b, ct[:, :], b_m[0:EXP, 256:256 + P], d_ct, d_ctT)

                return [p_xt, p_phi, p_att, p_x1, p_relu, p_xm, p_router, p_moe]

            def g_first(s, par, h):
                onehots(s, M)
                for q in range(NP):
                    weights(s, M, q)
                more(s, par)

            def more(s, par):
                def body(k, c):
                    onehots(k, V)
                    for q in range(NP):
                        weights(k, V, q)
                further_chunks(act, s, body, counter)

            def g_step(s, par, h):
                onehots(s, M)
                parts = dense_parts(s - 1)
                q = 0
                for part, k in zip(parts, (0, 1, 3, 5, 6, 8, 9, 9)):
                    while q < min(NP, k + 2):
                        weights(s, M, q)
                        q += 1
                    part()
                more(s, par)

            def g_last(s, par, h):
                for p in dense_parts(s - 1):
                    p()

            loop_steps(act, g_first, g_step, g_last)

        @block.tensor
        def _(pe):
            pe.wait_ge(s_const, 1)
            pe.matmul(b_a[:, 0:2 * (P + 1)], zero[:, 0:P], zero, start=True, stop=False, skip_group_check=True)

            def f_tr_kv(b, par, acc_prev):
                pe.wait_ge(f_xn[0], at(f_xn, b))
                for c in range(2):
                    ins = pe.transpose(tr_ps[par][:, c * P:(c + 1) * P], nrow[:, par, c * P:(c + 1) * P], identf[:, :])
                ins.then_inc(f_tr[0], 1)
                if acc_prev is not None:
                    f_sum(*acc_prev)
                pe.wait_ge(f_xt[0], at(f_xt, b))
                for c in range(2):
                    pe.matmul(kv_ps[par][:, :], xt0[:, par, c * P:(c + 1) * P], s_wkv[:, c, :], start=(c == 0), stop=(c == 1))
                for c in range(2):
                    ins = pe.matmul(qk_ps[par], xt0[:, par, c * P:(c + 1) * P], s_wqk[:, c, :], start=(c == 0), stop=(c == 1))
                ins.then_inc(f_kv[0], 1)

            def f_sum(b, par, n=P):
                pe.wait_ge(f_kphi[0], at(f_kphi, b))
                for c in range(2):
                    ins = pe.matmul(kva_ps[:, c, :], kphi[0:n, par, c * P:(c + 1) * P], vaug[0:n, par, c, :],
                                    start=False, stop=(n < P), skip_group_check=True)
                ins.then_inc(f_acc[0], 1)

            pe.wait_ge(s_wload, 16 * 12)
            loop_steps(pe, lambda b, par, h: f_tr_kv(b, par, None),
                       lambda b, par, h: f_tr_kv(b, par, (b - 1, 1 - par)),
                       lambda b, par, h: f_sum(b - 1, 1 - par, LAST))

            pe.wait_ge(s_kvm, 1)
            counter = pe.alloc_register("v_count_pe")
            pe.reg_mov(counter, 0)
            pe.wait_ge(s_ctl, 16)

            def keys(s, par, G, g):
                pe.wait_ge(G["oh"][0], at(G["oh"], s, g + 1))
                if g >= 1:
                    pe.wait_ge(G["ku"][0], at(G["ku"], s, g))
                for j in range(GT):
                    ins = pe.matmul(b_s[:, j * 3 * SM:(j + 1) * 3 * SM], onehot[:, g * GT + j, :], kcur[:, par, :],
                                    start=True, stop=True)
                ins.then_inc(G["ke"][0], 1)

            def spread_keys(s, par, h, G):
                pe.wait_ge(G["key"][par], h * 32 + 32)
                for g in range(NG):
                    pe.wait_ge(G["far"][0], at(G["far"], s, g + 1))
                    if g >= 2:
                        pe.wait_ge(G["oh"][0], at(G["oh"], s, g - 1))
                    for j in range(GT):
                        ins = pe.transpose(b_t[g % 2][:, j, :], farm[:, g * GT + j, :], identb[:, :])
                    ins.then_inc(G["tr"][0], 1)
                    if g >= 1:
                        keys(s, par, G, g - 1)
                keys(s, par, G, NG - 1)

            def maxima(s, par, G):
                pe.wait_ge(G["mx"][0], at(G["mx"], s))
                pe.transpose(b_m[:, 0:P], mxr[:, :], identf[:, :]).then_inc(G["mt"][0], 1)
                pe.wait_ge(G["sh"][0], at(G["sh"], s))
                for j in range(CH):
                    ins = pe.matmul(b_m[:, P + 2 * j:P + 2 * j + 2], onehot[:, j, :], shift2[:, :], start=True, stop=True)
                ins.then_inc(G["me"][0], 1)

            def aggregate(s, par, G, q):
                pe.wait_ge(G["w"][0], at(G["w"], s, q + 1))
                for j in range(q * PT, (q + 1) * PT):
                    ins = pe.matmul(b_a[:, 0:AGG], wgt[:, j % (RING * PT), :], rows[:, par, j, 0:AGG],
                                    start=(j == 0), stop=(j == CH - 1))
                ins.then_inc(G["wu"][0], 1)

            def dense_parts(b, par, h):
                def transpose2(src, ready, done):
                    pe.wait_ge(*ready)
                    for c in range(2):
                        ins = pe.transpose(b_d[0][:, c * P:(c + 1) * P], src[:, c * P:(c + 1) * P], identf[:, :])
                    ins.then_inc(done[0], 1)

                def p_t1():
                    if not (isinstance(b, int) and b == 0):
                        pe.wait_ge(d_done[0], at(d_done, b - 1))
                    transpose2(xd[:, par, 1, :], (d_x[par], h * 32 + 32), d_t1)

                def p_q():
                    pe.wait_ge(d_xt[0], at(d_xt, b))
                    for m in range(2):
                        for c in range(2):
                            ins = pe.matmul(b_d[1][:, m * P:(m + 1) * P], s_wq[:, c, m * P:(m + 1) * P], xt[:, c, :],
                                            start=(c == 0), stop=(c == 1))
                    ins.then_inc(d_q[0], 1)

                def p_att():
                    pe.wait_ge(d_qphi[0], at(d_qphi, b))
                    for c in range(2):
                        ins = pe.matmul(b_d[2][:, c * (P + 4):(c + 1) * (P + 4)], qphi[:, c, :], kvm[:, c, :],
                                        start=True, stop=True)
                    ins.then_inc(d_at[0], 1)

                def p_t2():
                    transpose2(att, (d_att[0], at(d_att, b)), d_t2)

                def p_o():
                    pe.wait_ge(d_attT[0], at(d_attT, b))
                    for c in range(2):
                        ins = pe.matmul(b_d[1][:, 0:D], xt[:, c, :], s_wo[:, c, :], start=(c == 0), stop=(c == 1))
                    ins.then_inc(d_o[0], 1)

                def p_t3():
                    transpose2(x1, (d_x1[0], at(d_x1, b)), d_t3)

                def p_f1():
                    pe.wait_ge(d_x1T[0], at(d_x1T, b))
                    for m in range(FC):
                        for c in range(2):
                            ins = pe.matmul(b_d[1 + m // 4][:, m % 4 * P:(m % 4 + 1) * P], s_w1[:, c, m * P:(m + 1) * P],
                                            xt[:, c, :], start=(c == 0), stop=(c == 1))
                        if m % 4 == 3:
                            ins.then_inc(d_f1[0], 1)

                def p_f2():
                    for m in range(FC):
                        if m % 4 == 0:
                            pe.wait_ge(d_h[0], at(d_h, b, m // 4 + 1))
                        ins = pe.matmul(b_d[0][:, 0:D], hff[:, m, :], s_w2[:, m, :], start=(m == 0), stop=(m == FC - 1))
                    ins.then_inc(d_f2[0], 1)

                def p_t4():
                    transpose2(xm, (d_xm[0], at(d_xm, b)), d_t4)

                def p_moe():
                    pe.wait_ge(d_xmT[0], at(d_xmT, b))
                    for c in range(2):
                        ins = pe.matmul(b_d[0][:, 0:EXP], xt[:, c, :], s_rw[:, c, :], start=(c == 0), stop=(c == 1))
                    ins.then_inc(d_lg[0], 1)

                    def hidden(p):
                        if p >= 2:
                            pe.wait_ge(d_eg[0], at(d_eg, b, p - 1))
                        for e in range(2):
                            for m in range(2):
                                for c in range(2):
                                    ins = pe.matmul(b_d[1 + p % 2][:, (2 * e + m) * P:(2 * e + m + 1) * P],
                                                    s_e1[:, 2 * p + e, c, m * P:(m + 1) * P], xt[:, c, :],
                                                    start=(c == 0), stop=(c == 1))
                        ins.then_inc(d_eh[0], 1)

                    def outputs(p):
                        pe.wait_ge(d_eg[0], at(d_eg, b, p + 1))
                        if p == 0:
                            pe.wait_ge(d_re[0], at(d_re, b))
                        else:
                            pe.wait_ge(d_eu[0], at(d_eu, b, p))
                        for e in range(2):
                            for m in range(2):
                                ins = pe.matmul(b_d[0][:, e * D:(e + 1) * D], hex_[:, p % 2, e, m, :],
                                                s_e2[:, 2 * p + e, m, :], start=(m == 0), stop=(m == 1))
                        ins.then_inc(d_ey[0], 1)

                    hidden(0)
                    hidden(1)
                    pe.wait_ge(d_cb[0], at(d_cb, b))
                    pe.transpose(b_m[0:EXP, 256:256 + P], rt[:, 1, :], identf[:, :]).then_inc(d_ct[0], 1)
                    outputs(0)
                    hidden(2)
                    pe.wait_ge(d_ctT[0], at(d_ctT, b))
                    pe.matmul(b_m[:, 256:512], ct[:, :], s_eb2[:, :], start=True, stop=True).then_inc(d_cb2[0], 1)
                    outputs(1)
                    hidden(3)
                    outputs(2)
                    outputs(3)

                return [p_t1, p_q, p_att, p_t2, p_o, p_t3, p_f1, p_f2, p_t4, p_moe]

            def graph_front(s, par, h):
                spread_keys(s, par, h, M)
                maxima(s, par, M)

            def more(s, par):
                def body(k, c):
                    for g in range(NG):
                        pe.wait_ge(V["far"][0], at(V["far"], k, g + 1))
                        if g >= 2:
                            pe.wait_ge(V["oh"][0], at(V["oh"], k, g - 1))
                        for j in range(GT):
                            ins = pe.transpose(b_t[g % 2][:, j, :], farm[:, g * GT + j, :], identb[:, :])
                        ins.then_inc(V["tr"][0], 1)
                        if g >= 1:
                            keys(k, par, V, g - 1)
                    keys(k, par, V, NG - 1)
                    maxima(k, par, V)
                    for q in range(NP):
                        aggregate(k, par, V, q)
                further_chunks(pe, s, body, counter)

            def g_first(s, par, h):
                graph_front(s, par, h)
                for q in range(NP):
                    aggregate(s, par, M, q)
                more(s, par)

            def g_step(s, par, h):
                graph_front(s, par, h)
                pe.wait_ge(M["agg"][0], at(M["agg"], s - 1))
                parts = dense_parts(s - 1, 1 - par, h if par == 1 else h - 1)
                for q in range(NP):
                    parts[q]()
                    aggregate(s, par, M, q)
                for p in parts[NP:]:
                    p()
                more(s, par)

            def g_last(s, par, h):
                for p in dense_parts(s - 1, 1 - par, h):
                    p()

            loop_steps(pe, g_first, g_step, g_last)

        @block.vector
        def _(dve):
            v = nc.vector
            _, _, link, _ = chain_of(dve, (s_set, 0), 0)
            v.memset(zero, 0.0).then_inc(s_const, 1)
            link(v.memset(nrow[:, :, :], 0.0))
            v.memset(nrow[:, :, C1:C1 + 1], 1.0)
            v.memset(vaug[:, :, :, P:P + 1], 1.0)
            v.memset(kvm[:, :, :], 0.0)
            v.memset(base[:, :], 0.0)
            dve.wait_ge(s_dn, 16)
            v.tensor_reduce(t_tmp[:, 0:TPP], dn[:, :, :], AX.X, ALU.max).then_inc(s_trng, 1)
            v.tensor_reduce(t_tmp[:, TPP:2 * TPP], dn[:, :, :], AX.X, ALU.min).then_inc(s_trng, 1)
            dve.wait_ge(s_pool, 4)
            v.tensor_copy(iota_b[:, :], iota_i[:, 0:P])
            v.tensor_copy(iota8[:, :], iota_i[:, 0:EXP])
            v.tensor_copy(identb[:, :], identf[:, :])
            v.tensor_copy(t_idx, iota_i[:, :])
            v.tensor_scalar(cols[:, 0:1], coli[:, 0:1], 1.0, None, ALU.mult)
            v.tensor_scalar(cols[:, 1:2], coli[:, 0:1], float(P - 1), None, ALU.add)
            link(v.tensor_scalar(chunk_steps[:, :], iota_i[:, 0:48], float(CH), float(CH), ALU.mult, ALU.add))
            dve.wait_ge(s_rng_r, 32)
            link(v.tensor_scalar(t_tmp, t_idx, -1.0, float(NT), ALU.mult, ALU.add))
            link(v.scalar_tensor_tensor(t_tmp, t_max, cols[:, 0:1], t_tmp, ALU.is_ge, ALU.mult))
            link(v.tensor_reduce(cols[:, 2:3], t_tmp, AX.X, ALU.max))
            link(v.tensor_scalar(cols[:, 3:4], cols[:, 2:3], -1.0, float(NT), ALU.mult, ALU.add))
            link(v.tensor_scalar(t_tmp, t_idx, 1.0, None, ALU.add))
            link(v.scalar_tensor_tensor(t_tmp, t_min, cols[:, 1:2], t_tmp, ALU.is_le, ALU.mult))
            link(v.tensor_reduce(cols[:, 4:5], t_tmp, AX.X, ALU.max))
            link(v.tensor_scalar(cols[:, 3:4], cols[:, 3:4], float(EDGES // P), None, ALU.min))
            link(v.tensor_tensor(cols[:, 5:6], cols[:, 4:5], cols[:, 3:4], ALU.subtract))
            link(v.tensor_scalar(chunk_steps[:, :], chunk_steps[:, :], cols[:, 5:6], None, ALU.is_lt))
            link(v.tensor_reduce(cols[:, 6:7], chunk_steps[:, :], AX.X, ALU.add))
            v.tensor_copy(coli[:, 0:1], cols[:, 3:4])
            v.tensor_copy(coli[:, 1:2], cols[:, 6:7]).then_inc(s_blk, 1)

            dve.wait_ge(s_xload, 16)
            for b in range(NB):
                ins = v.bn_stats(st[:, b, :], xall[:, b, :])
            link(ins)
            mean, var, rstd, nmr, t1, t2 = [lnm[:, i, :] for i in range(6)]
            s_ = lambda i: st[:, :, i]
            v.tensor_tensor(t1, s_(1), s_(4), ALU.add)
            v.tensor_tensor(t2, s_(1), s_(4), ALU.subtract)
            link(v.tensor_tensor(var, s_(2), s_(5), ALU.add))
            v.tensor_scalar(mean, t1, 0.5, None, ALU.mult)
            link(v.tensor_tensor(t2, t2, t2, ALU.mult))
            link(v.tensor_scalar(t2, t2, 0.25, EPS, ALU.mult, ALU.add))
            link(v.scalar_tensor_tensor(var, var, 1.0 / D, t2, ALU.mult, ALU.add))

            def inv_sqrt(y, x, t):
                link(v.tensor_scalar(y.bitcast(I32), x.bitcast(I32), -0.5, float(0x5f3759df), ALU.mult, ALU.add))
                for _ in range(4):
                    link(v.tensor_tensor(t, y, y, ALU.mult))
                    link(v.tensor_tensor(t, t, x, ALU.mult))
                    link(v.tensor_scalar(t, t, -0.5, 1.5, ALU.mult, ALU.add))
                    link(v.tensor_tensor(y, y, t, ALU.mult))

            inv_sqrt(rstd, var, t1)
            link(v.scalar_tensor_tensor(nmr, mean, -1.0, rstd, ALU.mult, ALU.mult))
            dve.wait_ge(s_wload, 16 * 12)
            link(v.tensor_scalar(bq1[:, :], cv[:, V_BQ:V_BQ + 2], 1.0, None, ALU.add))

            def f_norm(b, par, h, first=False):
                if not (isinstance(b, int) and b == 0) and not first:
                    dve.wait_ge(f_st[par], h * 32)
                v.tensor_scalar(nrow[:, par, 0:D], xall[:, b, :], rstd[:, bass.ds(b, 1)], nmr[:, bass.ds(b, 1)],
                                ALU.mult, ALU.add).then_inc(f_xn[0], 1)

            def f_rest(b, par):
                tick, wait, link, close = chain_of(dve, f_chain, b)
                dve.wait_ge(f_kv[0], at(f_kv, b))
                v.tensor_tensor(qkb[:, par, :], qk_ps[par], rv[:, R_BQK:R_BQK + 2 * SM], ALU.add).then_inc(f_qkb[0], 1)
                link(v.tensor_tensor(kb[:, par, :], kv_ps[par][:, 0:D], rv[:, R_BK:R_BK + D], ALU.add))
                v.tensor_scalar(km[:, par, :], kb[:, par, :], 0.0, None, ALU.min).then_inc(f_km[0], 1)
                v.tensor_tensor(vaug[:, par, :, 0:P], kv_ps[par][:, D:2 * D].rearrange("p (c n) -> p c n", c=2),
                                rv[:, R_BV:R_BV + D].rearrange("p (c n) -> p c n", c=2), ALU.add)
                dve.wait_ge(f_qkb[0], at(f_qkb, b))
                link(v.tensor_scalar(kf[:, :], qkb[:, par, SM:2 * SM], 1.0 / 5.0, None, ALU.mult))
                link(v.tensor_copy(krow[:, par, 0:SM], kf[:, :]))
                link(v.tensor_tensor(kr[:, 0, :], kf[:, :], krow[:, par, 0:SM], ALU.subtract))
                link(v.tensor_copy(krow[:, par, SM:2 * SM], kr[:, 0, :]))
                link(v.tensor_tensor(kr[:, 1, :], kr[:, 0, :], krow[:, par, SM:2 * SM], ALU.subtract))
                v.tensor_copy(krow[:, par, 2 * SM:3 * SM], kr[:, 1, :])
                dve.wait_ge(f_q[0], at(f_q, b))
                link(v.tensor_tensor(qkp[:, :], nrow[:, par, CQ:CQ + SM], kf[:, :], ALU.mult))
                v.tensor_reduce(nrow[:, par, CW:CW + 1], qkp[:, :], AX.X, ALU.add).then_inc(f_row[0], 1)
                dve.wait_ge(f_ke[0], at(f_ke, b))
                v.scalar_tensor_tensor(kphi[:, par, :], kb[:, par, :], 1.0, km[:, par, :], ALU.add,
                                       ALU.max).then_inc(f_kphi[0], 1)
                close()


            def f_step(b, par, h):
                f_norm(b, par, h)
                f_rest(b - 1, 1 - par)

            loop_steps(dve, f_norm, f_step, lambda b, par, h: f_rest(b - 1, 1 - par))

            dve.wait_ge(f_acc[0], at(f_acc, NB - 1))
            for c in range(2):
                for q in range(4):
                    r = slice(HD * q, HD * (q + 1))
                    v.tensor_copy(kvm[r, c, r], kva_ps[r, c, r])
                    ins = v.tensor_copy(kvm[r, c, P + q:P + q + 1], kva_ps[r, c, P:P + 1])
            ins.then_inc(s_kvm, 1)
            dve.wait_ge(s_kvm, 1)

            counter = dve.alloc_register("v_count_dve")
            dve.reg_mov(counter, 0)
            vh = [dve.alloc_register(f"v_half_dve{i}") for i in range(2)]
            dve.reg_mov(vh[0], 0)
            dve.reg_mov(vh[1], 0)
            dve.wait_ge(s_ctl, 16)

            def graph_front(s, par, h, G, prior, start_cols):
                tick, wait, link, close = chain_of(dve, G["chain"], s)
                dve.wait_ge(G["idx"][par], h * 32 + 32)
                link(v.tensor_scalar(dloc[:, :], dst_i[:, par, :], base[:, 0:1], None, ALU.subtract))
                if prior is not None:
                    dve.wait_ge(G["w"][0], at(G["w"], prior))
                for g in range(NG):
                    for j in range(g * GT, (g + 1) * GT):
                        ins = v.tensor_scalar(farm[:, j, :], iota_b[:, :], dloc[:, j:j + 1], -BIG, ALU.not_equal, ALU.mult)
                    ins.then_inc(G["far"][0], 1)
                for g in range(NG):
                    dve.wait_ge(G["ke"][0], at(G["ke"], s, g + 1))
                    dve.wait_ge(G["gat"][par][g], h * (GT * 16) + GT * 16)
                    n = tick(v.tensor_tensor(
                        prod[:, :, :].rearrange("p t (a k) -> p t a k", a=3),
                        b_s[:, 0:GT * 3 * SM].rearrange("p (t a k) -> p t a k", t=GT, a=3),
                        rows[:, par, g * GT:(g + 1) * GT, CQ:CQ + SM].unsqueeze(2).broadcast_to([P, GT, 3, SM]), ALU.mult))
                    dve.wait_ge(G["chain"][0], at(G["chain"], s, n))
                    dve.sem_inc(G["ku"][0], 1)
                    link(v.tensor_reduce(score[:, g * GT:(g + 1) * GT], prod[:, :, :], AX.X, ALU.add))
                    for j in range(g * GT, (g + 1) * GT):
                        k = j % GT
                        if g == 0:
                            ins = v.tensor_scalar(mx[:, k, :], farm[:, j, :], score[:, j:j + 1], None, ALU.add)
                        else:
                            ins = v.scalar_tensor_tensor(mx[:, k, :], farm[:, j, :], score[:, j:j + 1], mx[:, k, :],
                                                         ALU.add, ALU.max)
                    tick(ins)
                wait()
                v.tensor_reduce(mxr[:, :], mx[:, :, :].rearrange("p k n -> p n k"), AX.X, ALU.max).then_inc(G["mx"][0], 1)
                dve.wait_ge(G["mt"][0], at(G["mt"], s))
                link(v.tensor_reduce(sm[:, 0:1], b_m[:, 0:P], AX.X, ALU.max))
                link(v.tensor_tensor(sm[:, 1:2], sm[:, 0:1], start_cols, ALU.max))
                link(v.tensor_copy(shift2[:, 0:1], sm[:, 1:2]))
                link(v.tensor_tensor(sm[:, 2:3], sm[:, 1:2], shift2[:, 0:1], ALU.subtract))
                v.tensor_copy(shift2[:, 1:2], sm[:, 2:3]).then_inc(G["sh"][0], 1)
                dve.wait_ge(G["sh"][0], at(G["sh"], s))
                link(v.tensor_tensor(sm[:, 3:4], shift2[:, 0:1], shift2[:, 1:2], ALU.add))
                link(v.tensor_tensor(sm[:, 4:5], start_cols, sm[:, 3:4], ALU.subtract))
                dve.wait_ge(G["me"][0], at(G["me"], s))
                spread = b_m[:, P:P + 2 * CH].rearrange("p (j a) -> p j a", a=2)
                link(v.tensor_tensor(ebias[:, :], score[:, :], spread[:, :, 0], ALU.subtract))
                v.tensor_tensor(ebias[:, :], ebias[:, :], spread[:, :, 1], ALU.subtract).then_inc(G["eb"][0], 1)
                close()

            def graph_merge(s, par, G, old):
                dve.wait_ge(G["wu"][0], at(G["wu"], s))
                dve.wait_ge(G["es"][0], at(G["es"], s))
                v.tensor_copy(sm[:, 6:7], sm[:, 3:4])
                v.scalar_tensor_tensor(acc[:, par, :], old, sm[:, 5:6], b_a[:, 0:AGG], ALU.mult, ALU.add).then_inc(G["agg"][0], 1)


            def front(s, par, h, prior):
                graph_front(s, par, h, M, prior, own[:, par, CW:CW + 1])

            def merge(s, par):
                graph_merge(s, par, M, own[:, par, 0:AGG])

            def more(s, par):
                def body(k, c):
                    hv = dve.snap(vh[par], min_val=0, max_val=1 << 20)
                    graph_front(k, par, hv, V, None, sm[:, 6:7])
                    graph_merge(k, par, V, acc[:, par, :])
                    dve.reg_add(vh[par], vh[par], 1)
                further_chunks(dve, s, body, counter)
                dve.wait_ge(M["agg"][0], at(M["agg"], s))
                v.tensor_scalar(base[:, :], base[:, :], float(P), None, ALU.add).then_inc(b_sig[0], 1)
                dve.wait_ge(b_sig[0], at(b_sig, s))

            def layer_norm(link, dst, src, k, g=None, bias=None):
                s6, mv, r, t, nm = lns[:, k, 0:6], lns[:, k, 6:8], lns[:, k, 8:9], lns[:, k, 9:10], lns[:, k, 10:11]
                link(v.bn_stats(s6, src), hold=True)
                link(v.bn_aggr(mv, s6))
                link(v.tensor_scalar(lns[:, k, 7:8], lns[:, k, 7:8], EPS, None, ALU.add))
                x = lns[:, k, 7:8]
                link(v.tensor_scalar(r.bitcast(I32), x.bitcast(I32), -0.5, float(0x5f3759df), ALU.mult, ALU.add))
                for _ in range(3):
                    link(v.tensor_scalar(t, r, r, x, ALU.mult, ALU.mult))
                    link(v.tensor_scalar(t, t, -0.5, 1.5, ALU.mult, ALU.add))
                    link(v.tensor_tensor(r, r, t, ALU.mult))
                ins = v.tensor_scalar(dst, src, lns[:, k, 6:7], r, ALU.subtract, ALU.mult)
                if g is not None:
                    link(ins)
                    link(v.tensor_tensor(dst, dst, g, ALU.mult))
                    ins = v.tensor_tensor(dst, dst, bias, ALU.add)
                return ins

            def dense(b, par, h):
                tick, wait, link, close = chain_of(dve, d_chain, b, lambda: fence(dve))
                dve.wait_ge(d_q[0], at(d_q, b))
                for m in range(2):
                    ins = v.tensor_scalar(qm[:, m, :], b_d[1][:, m * P:(m + 1) * P], cv[:, V_BQ + m:V_BQ + m + 1], 0.0,
                                          ALU.add, ALU.min)
                ins.then_inc(d_qm[0], 1)
                dve.wait_ge(d_qe[0], at(d_qe, b))
                for m in range(2):
                    ins = v.scalar_tensor_tensor(qphi[:, m, :], b_d[1][:, m * P:(m + 1) * P], bq1[:, m:m + 1], qm[:, m, :],
                                                 ALU.add, ALU.max)
                ins.then_inc(d_qphi[0], 1)
                dve.wait_ge(d_x[par], h * 32 + 32)
                n = tick(v.tensor_tensor(y1[:, :], xd[:, par, 1, :], rv[:, R_BO:R_BO + D], ALU.add))
                dve.wait_ge(d_at[0], at(d_at, b))
                num = b_d[2][:, 0:2 * (P + 4)].rearrange("p (c n) -> p c n", c=2)
                link(v.tensor_scalar(den[:, 0, :].rearrange("p (c h) -> p c h", c=2), num[:, :, P:P + 4], 1e-6, None, ALU.add))
                link(v.reciprocal(den[:, 1, :], den[:, 0, :]))
                for c in range(2):
                    ins = v.tensor_tensor(att[:, c * P:(c + 1) * P].rearrange("p (h d) -> p h d", h=4),
                                          num[:, c, 0:P].rearrange("p (h d) -> p h d", h=4),
                                          den[:, 1, 4 * c:4 * c + 4].unsqueeze(2).broadcast_to([P, 4, HD]), ALU.mult)
                ins.then_inc(d_att[0], 1)
                dve.wait_ge(d_o[0], at(d_o, b))
                link(v.tensor_tensor(y1[:, :], b_d[1][:, 0:D], y1[:, :], ALU.add))
                layer_norm(link, x1[:, :], y1[:, :], 0, rv[:, R_G1:R_G1 + D], rv[:, R_B1:R_B1 + D]).then_inc(d_x1[0], 1)
                dve.wait_ge(d_x1[0], at(d_x1, b))
                tick(v.tensor_tensor(y1[:, :], x1[:, :], rv[:, R_F2:R_F2 + D], ALU.add))
                link(v.reciprocal(rl[:, :], acc[:, par, D:D + 1]))
                link(v.scalar_tensor_tensor(xr[:, :], acc[:, par, 0:D], rl[:, 0:1], xd[:, par, 0, :], ALU.mult, ALU.add))
                dve.wait_ge(d_f2[0], at(d_f2, b))
                link(v.tensor_tensor(y1[:, :], b_d[0][:, 0:D], y1[:, :], ALU.add))
                link(layer_norm(link, x1[:, :], y1[:, :], 1, rv[:, R_G2:R_G2 + D], rv[:, R_B2:R_B2 + D]))
                link(v.tensor_tensor(xr[:, :], xr[:, :], x1[:, :], ALU.add))
                layer_norm(link, xm[:, :], xr[:, :], 2).then_inc(d_xm[0], 1)
                dve.wait_ge(d_xm[0], at(d_xm, b))
                tick(v.tensor_tensor(xr[:, :], xr[:, :], xm[:, :], ALU.add))
                dve.wait_ge(d_lg[0], at(d_lg, b))
                v.tensor_reduce(rts[:, 0:1], b_d[0][:, 0:EXP], AX.X, ALU.max, negate=True).then_inc(d_nm[0], 1)
                dve.wait_ge(d_re[0], at(d_re, b))
                link(v.reciprocal(rts[:, 2:3], rts[:, 1:2]))
                link(v.tensor_scalar(rt[:, 2, :], rt[:, 0, :], rts[:, 2:3], None, ALU.mult), hold=True)
                link(v.max(rt[:, 3, :], rt[:, 2, :]), hold=True)
                tick(v.max_index(ridx[:, :], rt[:, 3, :], rt[:, 2, :]))
                link(v.tensor_tensor(rts[:, 3:4], rt[:, 3, 0:1], rt[:, 3, 1:2], ALU.add))
                link(v.tensor_scalar(rts[:, 3:4], rts[:, 3:4], 1e-12, None, ALU.max))
                link(v.reciprocal(rts[:, 4:5], rts[:, 3:4]))
                link(v.tensor_scalar(rt[:, 3, 0:2], rt[:, 3, 0:2], rts[:, 4:5], None, ALU.mult))
                link(v.tensor_copy(rts[:, 5:7], ridx[:, 0:2]))
                tick(v.tensor_scalar(rt[:, 0, :], iota8[:, :], rts[:, 5:6], rt[:, 3, 0:1], ALU.is_equal, ALU.mult))
                link(v.tensor_scalar(rt[:, 2, :], iota8[:, :], rts[:, 6:7], rt[:, 3, 1:2], ALU.is_equal, ALU.mult))
                v.tensor_tensor(rt[:, 1, :], rt[:, 0, :], rt[:, 2, :], ALU.add).then_inc(d_cb[0], 1)
                dve.wait_ge(d_cb2[0], at(d_cb2, b))
                link(v.tensor_tensor(xr[:, :], b_m[:, 256:512], xr[:, :], ALU.add))
                if not (isinstance(b, int) and b == 0):
                    dve.wait_ge(d_out[par], h * 16)
                for p in range(EXP // 2):
                    dve.wait_ge(d_ey[0], at(d_ey, b, p + 1))
                    for e in range(2):
                        i = 2 * p + e
                        dst = res[:, par, :] if i == EXP - 1 else xr[:, :]
                        ins = v.scalar_tensor_tensor(dst, b_d[0][:, e * D:(e + 1) * D], rt[:, 1, i:i + 1], xr[:, :],
                                                     ALU.mult, ALU.add)
                        if e == 0:
                            link(ins)
                    ins.then_inc(d_eu[0], 1)
                    dve.wait_ge(d_eu[0], at(d_eu, b, p + 1))
                dve.sem_inc(d_done[0], 1)
                close()

            def g_first(s, par, h):
                front(s, par, h, None)
                merge(s, par)
                more(s, par)

            def g_step(s, par, h):
                front(s, par, h, s - 1)
                dense(s - 1, 1 - par, h if par == 1 else h - 1)
                merge(s, par)
                more(s, par)

            loop_steps(dve, g_first, g_step, lambda s, par, h: dense(s - 1, 1 - par, h))


def kernel(**inputs):
    import concourse.bacc as bacc
    from concourse.bass_utils import run_bass_kernel_spmd

    g = {k: np.asarray(a) for k, a in inputs.items()}
    halves = lambda w: np.ascontiguousarray(w.reshape(w.shape[0] // P, P, -1).transpose(1, 0, 2))
    column = lambda a: a.reshape(-1, P).T
    edges = np.full(NT * P - EDGES, FAR, g["dst"].dtype)
    dst = np.concatenate([g["dst"], edges])
    src = np.concatenate([g["src"], np.zeros_like(edges)])
    experts = lambda w: np.ascontiguousarray(w.reshape(EXP, 2, P, D).transpose(2, 0, 1, 3))
    arrays = {
        "xpad": np.concatenate([g["x"], np.zeros((NPAD - NODES, D), g["x"].dtype)]),
        "src_t": np.ascontiguousarray(src.reshape(NT, P).T),
        "dst_t": np.ascontiguousarray(dst.reshape(NT, P).T),
        "dst_n": dst.reshape(P, TPP, P),
        "rowvec": np.concatenate([g[k] for k in (
            "L0_mix_bk", "L0_mix_bv", "L0_mix_bo", "L0_mix_ln1_g", "L0_mix_ln1_b", "L0_mix_ln2_g", "L0_mix_ln2_b",
            "L0_mix_b2", "L0_gnn_bq", "L0_gnn_bk")])[None],
        "colvec": np.ascontiguousarray(np.concatenate(
            [column(g["L0_mix_bq"]), column(g["L0_mix_b1"]), column(g["L0_ffn_b1"])], axis=1)),
        "wqk": halves(np.concatenate([g["L0_gnn_Wq"], g["L0_gnn_Wk"]], axis=1)),
        "wq": halves(g["L0_mix_Wq"]),
        "wkv": halves(np.concatenate([g["L0_mix_Wk"], g["L0_mix_Wv"]], axis=1)),
        "wo": halves(g["L0_mix_Wo"]),
        "w1": halves(g["L0_mix_W1"]),
        "w2": halves(g["L0_mix_W2"]),
        "rw": halves(np.ascontiguousarray(g["L0_ffn_router_w"].T)),
        "ew1": experts(g["L0_ffn_w1"]),
        "ew2": experts(g["L0_ffn_w2"]),
        "eb2": g["L0_ffn_b2"],
    }
    nc = bacc.Bacc("TRN2", target_bir_lowering=False, num_devices=1)
    args = [nc.dram_tensor(f"in_{k}", a.shape, mybir.dt.from_np(a.dtype), kind="ExternalInput").ap() for k, a in arrays.items()]
    out = nc.dram_tensor("out_0", (NPAD, D), F32, kind="ExternalOutput").ap()
    graph_block(nc, *args, out)
    r = run_bass_kernel_spmd(nc, [{f"in_{k}": a for k, a in arrays.items()}], core_ids=[0])
    return r.results[0]["out_0"][:NODES]
```

```python
from contextlib import ExitStack

import numpy as np

import concourse.bass as bass
from concourse import mybir

F32 = mybir.dt.float32
BF16 = mybir.dt.bfloat16
I32 = mybir.dt.int32
U32 = mybir.dt.uint32
ALU = mybir.AluOpType
ACT = mybir.ActivationFunctionType
AX = mybir.AxisListType

P = 128
NODES, D = 6250, 256
NB = (NODES + P - 1) // P
NPAD = NB * P
LAST = NODES - (NB - 1) * P
EDGES = 206250
TPP = 13
NT = TPP * P
CH = 36
GT = 6
NG = CH // GT
PT = 4
NP = CH // PT
RING = 3
SM = 25
ROW = 284
C1, CQ, CW = D, D + 1, D + 1 + SM
AGG = D + 1
HEADS, HD = 8, 32
FF = 1024
FC = FF // P
EXP = 8
EPS = 1e-5
D_CHAIN = 61
BIG = float(2.0 ** 100)
FAR = 1 << 14

R_BO, R_G1, R_B1, R_G2, R_B2, R_F2 = [D * i for i in range(6)]
R_END = 6 * D
R_BK, R_BV, R_BQK = 0, D, 2 * D
F_END = R_BQK + 2 * SM
V_BQ, V_FB1, V_EB1 = 0, 2, 2 + FC
V_END = V_EB1 + 2 * EXP
ORDER = """xt t0 w0 q t1 w1 qphi att k0 a0 w2 attT k1 a1 w3 o w4 t2 a2 w5 a3 w6 a4 w7 x1T f1a f1b k2 t3 f2 a5 w8 a6 a7 a8
           k3 t4 mg xmT lg h0 rt k4 h1 t5 cT y0 h2 cb2 k5 y1 mx h3 mt y2 me y3""".split()


def at(signal, step, n=None):
    _, per = signal
    return step * per + (per if n is None else n)


def chain_of(eng, signal, step, fence=None):
    semaphore, per = signal
    count = [0]

    def tick(ins):
        count[0] += 1
        ins.then_inc(semaphore, 1)
        return count[0]

    def wait(n=None):
        eng.wait_ge(semaphore, at(signal, step, count[0] if n is None else n))

    def link(ins, hold=False):
        tick(ins)
        wait()
        if hold:
            fence()

    def close():
        assert count[0] == per, (count[0], per)

    return tick, wait, link, close


def graph_block(nc, xpad, src_t, dst_t, dst_n, rowvec, firstvec, colvec, wqk, wq, wkv, wo, w1, w2, rw, ew1, ew2, eb2, out):
    ctx = ExitStack()
    with ctx:
        def sb(name, shape, dt=F32):
            return ctx.enter_context(nc.sbuf_tensor(name, shape, dt))

        def ps(name, shape, dt=F32):
            return ctx.enter_context(nc.psum_tensor(name, shape, dt))

        def sem(name):
            return ctx.enter_context(nc.semaphore(name))

        def sig(name, per=1):
            return sem(name), per

        table = nc.dram_tensor("node_table", (NPAD, ROW), F32).ap()
        knode = nc.dram_tensor("node_keys", (NPAD, 3 * SM), BF16).ap()
        tile_rng = nc.dram_tensor("tile_range", (2, NT), F32).ap()
        blk_rng = nc.dram_tensor("block_range", (2, P), I32).ap()

        rows = sb("gathered_rows", [P, 2, CH, ROW])
        flat = rows[:, :, :, :].rearrange("p a b c -> p (a b c)")
        xall = flat[:, 0:NB * D].rearrange("p (b d) -> p b d", d=D)
        o = NB * D
        t_max, t_min, t_idx, t_tmp = [flat[:, o + i * NT:o + (i + 1) * NT] for i in range(4)]
        farm = sb("far_mask", [P, 2, CH, P], BF16)
        onehot = sb("onehot_t", [P, CH, P], BF16)
        wgt = sb("weights", [P, RING * PT, P])
        mx = sb("max_partial", [P, GT, P])
        mxr = sb("max_rows", [P, P])
        prod = sb("score_products", [P, GT, 3 * SM])
        score = sb("scores", [P, CH])
        ebias = sb("exp_bias", [P, 2, CH])
        src_i = sb("src_idx", [P, 3, CH], I32)
        dst_i = sb("dst_idx", [P, 3, CH], I32)
        dloc = sb("dst_local", [P, CH])
        base = sb("block_base", [P, 2])
        kcur = sb("block_keys", [P, 2, 3 * SM], BF16)
        own = sb("own_rows", [P, 2, ROW])
        acc = sb("aggregate", [P, 2, AGG])
        shift2 = sb("shift_parts", [P, 2], BF16)
        sm = sb("softmax_cols", [P, 2, 8])
        iota_b = sb("iota_b", [P, P], BF16)
        identf = sb("ident_f", [P, P])
        identb = sb("ident_b", [P, P], BF16)
        zero = acc[:, :, :].rearrange("p a b -> p (a b)")[:, 0:2 * (P + 1)]
        ctl = sb("control", [1, 2 * P], I32)
        cols = sb("range_cols", [P, 8])
        coli = sb("range_cols_i", [P, 2], I32)
        chunk_steps = sb("chunk_steps", [P, 48])
        s_wqk = sb("w_graph_qk", [P, 2, 2 * SM])
        s_wq = sb("w_mix_q", [P, 2, D])
        s_wo = sb("w_mix_o", [P, 2, D])
        s_w1 = sb("w_ff1", [P, 2, FF])
        s_w2 = sb("w_ff2", [P, FC, D])
        s_rw = sb("w_router", [P, 2, EXP])
        s_e1 = sb("w_expert1", [P, EXP, 2, D])
        s_e2 = sb("w_expert2", [P, EXP, 2, D])
        s_eb2 = sb("b_expert2", [EXP, D])
        rv = sb("row_vectors", [P, R_END])
        cv = sb("col_vectors", [P, V_END])
        bq1 = sb("bq_plus_1", [P, 2])
        o += 4 * NT
        st = flat[:, o:o + 6 * NB].rearrange("p (b s) -> p b s", s=6)
        lnm = flat[:, o + 6 * NB:o + 12 * NB].rearrange("p (s b) -> p s b", s=6)
        nrow = flat[:, o + 12 * NB:o + 12 * NB + 2 * ROW].rearrange("p (a c) -> p a c", a=2)
        krow = sb("node_key_parts", [P, 2, 3 * SM], BF16)
        wflat = wgt[:, :, :].rearrange("p a b -> p (a b)")
        kb, km, kphi = [wflat[:, i * 2 * D:(i + 1) * 2 * D].rearrange("p (a b) -> p a b", a=2) for i in range(3)]
        vaug = mx[:, :, :].rearrange("p a b -> p (a b)")[:, 0:4 * (P + 1)].rearrange("p (a b c) -> p a b c", a=2, b=2)
        dn = onehot[:, 0:2 * TPP, :].rearrange("p a b -> p (a b)").bitcast(I32).rearrange("p (a b) -> p a b", b=P)
        iota_i = farm[:, 0, 0:2 * TPP, :].rearrange("p a b -> p (a b)").bitcast(I32)
        pflat = prod[:, :, :].rearrange("p a b -> p (a b)")
        qkb = pflat[:, 0:4 * SM].rearrange("p (a b) -> p a b", a=2)
        kr = pflat[:, 4 * SM:6 * SM].rearrange("p (a b) -> p a b", a=2)
        kf, qkp = pflat[:, 6 * SM:7 * SM], pflat[:, 7 * SM:8 * SM]
        kvm = sb("kv_blocks", [P, 2, P + 4])
        xd = sb("block_x", [P, 2, 2, D])
        xt = sb("xn_t", [P, 2, P])
        qm = sb("q_min", [P, 2, P])
        den = sb("attn_den", [P, 2, HEADS])
        att = sb("attn", [P, D])
        rowsum = sb("block_rows", [P, 4, D])
        y1, x1, xr, xm = [rowsum[:, i, :] for i in range(4)]
        s_wkv = rowsum[:, :, :].rearrange("p (c a) d -> p c (a d)", c=2)
        fv = xd[:, :, :, :].rearrange("p a b d -> p (a b d)")[:, 0:F_END]
        hff = sb("h_ff", [P, FC, P])
        xt0 = hff[:, 0:4, :].rearrange("p a b -> p (a b)").rearrange("p (a b) -> p a b", a=2)
        hex_ = hff[:, :, :].rearrange("p (a b c) n -> p a b c n", a=2, b=2)
        res = sb("result", [P, D])
        lns = sb("ln_small", [P, 3, 12])
        rt = sb("router", [P, 4, EXP])
        rts = sb("router_small", [P, 8])
        ridx = sb("router_idx", [P, 8], U32)
        ct = sb("combine_t", [EXP, P])
        iota8 = sb("iota8", [P, EXP])
        rl = sb("inv_sum", [P, 1])

        b_t = [ps(f"bank_t{i}", [P, GT, P], BF16) for i in range(2)]
        b_s = ps("bank_scores", [P, 512])
        b_m = ps("bank_max", [P, 512])
        b_a = ps("bank_agg", [P, 512])
        b_d = [ps(f"bank_d{i}", [P, 512]) for i in range(3)]
        b_y = [b_d[0], b_a]
        tr_ps = [b_s, b_m]
        kv_ps = [b_d[0], b_d[1]]
        qk_ps = [b_d[2][:, 0:2 * SM], b_d[2][:, 64:64 + 2 * SM]]
        kva_ps = b_a[:, 0:2 * (P + 1)].rearrange("p (c n) -> p c n", c=2)

        s_wload, s_xload, s_dn = sem("weights_loaded"), sem("x_loaded"), sem("dst_tiles_loaded")
        s_const = sem("constants_ready")
        s_pool = sem("pool_constants_ready")
        s_rng_w, s_rng_r, s_trng = sem("tile_range_stored"), sem("tile_range_loaded"), sem("tile_range_ready")
        s_blk, s_blk_w, s_ctl = sem("block_range_ready"), sem("block_range_stored"), sem("control_loaded")
        s_set = sem("dve_setup_chain")
        s_kvz, s_kvm = sem("kv_zeroed"), sem("kv_blocks_ready")
        f_xn, f_tr, f_xt, f_kv = sig("f_xn_ready"), sig("f_transposed"), sig("f_xt_ready"), sig("f_kv_ready")
        f_km, f_ke, f_kphi, f_acc = sig("f_kmin_ready"), sig("f_kexp_ready"), sig("f_kphi_ready"), sig("f_kv_added")
        f_qkb, f_q, f_row = sig("f_qk_biased"), sig("f_q_ready"), sig("f_row_ready")
        f_st = [sem("f_rows_stored0"), sem("f_rows_stored1")]
        f_chain = sig("f_dve_chain", 7)

        def graph_signals(tag):
            return {
                "idx": [sem(f"{tag}_edges_loaded{i}") for i in range(3)],
                "key": [sem(f"{tag}_keys_loaded{i}") for i in range(2)],
                "own": [sem(f"{tag}_own_loaded{i}") for i in range(2)],
                "gat": [[sem(f"{tag}_rows_gathered{i}_{g}") for g in range(NG)] for i in range(3)],
                "far": sig(f"{tag}_far_mask_ready", NG),
                "tr": sig(f"{tag}_mask_transposed", NG),
                "oh": sig(f"{tag}_onehot_ready", NG),
                "ke": sig(f"{tag}_keys_spread", NG),
                "ku": sig(f"{tag}_keys_used", NG),
                "mx": sig(f"{tag}_max_rows_ready"),
                "mt": sig(f"{tag}_max_transposed"),
                "sh": sig(f"{tag}_shift_ready"),
                "me": sig(f"{tag}_shift_spread"),
                "eb": sig(f"{tag}_exp_bias_ready"),
                "es": sig(f"{tag}_old_scale_ready"),
                "w": sig(f"{tag}_weights_ready", NP),
                "wu": sig(f"{tag}_weights_used", NP),
                "agg": sig(f"{tag}_aggregate_ready"),
                "chain": sig(f"{tag}_dve_chain", 2 * NG + 7),
                "loc": sig(f"{tag}_dst_local_ready", 2),
            }

        M = graph_signals("m")
        V = graph_signals("v")
        v_meet = sem("v_engines_meet")
        s_fence = sem("wait_carried")

        d_x = [sem("d_x_loaded0"), sem("d_x_loaded1")]
        d_out = sem("d_out_stored")
        (d_t1, d_xt, d_q, d_qm, d_qe, d_qphi, d_at, d_att, d_t2, d_attT, d_o, d_x1, d_t3, d_x1T) = [
            sig("d_" + n) for n in ("xn_transposed", "xn_t_ready", "q_ready", "qmin_ready", "qexp_ready", "qphi_ready",
                                    "attn_ready", "attn_normed", "attn_transposed", "attn_t_ready", "wo_ready",
                                    "x1_ready", "x1_transposed", "x1_t_ready")]
        d_f1, d_h, d_f2, d_xm, d_t4, d_xmT = [
            sig("d_" + n, k) for n, k in (("ff1_ready", 2), ("relu_ready", 2), ("ff2_ready", 1), ("xm_ready", 1),
                                          ("xm_transposed", 1), ("xm_t_ready", 1))]
        d_lg, d_nm, d_re, d_cb, d_ct, d_ctT, d_cb2 = [
            sig("d_" + n) for n in ("logits_ready", "logit_max_ready", "router_exp_ready", "combine_ready",
                                    "combine_transposed", "combine_t_ready", "combine_b2_ready")]
        d_eh, d_eg, d_ey, d_eu = [sig("d_" + n, EXP // 2) for n in ("expert_h_ready", "expert_gelu_ready",
                                                                   "expert_y_ready", "expert_y_used")]
        d_chain = sig("d_dve_chain", D_CHAIN)
        b_sig = sig("block_base_moved")
        v_again = sig("v_dst_local_restored")

        def fence(eng):
            eng.sem_inc(s_fence, 1)

        def loop_steps(eng, first, step, last):
            first(0, 0, 0)
            with eng.Fori(0, (NB - 1) // 2) as i:
                step(i * 2 + 1, 1, i)
                step(i * 2 + 2, 0, i + 1)
            last(NB, 1, (NB - 1) // 2)

        def pipeline(eng, front, step, last):
            front(0, 0, 0)
            step(0, 0, 0, dense=False)
            with eng.Fori(0, (NB - 3) // 2) as i:
                step(i * 2 + 1, 1, i)
                step(i * 2 + 2, 0, i + 1)
            step(NB - 2, 1, (NB - 3) // 2, masks_ahead=False)
            step(NB - 1, 0, (NB - 1) // 2, after=False, masks_ahead=False)
            last(NB - 1, 0, (NB - 1) // 2)

        def in_order(*parts):
            for stage in ORDER:
                for p in parts:
                    if stage in p:
                        p[stage]()

        def further_chunks(eng, block, body, counter):
            more = eng.value_load(ctl[0:1, bass.ds(block + P, 1)], min_val=0, max_val=NT // CH)
            with eng.If(more > 0):
                with eng.Fori(0, more) as c:
                    k = eng.snap(counter, min_val=0, max_val=NB * NT // CH)
                    eng.drain().then_inc(v_meet, 1)
                    eng.wait_ge(v_meet, k * 10 + 5)
                    fence(eng)
                    body(k, c)
                    eng.drain().then_inc(v_meet, 1)
                    eng.wait_ge(v_meet, k * 10 + 10)
                    fence(eng)
                    eng.reg_add(counter, counter, 1)

        block = ctx.enter_context(nc.Block())

        @block.sync
        def _(sp):
            sp.dma_start(dn[:, :, :], dst_n).then_inc(s_dn, 16)
            sp.dma_start(xall, xpad.rearrange("(b p) d -> p b d", p=P)).then_inc(s_xload, 16)
            sp.wait_ge(s_trng, 2)
            sp.dma_start(tile_rng[0].rearrange("(p c) -> p c", p=P), t_tmp[:, 0:TPP]).then_inc(s_rng_w, 16)
            sp.dma_start(tile_rng[1].rearrange("(p c) -> p c", p=P), t_tmp[:, TPP:2 * TPP]).then_inc(s_rng_w, 16)
            sp.wait_ge(s_rng_w, 32)
            sp.dma_start(t_max, tile_rng[0:1, :].broadcast_to([P, NT])).then_inc(s_rng_r, 16)
            sp.dma_start(t_min, tile_rng[1:2, :].broadcast_to([P, NT])).then_inc(s_rng_r, 16)
            sp.wait_ge(s_blk, 1)
            sp.dma_start(blk_rng[0], coli[:, 0]).then_inc(s_blk_w, 16)
            sp.dma_start(blk_rng[1], coli[:, 1]).then_inc(s_blk_w, 16)
            sp.wait_ge(s_blk_w, 32)
            sp.dma_start(ctl[0:1, :], blk_rng.rearrange("a b -> (a b)").unsqueeze(0)).then_inc(s_ctl, 16)

            def store_rows(b, par, h):
                sp.wait_ge(f_row[0], at(f_row, b))
                fence(sp)
                sp.dma_start(table[bass.ds(b * P, P), :], nrow[:, par, :]).then_inc(f_st[par], 16)
                sp.dma_start(knode[bass.ds(b * P, P), :], krow[:, par, :]).then_inc(f_st[par], 16)

            loop_steps(sp, store_rows, store_rows, lambda *a: None)
            sp.wait_ge(f_st[0], 32 * ((NB + 1) // 2))
            sp.wait_ge(f_st[1], 32 * (NB // 2))
            sp.wait_ge(s_ctl, 16)
            counter = sp.alloc_register("v_count_sp")
            sp.reg_mov(counter, 0)

            def load_edges(s, place, G, extra=0):
                lo = sp.value_load(ctl[0:1, bass.ds(s, 1)], min_val=0, max_val=EDGES // P)
                tile = nc.s_assert_within(lo + extra, 0, NT - CH, skip_runtime_bounds_check_because=(
                    "a chunk starts at one of its block's tiles, before the padding"))
                sp.dma_start(src_i[:, place, :], src_t[:, bass.ds(tile, CH)]).then_inc(G["idx"][place], 16)
                sp.dma_start(dst_i[:, place, :], dst_t[:, bass.ds(tile, CH)]).then_inc(G["idx"][place], 16)

            def load(s, par, first=False):
                if not first:
                    sp.wait_ge(M["eb"][0], at(M["eb"], s - 2))
                    fence(sp)
                load_edges(s, par, M)

            def load_keys(s, par):
                sp.dma_start(kcur[:, par, :], knode[bass.ds(s * P, P), :]).then_inc(M["key"][par], 16)

            def load_own(s, par, first=False):
                if not first:
                    sp.wait_ge(M["agg"][0], at(M["agg"], s - 2))
                    fence(sp)
                sp.dma_start(own[:, par, :], table[bass.ds(s * P, P), :]).then_inc(M["own"][par], 16)

            def load_x(b, par):
                sp.dma_start(xd[:, par, 0, :], xpad[bass.ds(b * P, P), :]).then_inc(d_x[par], 16)
                sp.dma_start(xd[:, par, 1, :], table[bass.ds(b * P, P), 0:D]).then_inc(d_x[par], 16)

            def more(s, par):
                def body(k, c):
                    load_edges(s, 2, V, (c + 1) * CH)
                further_chunks(sp, s, body, counter)

            def store(b):
                sp.wait_ge(d_eu[0], at(d_eu, b))
                fence(sp)
                sp.dma_start(out[bass.ds(b * P, P), :], res[:, :]).then_inc(d_out, 16)

            def step(s, par, ahead=True, nxt=True):
                if ahead:
                    load(s + 2, par)
                more(s, par)
                if ahead:
                    load_keys(s + 2, par)
                    load_own(s + 2, par)
                store(s - 1)
                if nxt:
                    load_x(s + 1, 1 - par)

            for s in range(2):
                load(s, s, True)
                load_keys(s, s)
                load_own(s, s, True)
                load_x(s, s)
            load(2, 0)
            more(0, 0)
            load_keys(2, 0)
            load_own(2, 0)
            with sp.Fori(0, (NB - 3) // 2) as i:
                step(i * 2 + 1, 1)
                step(i * 2 + 2, 0)
            step(NB - 2, 1, ahead=False)
            step(NB - 1, 0, ahead=False, nxt=False)
            store(NB - 1)
            sp.wait_ge(d_out, 16 * NB)

        @block.gpsimd
        def _(pool):
            nc.gpsimd.iota(iota_i[:, :], pattern=[[1, NT]], base=0, channel_multiplier=0).then_inc(s_pool, 1)
            nc.gpsimd.iota(coli[:, 0:1], pattern=[[0, 1]], base=0, channel_multiplier=P).then_inc(s_pool, 1)
            nc.gpsimd.memset(identf[:, :], 0.0).then_inc(s_pool, 1)
            pool.wait_ge(s_pool, 3)
            nc.gpsimd.affine_select(out=identf[:, :], in_=identf[:, :], compare_op=ALU.not_equal, fill=1.0, base=0,
                                    pattern=[[-1, P]], channel_multiplier=1).then_inc(s_pool, 1)
            counter = pool.alloc_register("v_count_pool")
            pool.reg_mov(counter, 0)
            pool.wait_ge(s_ctl, 16)
            pool.wait_ge(f_st[0], 32 * ((NB + 1) // 2))
            pool.wait_ge(f_st[1], 32 * (NB // 2))
            pool.wait_ge(s_blk, 1)

            def gather_chunk(par, place, G, free=None):
                for g in range(NG):
                    if free is not None:
                        free((g * GT + GT + PT - 1) // PT)
                    for j in range(g * GT, (g + 1) * GT):
                        nc.gpsimd.indirect_dma_start(
                            out=rows[:, par, j, :], out_offset=None, in_=table,
                            in_offset=bass.IndirectOffsetOnAxis(ap=src_i[:, place, j:j + 1], axis=0),
                        ).then_inc(G["gat"][place][g], 16)

            def gather(s, par, h, first=False):
                pool.wait_ge(M["idx"][par], h * 32 + 32)
                fence(pool)

                def free(q):
                    pool.wait_ge(M["wu"][0], at(M["wu"], s - 2, q))
                    fence(pool)

                gather_chunk(par, par, M, None if first else free)

            def more(s, par):
                def body(k, c):
                    pool.wait_ge(V["idx"][2], k * 32 + 32)
                    fence(pool)
                    gather_chunk(par, 2, V)
                further_chunks(pool, s, body, counter)

            gather(0, 0, 0, True)
            gather(1, 1, 0, True)
            with pool.Fori(0, (NB - 3) // 2) as i:
                more(i * 2, 0)
                gather(i * 2 + 2, 0, i + 1)
                more(i * 2 + 1, 1)
                gather(i * 2 + 3, 1, i + 1)
            more(NB - 3, 0)
            gather(NB - 1, 0, (NB - 1) // 2)
            more(NB - 2, 1)
            more(NB - 1, 0)

        @block.scalar
        def _(act):
            for dst, src in ((s_wqk, wqk), (s_wkv, wkv), (fv, firstvec.broadcast_to([P, F_END])),
                             (rv, rowvec.broadcast_to([P, R_END])), (cv, colvec),
                             (s_wq, wq), (s_wo, wo), (s_w1, w1), (s_w2, w2), (s_rw, rw), (s_e1, ew1), (s_e2, ew2),
                             (s_eb2, eb2)):
                full = tuple(slice(None) for _ in dst.shape)
                act.dma_start(dst[full], src).then_inc(s_wload, 16)

            def f_evac(b, par, h):
                act.wait_ge(f_tr[0], at(f_tr, b))
                nc.scalar.activation(xt0[:, par, :], tr_ps[par][:, 0:2 * P], ACT.Copy).then_inc(f_xt[0], 1)

            def f_phi(b, par):
                act.wait_ge(f_qkb[0], at(f_qkb, b))
                nc.scalar.activation(nrow[:, par, CQ:CQ + SM], qkb[:, par, 0:SM], ACT.Tanh).then_inc(f_q[0], 1)
                act.wait_ge(f_km[0], at(f_km, b))
                nc.scalar.activation(km[:, par, :], km[:, par, :], ACT.Exp).then_inc(f_ke[0], 1)

            def f_step(b, par, h):
                f_evac(b, par, h)
                f_phi(b - 1, 1 - par)

            loop_steps(act, f_evac, f_step, lambda b, par, h: f_phi(b - 1, 1 - par))

            counter = act.alloc_register("v_count_act")
            act.reg_mov(counter, 0)
            act.wait_ge(s_ctl, 16)

            def onehots(s, G, g):
                act.wait_ge(G["tr"][0], at(G["tr"], s, g + 1))
                nc.scalar.activation(onehot[:, g * GT:(g + 1) * GT, :], b_t[g % 2][:, :, :], ACT.Identity,
                                     bias=1.0, scale=1.0 / BIG).then_inc(G["oh"][0], 1)

            def weights(s, par, G, q, first=False):
                if q == 0:
                    act.wait_ge(G["eb"][0], at(G["eb"], s))
                    nc.scalar.activation(sm[:, par, 5:6], sm[:, par, 4:5], ACT.Exp).then_inc(G["es"][0], 1)
                if q >= RING:
                    act.wait_ge(G["wu"][0], at(G["wu"], s, q - RING + 1))
                elif not first:
                    act.wait_ge(G["wu"][0], at(G["wu"], s - 1, NP - RING + q + 1))
                for j in range(q * PT, (q + 1) * PT):
                    ins = nc.scalar.activation(wgt[:, j % (RING * PT), :], farm[:, par, j, :], ACT.Exp,
                                               bias=ebias[:, par, j:j + 1])
                ins.then_inc(G["w"][0], 1)

            def front_parts(f):
                return {f"t{g}": (lambda g=g: onehots(f, M, g)) for g in range(NG)}

            def weight_parts(s, par, first):
                return {f"w{q}": (lambda q=q: weights(s, par, M, q, first)) for q in range(NP)}

            flat2 = lambda t: t[:, :, :].rearrange("p a b -> p (a b)")

            def dense_parts(b):
                def evac(dst, src, ready, done):
                    act.wait_ge(ready[0], at(ready, b))
                    nc.scalar.activation(dst, src, ACT.Copy).then_inc(done[0], 1)

                def phi():
                    act.wait_ge(d_qm[0], at(d_qm, b))
                    nc.scalar.activation(flat2(qm), flat2(qm), ACT.Exp).then_inc(d_qe[0], 1)

                def relu(half):
                    act.wait_ge(d_f1[0], at(d_f1, b, half + 1))
                    for m in range(4 * half, 4 * half + 4):
                        ins = nc.scalar.activation(hff[:, m, :], b_d[1 + half][:, m % 4 * P:(m % 4 + 1) * P], ACT.Relu,
                                                   bias=cv[:, V_FB1 + m:V_FB1 + m + 1])
                    ins.then_inc(d_h[0], 1)

                def router():
                    act.wait_ge(d_nm[0], at(d_nm, b))
                    nc.scalar.activation(rt[:, 0, :], b_d[0][:, 0:EXP], ACT.Exp, bias=rts[:, 0:1],
                                         accum_out=rts[:, 1:2]).then_inc(d_re[0], 1)

                def gelu(p):
                    act.wait_ge(d_eh[0], at(d_eh, b, p + 1))
                    for e in range(2):
                        for m in range(2):
                            c = V_EB1 + (2 * p + e) * 2 + m
                            ins = nc.scalar.activation(hex_[:, p % 2, e, m, :],
                                                       b_d[1 + p % 2][:, (2 * e + m) * P:(2 * e + m + 1) * P],
                                                       ACT.Gelu, bias=cv[:, c:c + 1])
                    ins.then_inc(d_eg[0], 1)

                turned = lambda ready, done: (lambda: evac(flat2(xt), b_d[0][:, 0:D], ready, done))
                return {
                    "xt": turned(d_t1, d_xt), "q": phi, "attT": turned(d_t2, d_attT), "x1T": turned(d_t3, d_x1T),
                    "f1a": lambda: relu(0), "f1b": lambda: relu(1), "xmT": turned(d_t4, d_xmT), "lg": router,
                    "h0": lambda: gelu(0), "h1": lambda: gelu(1), "h2": lambda: gelu(2), "h3": lambda: gelu(3),
                    "cT": lambda: evac(ct[:, :], b_m[0:EXP, 256:256 + P], d_ct, d_ctT),
                }

            def more(s, par):
                def body(k, c):
                    for g in range(NG):
                        onehots(k, V, g)
                    for q in range(NP):
                        weights(k, par, V, q, first=True)
                further_chunks(act, s, body, counter)

            def step(s, par, h, dense=True, after=True, masks_ahead=True):
                in_order(weight_parts(s, par, not dense), dense_parts(s - 1) if dense else {},
                         front_parts(s + 1) if after else {})
                more(s, par)

            pipeline(act, lambda s, par, h: in_order(front_parts(s)), step, lambda b, par, h: in_order(dense_parts(b)))

        @block.tensor
        def _(pe):
            pe.wait_ge(s_const, 1)
            pe.matmul(b_a[:, 0:2 * (P + 1)], zero[:, 0:P], zero, start=True, stop=False, skip_group_check=True)

            def f_tr_kv(b, par, acc_prev):
                pe.wait_ge(f_xn[0], at(f_xn, b))
                for c in range(2):
                    ins = pe.transpose(tr_ps[par][:, c * P:(c + 1) * P], nrow[:, par, c * P:(c + 1) * P], identf[:, :])
                ins.then_inc(f_tr[0], 1)
                if acc_prev is not None:
                    f_sum(*acc_prev)
                pe.wait_ge(f_xt[0], at(f_xt, b))
                for c in range(2):
                    pe.matmul(kv_ps[par][:, :], xt0[:, par, c * P:(c + 1) * P], s_wkv[:, c, :], start=(c == 0), stop=(c == 1))
                for c in range(2):
                    ins = pe.matmul(qk_ps[par], xt0[:, par, c * P:(c + 1) * P], s_wqk[:, c, :], start=(c == 0), stop=(c == 1))
                ins.then_inc(f_kv[0], 1)

            def f_sum(b, par, n=P):
                pe.wait_ge(f_kphi[0], at(f_kphi, b))
                for c in range(2):
                    ins = pe.matmul(kva_ps[:, c, :], kphi[0:n, par, c * P:(c + 1) * P], vaug[0:n, par, c, :],
                                    start=False, stop=(n < P), skip_group_check=True)
                ins.then_inc(f_acc[0], 1)

            pe.wait_ge(s_wload, 16 * 13)
            loop_steps(pe, lambda b, par, h: f_tr_kv(b, par, None),
                       lambda b, par, h: f_tr_kv(b, par, (b - 1, 1 - par)),
                       lambda b, par, h: f_sum(b - 1, 1 - par, LAST))

            pe.wait_ge(s_kvm, 1)
            counter = pe.alloc_register("v_count_pe")
            pe.reg_mov(counter, 0)
            pe.wait_ge(s_ctl, 16)

            def turn_mask(s, par, G, g):
                pe.wait_ge(G["far"][0], at(G["far"], s, g + 1))
                if g >= 2:
                    pe.wait_ge(G["oh"][0], at(G["oh"], s, g - 1))
                for j in range(GT):
                    ins = pe.transpose(b_t[g % 2][:, j, :], farm[:, par, g * GT + j, :], identb[:, :])
                ins.then_inc(G["tr"][0], 1)

            def keys(s, par, G, g):
                pe.wait_ge(G["oh"][0], at(G["oh"], s, g + 1))
                if g >= 1:
                    pe.wait_ge(G["ku"][0], at(G["ku"], s, g))
                for j in range(GT):
                    ins = pe.matmul(b_s[:, j * 3 * SM:(j + 1) * 3 * SM], onehot[:, g * GT + j, :], kcur[:, par, :],
                                    start=True, stop=True)
                ins.then_inc(G["ke"][0], 1)

            def turn_max(s, G):
                pe.wait_ge(G["mx"][0], at(G["mx"], s))
                pe.transpose(b_m[:, 0:P], mxr[:, :], identf[:, :]).then_inc(G["mt"][0], 1)

            def spread_max(s, G):
                pe.wait_ge(G["sh"][0], at(G["sh"], s))
                for j in range(CH):
                    ins = pe.matmul(b_m[:, P + 2 * j:P + 2 * j + 2], onehot[:, j, :], shift2[:, :], start=True, stop=True)
                ins.then_inc(G["me"][0], 1)

            def front_parts(f, par, h):
                def first_keys():
                    pe.wait_ge(M["key"][par], h * 16 + 16)
                    keys(f, par, M, 0)

                parts = {f"t{g}": (lambda g=g: turn_mask(f, par, M, g)) for g in range(NG)}
                parts.update({f"k{g}": (lambda g=g: keys(f, par, M, g)) for g in range(1, NG)})
                parts.update({"k0": first_keys, "mt": lambda: turn_max(f, M), "me": lambda: spread_max(f, M)})
                return parts

            def aggregate(s, par, G, q):
                pe.wait_ge(G["w"][0], at(G["w"], s, q + 1))
                for j in range(q * PT, (q + 1) * PT):
                    ins = pe.matmul(b_a[:, 0:AGG], wgt[:, j % (RING * PT), :], rows[:, par, j, 0:AGG],
                                    start=(j == 0), stop=(j == CH - 1))
                ins.then_inc(G["wu"][0], 1)

            def aggregate_parts(s, par, first):
                def first_group():
                    if not first:
                        pe.wait_ge(M["agg"][0], at(M["agg"], s - 1))
                    aggregate(s, par, M, 0)

                parts = {f"a{q}": (lambda q=q: aggregate(s, par, M, q)) for q in range(1, NP)}
                parts["a0"] = first_group
                return parts

            def dense_parts(b, par, h, merged):
                def transpose2(src, ready, done):
                    pe.wait_ge(*ready)
                    for c in range(2):
                        ins = pe.transpose(b_d[0][:, c * P:(c + 1) * P], src[:, c * P:(c + 1) * P], identf[:, :])
                    ins.then_inc(done[0], 1)

                def p_t1():
                    if not (isinstance(b, int) and b == 0):
                        pe.wait_ge(d_eu[0], at(d_eu, b - 1))
                    transpose2(xd[:, par, 1, :], (d_x[par], h * 32 + 32), d_t1)

                def p_q():
                    pe.wait_ge(d_xt[0], at(d_xt, b))
                    for m in range(2):
                        for c in range(2):
                            ins = pe.matmul(b_d[1][:, m * P:(m + 1) * P], s_wq[:, c, m * P:(m + 1) * P], xt[:, c, :],
                                            start=(c == 0), stop=(c == 1))
                    ins.then_inc(d_q[0], 1)

                def p_att():
                    pe.wait_ge(d_qphi[0], at(d_qphi, b))
                    for c in range(2):
                        ins = pe.matmul(b_d[2][:, c * (P + 4):(c + 1) * (P + 4)], qm[:, c, :], kvm[:, c, :],
                                        start=True, stop=True)
                    ins.then_inc(d_at[0], 1)

                def p_t2():
                    transpose2(att, (d_att[0], at(d_att, b)), d_t2)

                def p_o():
                    pe.wait_ge(d_attT[0], at(d_attT, b))
                    for c in range(2):
                        ins = pe.matmul(b_d[1][:, 0:D], xt[:, c, :], s_wo[:, c, :], start=(c == 0), stop=(c == 1))
                    ins.then_inc(d_o[0], 1)

                def p_t3():
                    transpose2(x1, (d_x1[0], at(d_x1, b)), d_t3)

                def p_f1(half):
                    if half == 0:
                        pe.wait_ge(d_x1T[0], at(d_x1T, b))
                    for m in range(4 * half, 4 * half + 4):
                        for c in range(2):
                            ins = pe.matmul(b_d[1 + half][:, m % 4 * P:(m % 4 + 1) * P], s_w1[:, c, m * P:(m + 1) * P],
                                            xt[:, c, :], start=(c == 0), stop=(c == 1))
                    ins.then_inc(d_f1[0], 1)

                def p_f2():
                    for m in range(FC):
                        if m % 4 == 0:
                            pe.wait_ge(d_h[0], at(d_h, b, m // 4 + 1))
                        ins = pe.matmul(b_d[0][:, 0:D], hff[:, m, :], s_w2[:, m, :], start=(m == 0), stop=(m == FC - 1))
                    ins.then_inc(d_f2[0], 1)

                def p_t4():
                    transpose2(xm, (d_xm[0], at(d_xm, b)), d_t4)

                def p_logits():
                    pe.wait_ge(d_xmT[0], at(d_xmT, b))
                    for c in range(2):
                        ins = pe.matmul(b_d[0][:, 0:EXP], xt[:, c, :], s_rw[:, c, :], start=(c == 0), stop=(c == 1))
                    ins.then_inc(d_lg[0], 1)

                def hidden(p):
                    if p >= 2:
                        pe.wait_ge(d_eg[0], at(d_eg, b, p - 1))
                    for e in range(2):
                        for m in range(2):
                            for c in range(2):
                                ins = pe.matmul(b_d[1 + p % 2][:, (2 * e + m) * P:(2 * e + m + 1) * P],
                                                s_e1[:, 2 * p + e, c, m * P:(m + 1) * P], xt[:, c, :],
                                                start=(c == 0), stop=(c == 1))
                    ins.then_inc(d_eh[0], 1)

                def outputs(p):
                    pe.wait_ge(d_eg[0], at(d_eg, b, p + 1))
                    if p == 0:
                        pe.wait_ge(d_re[0], at(d_re, b))
                    elif p == 1:
                        pe.wait_ge(M["agg"][0], at(M["agg"], merged))
                    else:
                        pe.wait_ge(d_eu[0], at(d_eu, b, p - 1))
                    for e in range(2):
                        for m in range(2):
                            ins = pe.matmul(b_y[p % 2][:, e * D:(e + 1) * D], hex_[:, p % 2, e, m, :],
                                            s_e2[:, 2 * p + e, m, :], start=(m == 0), stop=(m == 1))
                    ins.then_inc(d_ey[0], 1)

                def p_ct():
                    pe.wait_ge(d_cb[0], at(d_cb, b))
                    pe.transpose(b_m[0:EXP, 256:256 + P], rt[:, 1, :], identf[:, :]).then_inc(d_ct[0], 1)

                def p_b2():
                    pe.wait_ge(d_ctT[0], at(d_ctT, b))
                    pe.matmul(b_m[:, 256:512], ct[:, :], s_eb2[:, :], start=True, stop=True).then_inc(d_cb2[0], 1)

                parts = {f"h{p}": (lambda p=p: hidden(p)) for p in range(EXP // 2)}
                parts.update({f"y{p}": (lambda p=p: outputs(p)) for p in range(EXP // 2)})
                parts.update({"xt": p_t1, "q": p_q, "att": p_att, "attT": p_t2, "o": p_o, "x1T": p_t3,
                              "f1a": lambda: p_f1(0), "f1b": lambda: p_f1(1), "f2": p_f2, "xmT": p_t4, "lg": p_logits,
                              "cT": p_ct, "cb2": p_b2})
                return parts

            def more(s, par):
                def body(k, c):
                    for g in range(NG):
                        turn_mask(k, par, V, g)
                        if g >= 1:
                            keys(k, par, V, g - 1)
                    keys(k, par, V, NG - 1)
                    turn_max(k, V)
                    spread_max(k, V)
                    for q in range(NP):
                        aggregate(k, par, V, q)
                further_chunks(pe, s, body, counter)

            def step(s, par, h, dense=True, after=True, masks_ahead=True):
                in_order(aggregate_parts(s, par, not dense),
                         dense_parts(s - 1, 1 - par, h if par == 1 else h - 1, s) if dense else {},
                         front_parts(s + 1, 1 - par, h + 1 if par == 1 else h) if after else {})
                more(s, par)

            pipeline(pe, lambda s, par, h: in_order(front_parts(s, par, h)), step,
                     lambda b, par, h: in_order(dense_parts(b, par, h, b)))

        @block.vector
        def _(dve):
            v = nc.vector
            _, _, link, _ = chain_of(dve, (s_set, 0), 0)
            v.memset(zero, 0.0).then_inc(s_const, 1)
            link(v.memset(nrow[:, :, :], 0.0))
            v.memset(nrow[:, :, C1:C1 + 1], 1.0)
            v.memset(vaug[:, :, :, P:P + 1], 1.0)
            v.memset(kvm[:, :, :], 0.0)
            v.memset(base[:, :], 0.0)
            dve.wait_ge(s_dn, 16)
            v.tensor_reduce(t_tmp[:, 0:TPP], dn[:, :, :], AX.X, ALU.max).then_inc(s_trng, 1)
            v.tensor_reduce(t_tmp[:, TPP:2 * TPP], dn[:, :, :], AX.X, ALU.min).then_inc(s_trng, 1)
            dve.wait_ge(s_pool, 4)
            v.tensor_copy(iota_b[:, :], iota_i[:, 0:P])
            v.tensor_copy(iota8[:, :], iota_i[:, 0:EXP])
            v.tensor_copy(identb[:, :], identf[:, :])
            v.tensor_copy(t_idx, iota_i[:, :])
            v.tensor_scalar(cols[:, 0:1], coli[:, 0:1], 1.0, None, ALU.mult)
            v.tensor_scalar(cols[:, 1:2], coli[:, 0:1], float(P - 1), None, ALU.add)
            link(v.tensor_scalar(chunk_steps[:, :], iota_i[:, 0:48], float(CH), float(CH), ALU.mult, ALU.add))
            dve.wait_ge(s_rng_r, 32)
            link(v.tensor_scalar(t_tmp, t_idx, -1.0, float(NT), ALU.mult, ALU.add))
            link(v.scalar_tensor_tensor(t_tmp, t_max, cols[:, 0:1], t_tmp, ALU.is_ge, ALU.mult))
            link(v.tensor_reduce(cols[:, 2:3], t_tmp, AX.X, ALU.max))
            link(v.tensor_scalar(cols[:, 3:4], cols[:, 2:3], -1.0, float(NT), ALU.mult, ALU.add))
            link(v.tensor_scalar(t_tmp, t_idx, 1.0, None, ALU.add))
            link(v.scalar_tensor_tensor(t_tmp, t_min, cols[:, 1:2], t_tmp, ALU.is_le, ALU.mult))
            link(v.tensor_reduce(cols[:, 4:5], t_tmp, AX.X, ALU.max))
            link(v.tensor_scalar(cols[:, 3:4], cols[:, 3:4], float(EDGES // P), None, ALU.min))
            link(v.tensor_tensor(cols[:, 5:6], cols[:, 4:5], cols[:, 3:4], ALU.subtract))
            link(v.tensor_scalar(chunk_steps[:, :], chunk_steps[:, :], cols[:, 5:6], None, ALU.is_lt))
            link(v.tensor_reduce(cols[:, 6:7], chunk_steps[:, :], AX.X, ALU.add))
            v.tensor_copy(coli[:, 0:1], cols[:, 3:4])
            v.tensor_copy(coli[:, 1:2], cols[:, 6:7]).then_inc(s_blk, 1)

            dve.wait_ge(s_xload, 16)
            for b in range(NB):
                ins = v.bn_stats(st[:, b, :], xall[:, b, :])
            link(ins)
            mean, var, rstd, nmr, t1, t2 = [lnm[:, i, :] for i in range(6)]
            s_ = lambda i: st[:, :, i]
            v.tensor_tensor(t1, s_(1), s_(4), ALU.add)
            v.tensor_tensor(t2, s_(1), s_(4), ALU.subtract)
            link(v.tensor_tensor(var, s_(2), s_(5), ALU.add))
            v.tensor_scalar(mean, t1, 0.5, None, ALU.mult)
            link(v.tensor_tensor(t2, t2, t2, ALU.mult))
            link(v.tensor_scalar(t2, t2, 0.25, EPS, ALU.mult, ALU.add))
            link(v.scalar_tensor_tensor(var, var, 1.0 / D, t2, ALU.mult, ALU.add))

            def inv_sqrt(y, x, t):
                link(v.tensor_scalar(y.bitcast(I32), x.bitcast(I32), -0.5, float(0x5f3759df), ALU.mult, ALU.add))
                for _ in range(4):
                    link(v.tensor_tensor(t, y, y, ALU.mult))
                    link(v.tensor_tensor(t, t, x, ALU.mult))
                    link(v.tensor_scalar(t, t, -0.5, 1.5, ALU.mult, ALU.add))
                    link(v.tensor_tensor(y, y, t, ALU.mult))

            inv_sqrt(rstd, var, t1)
            link(v.scalar_tensor_tensor(nmr, mean, -1.0, rstd, ALU.mult, ALU.mult))
            dve.wait_ge(s_wload, 16 * 13)
            link(v.tensor_scalar(bq1[:, :], cv[:, V_BQ:V_BQ + 2], 1.0, None, ALU.add))

            def f_norm(b, par, h, first=False):
                if not (isinstance(b, int) and b == 0) and not first:
                    dve.wait_ge(f_st[par], h * 32)
                v.tensor_scalar(nrow[:, par, 0:D], xall[:, b, :], rstd[:, bass.ds(b, 1)], nmr[:, bass.ds(b, 1)],
                                ALU.mult, ALU.add).then_inc(f_xn[0], 1)

            def f_rest(b, par):
                tick, wait, link, close = chain_of(dve, f_chain, b)
                dve.wait_ge(f_kv[0], at(f_kv, b))
                v.tensor_tensor(qkb[:, par, :], qk_ps[par], fv[:, R_BQK:R_BQK + 2 * SM], ALU.add).then_inc(f_qkb[0], 1)
                link(v.tensor_tensor(kb[:, par, :], kv_ps[par][:, 0:D], fv[:, R_BK:R_BK + D], ALU.add))
                v.tensor_scalar(km[:, par, :], kb[:, par, :], 0.0, None, ALU.min).then_inc(f_km[0], 1)
                v.tensor_tensor(vaug[:, par, :, 0:P], kv_ps[par][:, D:2 * D].rearrange("p (c n) -> p c n", c=2),
                                fv[:, R_BV:R_BV + D].rearrange("p (c n) -> p c n", c=2), ALU.add)
                dve.wait_ge(f_qkb[0], at(f_qkb, b))
                link(v.tensor_scalar(kf[:, :], qkb[:, par, SM:2 * SM], 1.0 / 5.0, None, ALU.mult))
                link(v.tensor_copy(krow[:, par, 0:SM], kf[:, :]))
                link(v.tensor_tensor(kr[:, 0, :], kf[:, :], krow[:, par, 0:SM], ALU.subtract))
                link(v.tensor_copy(krow[:, par, SM:2 * SM], kr[:, 0, :]))
                link(v.tensor_tensor(kr[:, 1, :], kr[:, 0, :], krow[:, par, SM:2 * SM], ALU.subtract))
                v.tensor_copy(krow[:, par, 2 * SM:3 * SM], kr[:, 1, :])
                dve.wait_ge(f_q[0], at(f_q, b))
                link(v.tensor_tensor(qkp[:, :], nrow[:, par, CQ:CQ + SM], kf[:, :], ALU.mult))
                v.tensor_reduce(nrow[:, par, CW:CW + 1], qkp[:, :], AX.X, ALU.add).then_inc(f_row[0], 1)
                dve.wait_ge(f_ke[0], at(f_ke, b))
                v.scalar_tensor_tensor(kphi[:, par, :], kb[:, par, :], 1.0, km[:, par, :], ALU.add,
                                       ALU.max).then_inc(f_kphi[0], 1)
                close()


            def f_step(b, par, h):
                f_norm(b, par, h)
                f_rest(b - 1, 1 - par)

            loop_steps(dve, f_norm, f_step, lambda b, par, h: f_rest(b - 1, 1 - par))

            dve.wait_ge(f_acc[0], at(f_acc, NB - 1))
            for c in range(2):
                for q in range(4):
                    r = slice(HD * q, HD * (q + 1))
                    v.tensor_copy(kvm[r, c, r], kva_ps[r, c, r])
                    ins = v.tensor_copy(kvm[r, c, P + q:P + q + 1], kva_ps[r, c, P:P + 1])
            ins.then_inc(s_kvm, 1)
            dve.wait_ge(s_kvm, 1)

            counter = dve.alloc_register("v_count_dve")
            dve.reg_mov(counter, 0)
            dve.wait_ge(s_ctl, 16)

            def masks(s, par, place, seen, G, replaced=None):
                _, _, link, close = chain_of(dve, G["loc"], s)
                dve.wait_ge(G["idx"][place], seen)
                if G is M and not (isinstance(s, int) and s == 0):
                    dve.wait_ge(M["far"][0], at(M["far"], s - 1))
                b = 0 if G is M else 1
                link(v.tensor_scalar(dloc[:, :], dst_i[:, place, :], base[:, b:b + 1], None, ALU.subtract))
                link(v.tensor_scalar(base[:, b:b + 1], base[:, b:b + 1], float(P) if G is M else 0.0, None, ALU.add))
                close()
                for g in range(NG):
                    if replaced is not None:
                        dve.wait_ge(M["w"][0], at(M["w"], replaced, (g * GT + GT + PT - 1) // PT))
                    for j in range(g * GT, (g + 1) * GT):
                        ins = one_mask(par, j)
                        if j == (g + 1) * GT - 1:
                            ins.then_inc(G["far"][0], 1)
                        yield

            def one_mask(par, j):
                return v.tensor_scalar(farm[:, par, j, :], iota_b[:, :], dloc[:, j:j + 1], -BIG, ALU.not_equal, ALU.mult)

            def finish(mask):
                for _ in mask:
                    pass

            def graph_front(s, par, place, h, G, start_cols, own_loaded=None):
                tick, wait, link, close = chain_of(dve, G["chain"], s)
                c = lambda i: sm[:, par, i:i + 1]

                def scores(g):
                    dve.wait_ge(G["ke"][0], at(G["ke"], s, g + 1))
                    dve.wait_ge(G["gat"][place][g], h * (GT * 16) + GT * 16)
                    v.tensor_tensor(
                        prod[:, :, :].rearrange("p t (a k) -> p t a k", a=3),
                        b_s[:, 0:GT * 3 * SM].rearrange("p (t a k) -> p t a k", t=GT, a=3),
                        rows[:, par, g * GT:(g + 1) * GT, CQ:CQ + SM].unsqueeze(2).broadcast_to([P, GT, 3, SM]),
                        ALU.mult).then_inc(G["ku"][0], 1)
                    dve.wait_ge(G["ku"][0], at(G["ku"], s, g + 1))
                    link(v.tensor_reduce(score[:, g * GT:(g + 1) * GT], prod[:, :, :], AX.X, ALU.add))
                    for j in range(g * GT, (g + 1) * GT):
                        k = j % GT
                        if g == 0:
                            ins = v.tensor_scalar(mx[:, k, :], farm[:, par, j, :], score[:, j:j + 1], None, ALU.add)
                        else:
                            ins = v.scalar_tensor_tensor(mx[:, k, :], farm[:, par, j, :], score[:, j:j + 1], mx[:, k, :],
                                                         ALU.add, ALU.max)
                    tick(ins)

                def greatest():
                    wait()
                    v.tensor_reduce(mxr[:, :], mx[:, :, :].rearrange("p k n -> p n k"), AX.X, ALU.max).then_inc(G["mx"][0], 1)

                def shift():
                    if own_loaded is not None:
                        dve.wait_ge(own_loaded, h * 16 + 16)
                    dve.wait_ge(G["mt"][0], at(G["mt"], s))
                    link(v.tensor_reduce(c(0), b_m[:, 0:P], AX.X, ALU.max))
                    link(v.tensor_tensor(c(1), c(0), start_cols, ALU.max))
                    link(v.tensor_copy(shift2[:, 0:1], c(1)))
                    link(v.tensor_tensor(c(2), c(1), shift2[:, 0:1], ALU.subtract))
                    v.tensor_copy(shift2[:, 1:2], c(2)).then_inc(G["sh"][0], 1)
                    dve.wait_ge(G["sh"][0], at(G["sh"], s))
                    link(v.tensor_tensor(c(3), shift2[:, 0:1], shift2[:, 1:2], ALU.add))
                    tick(v.tensor_tensor(c(4), start_cols, c(3), ALU.subtract))

                def bias():
                    dve.wait_ge(G["me"][0], at(G["me"], s))
                    spread = b_m[:, P:P + 2 * CH].rearrange("p (j a) -> p j a", a=2)
                    link(v.tensor_tensor(ebias[:, par, :], score[:, :], spread[:, :, 0], ALU.subtract))
                    v.tensor_tensor(ebias[:, par, :], ebias[:, par, :], spread[:, :, 1], ALU.subtract).then_inc(G["eb"][0], 1)
                    close()

                parts = {f"k{g}": (lambda g=g: scores(g)) for g in range(NG)}
                parts.update({"mx": greatest, "mt": shift, "me": bias})
                return parts

            def graph_merge(s, par, G, old):
                dve.wait_ge(G["wu"][0], at(G["wu"], s))
                dve.wait_ge(G["es"][0], at(G["es"], s))
                v.tensor_copy(sm[:, par, 6:7], sm[:, par, 3:4])
                v.scalar_tensor_tensor(acc[:, par, :], old, sm[:, par, 5:6], b_a[:, 0:AGG], ALU.mult,
                                       ALU.add).then_inc(G["agg"][0], 1)

            def front(s, par, h):
                return graph_front(s, par, par, h, M, own[:, par, CW:CW + 1], M["own"][par])

            def more(s, par, restore):
                def body(k, c):
                    finish(masks(k, par, 2, k * 32 + 32, V))
                    in_order(graph_front(k, par, 2, k, V, sm[:, par, 6:7]))
                    graph_merge(k, par, V, acc[:, par, :])
                    if restore:
                        dve.wait_ge(V["agg"][0], at(V["agg"], k))
                        v.tensor_scalar(dloc[:, :], dst_i[:, par, :], base[:, 1:2], -2.0 * P, ALU.subtract,
                                        ALU.add).then_inc(v_again[0], 1)
                        dve.wait_ge(v_again[0], at(v_again, k))
                        for j in range(CH):
                            one_mask(par, j)
                further_chunks(dve, s, body, counter)
                dve.wait_ge(M["agg"][0], at(M["agg"], s))
                v.tensor_scalar(base[:, 1:2], base[:, 1:2], float(P), None, ALU.add).then_inc(b_sig[0], 1)
                dve.wait_ge(b_sig[0], at(b_sig, s))

            def layer_norm(link, dst, src, k, g=None, bias=None):
                s6, r, t = lns[:, k, 0:6], lns[:, k, 8:9], lns[:, k, 9:10]
                link(v.bn_stats(s6, src), hold=True)
                link(v.bn_aggr(lns[:, k, 6:8], s6))
                x = lns[:, k, 7:8]
                link(v.tensor_scalar(x, x, 2.0 ** 26, EPS * 2.0 ** 26, ALU.mult, ALU.add))
                link(v.tensor_scalar(r.bitcast(I32), x.bitcast(I32), -0.5, float(0x5f3759df - 2 ** 31), ALU.mult, ALU.add))
                for factor in (1.0, 2.0, 16.0):
                    link(v.tensor_scalar(t, r, r, x, ALU.mult, ALU.mult))
                    link(v.scalar_tensor_tensor(r, t, -3.0 * factor * factor, r, ALU.add, ALU.mult))
                ins = v.tensor_scalar(dst, src, lns[:, k, 6:7], r, ALU.subtract, ALU.mult)
                if g is not None:
                    link(ins)
                    link(v.tensor_tensor(dst, dst, g, ALU.mult))
                    ins = v.tensor_tensor(dst, dst, bias, ALU.add)
                return ins

            def dense_parts(b, par, h, mask):
                tick, wait, link, close = chain_of(dve, d_chain, b, lambda: fence(dve))

                def link_mask(ins, hold=False):
                    tick(ins)
                    next(mask, None)
                    wait()
                    if hold:
                        fence(dve)

                def q_min():
                    dve.wait_ge(d_q[0], at(d_q, b))
                    for m in range(2):
                        ins = v.tensor_scalar(qm[:, m, :], b_d[1][:, m * P:(m + 1) * P], cv[:, V_BQ + m:V_BQ + m + 1], 0.0,
                                              ALU.add, ALU.min)
                    ins.then_inc(d_qm[0], 1)

                def q_phi():
                    dve.wait_ge(d_qe[0], at(d_qe, b))
                    for m in range(2):
                        ins = v.scalar_tensor_tensor(qm[:, m, :], b_d[1][:, m * P:(m + 1) * P], bq1[:, m:m + 1], qm[:, m, :],
                                                     ALU.add, ALU.max)
                    ins.then_inc(d_qphi[0], 1)
                    dve.wait_ge(d_x[par], h * 32 + 32)
                    tick(v.tensor_tensor(y1, xd[:, par, 1, :], rv[:, R_BO:R_BO + D], ALU.add))

                def attention():
                    dve.wait_ge(d_at[0], at(d_at, b))
                    num = b_d[2][:, 0:2 * (P + 4)].rearrange("p (c n) -> p c n", c=2)
                    link(v.tensor_scalar(den[:, 0, :].rearrange("p (c h) -> p c h", c=2), num[:, :, P:P + 4], 1e-6,
                                         None, ALU.add))
                    link(v.reciprocal(den[:, 1, :], den[:, 0, :]))
                    for c in range(2):
                        ins = v.tensor_tensor(att[:, c * P:(c + 1) * P].rearrange("p (h d) -> p h d", h=4),
                                              num[:, c, 0:P].rearrange("p (h d) -> p h d", h=4),
                                              den[:, 1, 4 * c:4 * c + 4].unsqueeze(2).broadcast_to([P, 4, HD]), ALU.mult)
                    ins.then_inc(d_att[0], 1)

                def norm_1():
                    dve.wait_ge(d_o[0], at(d_o, b))
                    link(v.tensor_tensor(y1, b_d[1][:, 0:D], y1, ALU.add))
                    layer_norm(link, x1, y1, 0, rv[:, R_G1:R_G1 + D], rv[:, R_B1:R_B1 + D]).then_inc(d_x1[0], 1)
                    dve.wait_ge(d_x1[0], at(d_x1, b))
                    tick(v.tensor_tensor(y1, x1, rv[:, R_F2:R_F2 + D], ALU.add))
                    link(v.reciprocal(rl[:, :], acc[:, par, D:D + 1]))
                    link(v.scalar_tensor_tensor(xr, acc[:, par, 0:D], rl[:, 0:1], xd[:, par, 0, :], ALU.mult, ALU.add))

                def norm_2_3():
                    dve.wait_ge(d_f2[0], at(d_f2, b))
                    link_mask(v.tensor_tensor(y1, b_d[0][:, 0:D], y1, ALU.add))
                    link_mask(layer_norm(link_mask, x1, y1, 1, rv[:, R_G2:R_G2 + D], rv[:, R_B2:R_B2 + D]))
                    link_mask(v.tensor_tensor(xr, xr, x1, ALU.add))
                    layer_norm(link_mask, xm, xr, 2).then_inc(d_xm[0], 1)
                    dve.wait_ge(d_xm[0], at(d_xm, b))
                    tick(v.tensor_tensor(xr, xr, xm, ALU.add))

                def logits():
                    dve.wait_ge(d_lg[0], at(d_lg, b))
                    v.tensor_reduce(rts[:, 0:1], b_d[0][:, 0:EXP], AX.X, ALU.max, negate=True).then_inc(d_nm[0], 1)

                def router():
                    dve.wait_ge(d_re[0], at(d_re, b))
                    link_mask(v.reciprocal(rts[:, 2:3], rts[:, 1:2]))
                    link_mask(v.tensor_scalar(rt[:, 2, :], rt[:, 0, :], rts[:, 2:3], None, ALU.mult), hold=True)
                    link_mask(v.max(rt[:, 3, :], rt[:, 2, :]), hold=True)
                    tick(v.max_index(ridx[:, :], rt[:, 3, :], rt[:, 2, :]))
                    link_mask(v.tensor_tensor(rts[:, 3:4], rt[:, 3, 0:1], rt[:, 3, 1:2], ALU.add))
                    link_mask(v.tensor_scalar(rts[:, 3:4], rts[:, 3:4], 1e-12, None, ALU.max))
                    link_mask(v.reciprocal(rts[:, 4:5], rts[:, 3:4]))
                    link_mask(v.tensor_scalar(rt[:, 3, 0:2], rt[:, 3, 0:2], rts[:, 4:5], None, ALU.mult))
                    link_mask(v.tensor_copy(rts[:, 5:7], ridx[:, 0:2]))
                    tick(v.tensor_scalar(rt[:, 0, :], iota8[:, :], rts[:, 5:6], rt[:, 3, 0:1], ALU.is_equal, ALU.mult))
                    link_mask(v.tensor_scalar(rt[:, 2, :], iota8[:, :], rts[:, 6:7], rt[:, 3, 1:2], ALU.is_equal, ALU.mult))
                    v.tensor_tensor(rt[:, 1, :], rt[:, 0, :], rt[:, 2, :], ALU.add).then_inc(d_cb[0], 1)
                    finish(mask)
                    dve.wait_ge(d_cb[0], at(d_cb, b))

                def add_experts(p):
                    dve.wait_ge(d_ey[0], at(d_ey, b, p + 1))
                    if p == 3 and not (isinstance(b, int) and b == 0):
                        dve.wait_ge(d_out, b * 16)
                    for e in range(2):
                        i = 2 * p + e
                        dst = res[:, :] if i == EXP - 1 else xr
                        ins = v.scalar_tensor_tensor(dst, b_y[p % 2][:, e * D:(e + 1) * D], rt[:, 1, i:i + 1], xr, ALU.mult, ALU.add)
                        if e == 0:
                            link(ins)
                    ins.then_inc(d_eu[0], 1)
                    dve.wait_ge(d_eu[0], at(d_eu, b, p + 1))
                    if p == 3:
                        close()

                def add_b2():
                    dve.wait_ge(d_cb2[0], at(d_cb2, b))
                    link(v.tensor_tensor(xr, b_m[:, 256:512], xr, ALU.add))

                parts = {f"y{p}": (lambda p=p: add_experts(p)) for p in range(EXP // 2)}
                parts.update({"q": q_min, "qphi": q_phi, "att": attention, "o": norm_1, "f2": norm_2_3, "lg": logits,
                              "rt": router, "cb2": add_b2})
                return parts

            def front_alone(s, par, h):
                finish(masks(0, 0, 0, 32, M))
                finish(masks(1, 1, 1, 32, M))
                in_order(front(s, par, h))

            def step(s, par, h, dense=True, after=True, masks_ahead=True):
                ahead = masks(s + 2, par, par, (h + 2) * 32, M, s) if masks_ahead else iter(())
                merge = {"mg": lambda: graph_merge(s, par, M, own[:, par, 0:AGG])}
                scores = front(s + 1, 1 - par, h + 1 if par == 1 else h) if after else {}
                if dense:
                    in_order(dense_parts(s - 1, 1 - par, h if par == 1 else h - 1, ahead), merge, scores)
                else:
                    in_order(merge, scores)
                    finish(ahead)
                more(s, par, masks_ahead)

            pipeline(dve, front_alone, step, lambda b, par, h: in_order(dense_parts(b, par, h, iter(()))))


def kernel(**inputs):
    import concourse.bacc as bacc
    from concourse.bass_utils import run_bass_kernel_spmd

    g = {k: np.asarray(a) for k, a in inputs.items()}
    halves = lambda w: np.ascontiguousarray(w.reshape(w.shape[0] // P, P, -1).transpose(1, 0, 2))
    column = lambda a: a.reshape(-1, P).T
    edges = np.full(NT * P - EDGES, FAR, g["dst"].dtype)
    dst = np.concatenate([g["dst"], edges])
    src = np.concatenate([g["src"], np.zeros_like(edges)])
    experts = lambda w: np.ascontiguousarray(w.reshape(EXP, 2, P, D).transpose(2, 0, 1, 3))
    arrays = {
        "xpad": np.concatenate([g["x"], np.zeros((NPAD - NODES, D), g["x"].dtype)]),
        "src_t": np.ascontiguousarray(src.reshape(NT, P).T),
        "dst_t": np.ascontiguousarray(dst.reshape(NT, P).T),
        "dst_n": dst.reshape(P, TPP, P),
        "rowvec": np.concatenate([g[k] for k in (
            "L0_mix_bo", "L0_mix_ln1_g", "L0_mix_ln1_b", "L0_mix_ln2_g", "L0_mix_ln2_b",
            "L0_mix_b2")])[None],
        "firstvec": np.concatenate([g[k] for k in ("L0_mix_bk", "L0_mix_bv", "L0_gnn_bq", "L0_gnn_bk")])[None],
        "colvec": np.ascontiguousarray(np.concatenate(
            [column(g["L0_mix_bq"]), column(g["L0_mix_b1"]), column(g["L0_ffn_b1"])], axis=1)),
        "wqk": halves(np.concatenate([g["L0_gnn_Wq"], g["L0_gnn_Wk"]], axis=1)),
        "wq": halves(g["L0_mix_Wq"]),
        "wkv": halves(np.concatenate([g["L0_mix_Wk"], g["L0_mix_Wv"]], axis=1)),
        "wo": halves(g["L0_mix_Wo"]),
        "w1": halves(g["L0_mix_W1"]),
        "w2": halves(g["L0_mix_W2"]),
        "rw": halves(np.ascontiguousarray(g["L0_ffn_router_w"].T)),
        "ew1": experts(g["L0_ffn_w1"]),
        "ew2": experts(g["L0_ffn_w2"]),
        "eb2": g["L0_ffn_b2"],
    }
    nc = bacc.Bacc("TRN2", target_bir_lowering=False, num_devices=1)
    args = [nc.dram_tensor(f"in_{k}", a.shape, mybir.dt.from_np(a.dtype), kind="ExternalInput").ap() for k, a in arrays.items()]
    out = nc.dram_tensor("out_0", (NPAD, D), F32, kind="ExternalOutput").ap()
    graph_block(nc, *args, out)
    r = run_bass_kernel_spmd(nc, [{f"in_{k}": a for k, a in arrays.items()}], core_ids=[0])
    return r.results[0]["out_0"][:NODES]
```

```python
from contextlib import ExitStack

import numpy as np

import concourse.bass as bass
from concourse import mybir

F32 = mybir.dt.float32
BF16 = mybir.dt.bfloat16
I32 = mybir.dt.int32
U32 = mybir.dt.uint32
ALU = mybir.AluOpType
ACT = mybir.ActivationFunctionType
AX = mybir.AxisListType

P = 128
NODES, D = 6250, 256
NB = (NODES + P - 1) // P
NPAD = NB * P
LAST = NODES - (NB - 1) * P
EDGES = 206250
TPP = 13
NT = TPP * P
CH = 36
GT = 6
NG = CH // GT
PT = 4
NP = CH // PT
LATE = 4
RING = 3
SM = 25
ROW = 284
C1, CQ, CW = D, D + 1, D + 1 + SM
AGG = D + 1
HEADS, HD = 8, 32
FF = 1024
FC = FF // P
EXP = 8
EPS = 1e-5
D_CHAIN = 57
XC = 7
BIG = float(2.0 ** 100)
FAR = 1 << 14

R_BO, R_G1, R_B1, R_G2, R_B2, R_F2 = [D * i for i in range(6)]
R_END = 6 * D
R_BK, R_BV, R_BQK = 0, D, 2 * D
F_END = R_BQK + 2 * SM
V_BQ, V_FB1, V_EB1 = 0, 2, 2 + FC
V_END = V_EB1 + 2 * EXP
ORDER = """xt t0 q qphi w0 y2 w1 e0 s2 att y3 w2 s3 a0 attT nb t1 k0 e1 w3 a1 o w4 t2 a2 w5 e2 a3 w6 a4 c x1T w7 t3
           e3 k1 f1a k2 f1b k3 f2a t4 f2b e4 a5 w8 a6 a7 a8 t5 e5 mg k4 xmT lg h0 rt h1 k5 h2 y0 cT mx h3 mt cb2 s0
           y1 s1 me""".split()


def at(signal, step, n=None):
    _, per = signal
    return step * per + (per if n is None else n)


def chain_of(eng, signal, step, fence=None):
    semaphore, per = signal
    count = [0]

    def tick(ins):
        count[0] += 1
        ins.then_inc(semaphore, 1)
        return count[0]

    def wait(n=None):
        eng.wait_ge(semaphore, at(signal, step, count[0] if n is None else n))

    def link(ins, hold=False):
        tick(ins)
        wait()
        if hold:
            fence()

    def close():
        assert count[0] == per, (count[0], per)

    return tick, wait, link, close


def graph_block(nc, xpad, src_t, dst_t, dst_n, rowvec, firstvec, colvec, wqk, wq, wkv, wo, w1, w2, rw, ew1, ew2, eb2, out):
    ctx = ExitStack()
    with ctx:
        def sb(name, shape, dt=F32):
            return ctx.enter_context(nc.sbuf_tensor(name, shape, dt))

        def ps(name, shape, dt=F32):
            return ctx.enter_context(nc.psum_tensor(name, shape, dt))

        def sem(name):
            return ctx.enter_context(nc.semaphore(name))

        def sig(name, per=1):
            return sem(name), per

        table = nc.dram_tensor("node_table", (NPAD, ROW), F32).ap()
        knode = nc.dram_tensor("node_keys", (NPAD, 3 * SM), BF16).ap()
        tile_rng = nc.dram_tensor("tile_range", (2, NT), F32).ap()
        blk_rng = nc.dram_tensor("block_range", (2, P), I32).ap()

        rows = sb("gathered_rows", [P, 2, CH, ROW])
        flat = rows[:, :, :, :].rearrange("p a b c -> p (a b c)")
        xall = flat[:, 0:NB * D].rearrange("p (b d) -> p b d", d=D)
        o = NB * D
        t_max, t_min, t_idx, t_tmp = [flat[:, o + i * NT:o + (i + 1) * NT] for i in range(4)]
        farm = sb("far_mask", [P, 2, CH, P], BF16)
        onehot = sb("onehot_t", [P, CH, P], BF16)
        wgt = sb("weights", [P, RING * PT, P])
        mx = sb("max_partial", [P, GT, P])
        mxr = sb("max_rows", [P, P])
        pflat = sb("score_products", [P, 8 * SM])
        prod = pflat[:, 0:GT * SM].rearrange("p (t k) -> p t k", k=SM)
        score = sb("scores", [P, CH])
        ebias = sb("exp_bias", [P, 2, CH])
        src_i = sb("src_idx", [P, 3, CH], I32)
        dst_i = sb("dst_idx", [P, 3, CH], I32)
        dloc = sb("dst_local", [P, CH])
        base = sb("block_base", [P, 2])
        kcur = sb("block_keys", [P, 2, 3 * SM], BF16)
        own = sb("own_rows", [P, 2, ROW])
        acc = sb("aggregate", [P, 2, AGG])
        shift2 = sb("shift_parts", [P, 2], BF16)
        sm = sb("softmax_cols", [P, 2, 8])
        iota_b = sb("iota_b", [P, P], BF16)
        identf = sb("ident_f", [P, P])
        identb = sb("ident_b", [P, P], BF16)
        zero = acc[:, :, :].rearrange("p a b -> p (a b)")[:, 0:2 * (P + 1)]
        ctl = sb("control", [1, 2 * P], I32)
        cols = sb("range_cols", [P, 8])
        coli = sb("range_cols_i", [P, 2], I32)
        chunk_steps = sb("chunk_steps", [P, 48])
        s_wqk = sb("w_graph_qk", [P, 2, 2 * SM])
        s_wq = sb("w_mix_q", [P, 2, D])
        s_wo = sb("w_mix_o", [P, 2, D])
        s_w1 = sb("w_ff1", [P, 2, FF])
        s_w2 = sb("w_ff2", [P, FC, D])
        s_rw = sb("w_router", [P, 2, EXP])
        s_e1 = sb("w_expert1", [P, EXP, 2, D])
        s_e2 = sb("w_expert2", [P, EXP, 2, D])
        s_eb2 = sb("b_expert2", [EXP, D])
        rv = sb("row_vectors", [P, R_END])
        cv = sb("col_vectors", [P, V_END])
        bq1 = sb("bq_plus_1", [P, 2])
        bqn = sb("bq_negated", [P, 2])
        o += 4 * NT
        st = flat[:, o:o + 6 * NB].rearrange("p (b s) -> p b s", s=6)
        lnm = flat[:, o + 6 * NB:o + 12 * NB].rearrange("p (s b) -> p s b", s=6)
        nrow = t_max[:, 0:4 * ROW].rearrange("p (a c) -> p a c", a=4)
        krow = sb("node_key_parts", [P, 4, 3 * SM], BF16)
        wflat = wgt[:, :, :].rearrange("p a b -> p (a b)")
        kb, km, kphi = [wflat[:, i * 2 * D:(i + 1) * 2 * D].rearrange("p (a b) -> p a b", a=2) for i in range(3)]
        vaug = mx[:, :, :].rearrange("p a b -> p (a b)")[:, 0:4 * (P + 1)].rearrange("p (a b c) -> p a b c", a=2, b=2)
        dn = onehot[:, 0:2 * TPP, :].rearrange("p a b -> p (a b)").bitcast(I32).rearrange("p (a b) -> p a b", b=P)
        iota_i = farm[:, 0, 0:2 * TPP, :].rearrange("p a b -> p (a b)").bitcast(I32)
        qkb = pflat[:, 0:4 * SM].rearrange("p (a b) -> p a b", a=2)
        kr = pflat[:, 4 * SM:6 * SM].rearrange("p (a b) -> p a b", a=2)
        kf, qkp = pflat[:, 6 * SM:7 * SM], pflat[:, 7 * SM:8 * SM]
        kvm = sb("kv_blocks", [P, 2, P + 4])
        xd = sb("block_x", [P, 2, 2, D])
        xt = sb("xn_t", [P, 2, P])
        qm = sb("q_min", [P, 2, P])
        den = sb("attn_den", [P, 2, HEADS])
        att = sb("attn", [P, D])
        rowsum = sb("block_rows", [P, 4, D])
        y1, x1, xr, xm = [rowsum[:, i, :] for i in range(4)]
        s_wkv = rowsum[:, :, :].rearrange("p (c a) d -> p c (a d)", c=2)
        fv = xd[:, :, :, :].rearrange("p a b d -> p (a b d)")[:, 0:F_END]
        hff = sb("h_ff", [P, FC, P])
        xt0 = hff[:, 0:4, :].rearrange("p a b -> p (a b)").rearrange("p (a b) -> p a b", a=2)
        quarters = hff[:, :, :].rearrange("p (a b c) n -> p a b c n", a=2, b=2)
        third = rowsum[:, 0:2, :].rearrange("p b (c n) -> p b c n", c=2)
        hex_ = [quarters[:, 0], quarters[:, 1], third, quarters[:, 0]]
        warm = sb("table_warm", [P, 1])
        res = sb("result", [P, D])
        lns = sb("ln_small", [P, 3, 12])
        rt = sb("router", [P, 4, EXP])
        rts = sb("router_small", [P, 8])
        ridx = sb("router_idx", [P, 8], U32)
        ct = sb("combine_t", [EXP, P])
        iota8 = sb("iota8", [P, EXP])
        rl = sb("inv_sum", [P, 1])

        b_t = [ps(f"bank_t{i}", [P, GT, P], BF16) for i in range(2)]
        b_s = ps("bank_scores", [P, 512])
        b_m = ps("bank_max", [P, 512])
        b_a = ps("bank_agg", [P, 512])
        b_d = [ps(f"bank_d{i}", [P, 512]) for i in range(3)]
        b_c = b_d[1]
        b_y = [b_d[0], b_a, b_a, b_d[0]]
        tr_ps = [b_s, b_m]
        kv_ps = [b_d[0], b_d[1]]
        qk_ps = [b_d[2][:, 0:2 * SM], b_t[0][:, :, :].rearrange("p a b -> p (a b)").bitcast(F32)[:, 0:2 * SM]]
        kva_ps = b_a[:, 0:2 * (P + 1)].rearrange("p (c n) -> p c n", c=2)

        s_fload, s_wload, s_xload, s_dn = sem("first_weights_loaded"), sem("weights_loaded"), [sem(f"x_loaded{i}") for i in range(XC)], sem("dst_tiles_loaded")
        s_const = sem("constants_ready")
        s_pool = sem("pool_constants_ready")
        s_rng_w, s_rng_r, s_trng = sem("tile_range_stored"), sem("tile_range_loaded"), sem("tile_range_ready")
        s_blk, s_blk_w, s_ctl = sem("block_range_ready"), sem("block_range_stored"), sem("control_loaded")
        s_set = sem("dve_setup_chain")
        s_kvz, s_kvm = sem("kv_zeroed"), sem("kv_blocks_ready")
        f_xn, f_tr, f_xt, f_kv = sig("f_xn_ready"), sig("f_transposed"), sig("f_xt_ready"), sig("f_kv_ready")
        f_km, f_ke, f_kphi, f_acc = sig("f_k_biased"), sig("f_kexp_ready"), sig("f_kphi_ready"), sig("f_kv_added")
        f_qkb, f_q, f_row = sig("f_qk_biased"), sig("f_q_ready"), sig("f_row_ready")
        f_kr = sig("f_kmin_negated")
        f_st = [sem(f"f_rows_stored{i}") for i in range(4)]
        f_chain = sig("f_dve_chain", 6)

        def graph_signals(tag, places):
            return {
                "idx": {i: sem(f"{tag}_edges_loaded{i}") for i in places},
                "key": {i: sem(f"{tag}_keys_loaded{i}") for i in places},
                "own": {i: sem(f"{tag}_own_loaded{i}") for i in places},
                "gat": {i: [sem(f"{tag}_rows_gathered{i}_{g}") for g in range(NG)] for i in places},
                "far": sig(f"{tag}_far_mask_ready", NG),
                "tr": sig(f"{tag}_mask_transposed", NG),
                "oh": sig(f"{tag}_onehot_ready", NG),
                "ke": sig(f"{tag}_keys_spread", NG),
                "ku": sig(f"{tag}_keys_used", NG),
                "mx": sig(f"{tag}_max_rows_ready"),
                "mt": sig(f"{tag}_max_transposed"),
                "sh": sig(f"{tag}_shift_ready"),
                "me": sig(f"{tag}_shift_spread"),
                "eb": sig(f"{tag}_exp_bias_ready"),
                "es": sig(f"{tag}_old_scale_ready"),
                "w": sig(f"{tag}_weights_ready", NP),
                "wu": sig(f"{tag}_weights_used", NP),
                "agg": sig(f"{tag}_aggregate_ready"),
                "chain": sig(f"{tag}_dve_chain", 2 * NG + 7),
                "loc": sig(f"{tag}_dst_local_ready", 2),
            }

        M = graph_signals("m", (0, 1))
        V = graph_signals("v", (2,))
        v_meet = sem("v_engines_meet")
        s_fence = sem("wait_carried")

        d_x = [sem("d_x_loaded0"), sem("d_x_loaded1")]
        d_out = sem("d_out_stored")
        (d_t1, d_xt, d_q, d_qm, d_qe, d_qphi, d_at, d_att, d_t2, d_attT, d_o, d_x1, d_t3, d_x1T) = [
            sig("d_" + n) for n in ("xn_transposed", "xn_t_ready", "q_ready", "qmin_ready", "qexp_ready", "qphi_ready",
                                    "attn_ready", "attn_normed", "attn_transposed", "attn_t_ready", "wo_ready",
                                    "x1_ready", "x1_transposed", "x1_t_ready")]
        d_f1, d_h, d_f2, d_xm, d_t4, d_xmT = [
            sig("d_" + n, k) for n, k in (("ff1_ready", 2), ("relu_ready", 2), ("ff2_ready", 1), ("xm_ready", 1),
                                          ("xm_transposed", 1), ("xm_t_ready", 1))]
        d_lg, d_nm, d_re, d_cb, d_ct, d_ctT, d_cb2 = [
            sig("d_" + n) for n in ("logits_ready", "logit_max_ready", "router_exp_ready", "combine_ready",
                                    "combine_transposed", "combine_t_ready", "combine_b2_ready")]
        d_eh, d_eg, d_ey, d_eu = [sig("d_" + n, EXP // 2) for n in ("expert_h_ready", "expert_gelu_ready",
                                                                   "expert_y_ready", "expert_y_used")]
        d_chain = sig("d_dve_chain", D_CHAIN)
        l_chain = sig("late_experts_chain", 2)
        b_sig = sig("block_base_moved")
        v_again = sig("v_dst_local_restored")

        def fence(eng):
            eng.sem_inc(s_fence, 1)

        def first_pass(eng, step):
            for b in range(4):
                step((b, b, 0))
            with eng.Fori(1, NB // 4) as i:
                for u in range(4):
                    step((i * 4 + u, u, i))
            for b in range(NB // 4 * 4, NB + 3):
                step((b, b % 4, b // 4))

        def back(place, k):
            b, r, q = place
            return b - k, (r - k) % 4, q - 1 if r < k else q

        def exists(place, k=0):
            b = place[0]
            return not isinstance(b, int) or 0 <= b - k < NB

        def pipeline(eng, front, step, last):
            front(0, 0, 0)
            step(0, 0, 0, dense=False, late=False)
            step(1, 1, 0, late=False)
            step(2, 0, 1)
            with eng.Fori(1, (NB - 3) // 2) as i:
                step(i * 2 + 1, 1, i)
                step(i * 2 + 2, 0, i + 1)
            step(NB - 2, 1, (NB - 3) // 2, masks_ahead=False)
            step(NB - 1, 0, (NB - 1) // 2, after=False, masks_ahead=False)
            last(NB - 1, 0, (NB - 1) // 2)

        def in_order(*parts):
            for stage in ORDER:
                for p in parts:
                    if stage in p:
                        p[stage]()

        def chunk_count(eng, block):
            return eng.value_load(ctl[0:1, bass.ds(block + P, 1)], min_val=0, max_val=NT // CH)

        def further_chunks(eng, more, body, counter):
            with eng.If(more > 0):
                with eng.Fori(0, more) as c:
                    k = eng.snap(counter, min_val=0, max_val=NB * NT // CH)
                    eng.drain().then_inc(v_meet, 1)
                    eng.wait_ge(v_meet, k * 10 + 5)
                    fence(eng)
                    body(k, c)
                    eng.drain().then_inc(v_meet, 1)
                    eng.wait_ge(v_meet, k * 10 + 10)
                    fence(eng)
                    eng.reg_add(counter, counter, 1)

        block = ctx.enter_context(nc.Block())

        @block.sync
        def _(sp):
            sp.dma_start(dn[:, :, :], dst_n).then_inc(s_dn, 16)

            def load_x_part(i):
                w = NB // XC
                sp.dma_start(xall[:, i * w:(i + 1) * w, :],
                             xpad[i * w * P:(i + 1) * w * P, :].rearrange("(b p) d -> p b d", p=P)).then_inc(s_xload[i], 16)

            load_x_part(0)
            load_x_part(1)
            sp.wait_ge(s_trng, 2)
            sp.dma_start(tile_rng[0].rearrange("(p c) -> p c", p=P), t_tmp[:, 0:TPP]).then_inc(s_rng_w, 16)
            sp.dma_start(tile_rng[1].rearrange("(p c) -> p c", p=P), t_tmp[:, TPP:2 * TPP]).then_inc(s_rng_w, 16)
            load_x_part(2)
            sp.wait_ge(s_rng_w, 32)
            sp.dma_start(t_max, tile_rng[0:1, :].broadcast_to([P, NT])).then_inc(s_rng_r, 16)
            sp.dma_start(t_min, tile_rng[1:2, :].broadcast_to([P, NT])).then_inc(s_rng_r, 16)
            for i in range(3, XC):
                load_x_part(i)
            sp.wait_ge(s_blk, 1)
            sp.dma_start(blk_rng[0], coli[:, 0]).then_inc(s_blk_w, 16)
            sp.dma_start(blk_rng[1], coli[:, 1]).then_inc(s_blk_w, 16)
            sp.wait_ge(s_blk_w, 32)
            sp.dma_start(ctl[0:1, :], blk_rng.rearrange("a b -> (a b)").unsqueeze(0)).then_inc(s_ctl, 16)

            sp.wait_ge(s_ctl, 16)
            counter = sp.alloc_register("v_count_sp")
            sp.reg_mov(counter, 0)

            def load_edges(s, place, G, extra=0):
                lo = sp.value_load(ctl[0:1, bass.ds(s, 1)], min_val=0, max_val=EDGES // P)
                tile = nc.s_assert_within(lo + extra, 0, NT - CH, skip_runtime_bounds_check_because=(
                    "a chunk starts at one of its block's tiles, before the padding"))
                sp.dma_start(src_i[:, place, :], src_t[:, bass.ds(tile, CH)]).then_inc(G["idx"][place], 16)
                sp.dma_start(dst_i[:, place, :], dst_t[:, bass.ds(tile, CH)]).then_inc(G["idx"][place], 16)

            def load(s, par, first=False):
                if not first:
                    sp.wait_ge(M["eb"][0], at(M["eb"], s - 2))
                    fence(sp)
                load_edges(s, par, M)

            for s in range(2):
                load(s, s, True)

            def store_rows(place):
                b, r, _ = place
                if exists(place):
                    sp.wait_ge(f_row[0], at(f_row, b))
                    fence(sp)
                    sp.dma_start(table[bass.ds(b * P, P), :], nrow[:, r, :]).then_inc(f_st[r], 16)
                    sp.dma_start(knode[bass.ds(b * P, P), :], krow[:, r, :]).then_inc(f_st[r], 16)

            first_pass(sp, store_rows)
            for r in range(4):
                sp.wait_ge(f_st[r], 32 * len(range(r, NB, 4)))
            def load_keys(s, par):
                sp.dma_start(kcur[:, par, :], knode[bass.ds(s * P, P), :]).then_inc(M["key"][par], 16)

            def load_own(s, par, first=False):
                if not first:
                    sp.wait_ge(M["agg"][0], at(M["agg"], s - 2))
                    fence(sp)
                sp.dma_start(own[:, par, :], table[bass.ds(s * P, P), :]).then_inc(M["own"][par], 16)

            def load_x(b, par):
                sp.dma_start(xd[:, par, 0, :], xpad[bass.ds(b * P, P), :]).then_inc(d_x[par], 16)
                sp.dma_start(xd[:, par, 1, :], table[bass.ds(b * P, P), 0:D]).then_inc(d_x[par], 16)

            def more(s, par):
                def body(k, c):
                    load_edges(s, 2, V, (c + 1) * CH)
                further_chunks(sp, chunk_count(sp, s), body, counter)

            def store(b):
                sp.wait_ge(d_eu[0], at(d_eu, b))
                fence(sp)
                sp.dma_start(out[bass.ds(b * P, P), :], res[:, :]).then_inc(d_out, 16)

            def step(s, par, late=True, ahead=True, nxt=True):
                if ahead:
                    load(s + 2, par)
                if late:
                    store(s - 2)
                more(s, par)
                if ahead:
                    load_keys(s + 2, par)
                    load_own(s + 2, par)
                if nxt:
                    sp.wait_ge(d_eu[0], at(d_eu, s - 1, 1))
                    fence(sp)
                    load_x(s + 1, 1 - par)

            for s in range(2):
                load_keys(s, s)
                load_own(s, s, True)
                load_x(s, s)
            step(0, 0, late=False, nxt=False)
            step(1, 1, late=False)
            step(2, 0)
            with sp.Fori(1, (NB - 3) // 2) as i:
                step(i * 2 + 1, 1)
                step(i * 2 + 2, 0)
            step(NB - 2, 1, ahead=False)
            step(NB - 1, 0, ahead=False, nxt=False)
            store(NB - 2)
            store(NB - 1)
            sp.wait_ge(d_out, 16 * NB)

        @block.gpsimd
        def _(pool):
            nc.gpsimd.iota(iota_i[:, :], pattern=[[1, NT]], base=0, channel_multiplier=0).then_inc(s_pool, 1)
            nc.gpsimd.iota(coli[:, 0:1], pattern=[[0, 1]], base=0, channel_multiplier=P).then_inc(s_pool, 1)
            nc.gpsimd.memset(identf[:, :], 0.0).then_inc(s_pool, 1)
            pool.wait_ge(s_pool, 3)
            nc.gpsimd.affine_select(out=identf[:, :], in_=identf[:, :], compare_op=ALU.not_equal, fill=1.0, base=0,
                                    pattern=[[-1, P]], channel_multiplier=1).then_inc(s_pool, 1)
            counter = pool.alloc_register("v_count_pool")
            pool.reg_mov(counter, 0)
            pool.wait_ge(s_ctl, 16)
            for r in range(4):
                pool.wait_ge(f_st[r], 32 * len(range(r, NB, 4)))
            pool.wait_ge(s_blk, 1)

            def gather_chunk(par, place, G, free=None):
                for g in range(NG):
                    if free is not None:
                        free((g * GT + GT + PT - 1) // PT)
                    for j in range(g * GT, (g + 1) * GT):
                        nc.gpsimd.indirect_dma_start(
                            out=rows[:, par, j, :], out_offset=None, in_=table,
                            in_offset=bass.IndirectOffsetOnAxis(ap=src_i[:, place, j:j + 1], axis=0),
                        ).then_inc(G["gat"][place][g], 16)

            def gather(s, par, h, first=False):
                pool.wait_ge(M["idx"][par], h * 32 + 32)
                fence(pool)

                def free(q):
                    pool.wait_ge(M["wu"][0], at(M["wu"], s - 2, q))
                    fence(pool)

                gather_chunk(par, par, M, None if first else free)

            def more(s, par):
                def body(k, c):
                    pool.wait_ge(V["idx"][2], k * 32 + 32)
                    fence(pool)
                    gather_chunk(par, 2, V)
                further_chunks(pool, chunk_count(pool, s), body, counter)

            gather(0, 0, 0, True)
            gather(1, 1, 0, True)
            with pool.Fori(0, (NB - 3) // 2) as i:
                more(i * 2, 0)
                gather(i * 2 + 2, 0, i + 1)
                more(i * 2 + 1, 1)
                gather(i * 2 + 3, 1, i + 1)
            more(NB - 3, 0)
            gather(NB - 1, 0, (NB - 1) // 2)
            more(NB - 2, 1)
            more(NB - 1, 0)

        @block.scalar
        def _(act):
            def load_weights(pairs, loaded):
                for dst, src in pairs:
                    full = tuple(slice(None) for _ in dst.shape)
                    act.dma_start(dst[full], src).then_inc(loaded, 16)

            load_weights(((s_wqk, wqk), (s_wkv, wkv), (fv, firstvec.broadcast_to([P, F_END])), (cv, colvec)), s_fload)
            act.wait_ge(s_rng_w, 32)
            load_weights(((rv, rowvec.broadcast_to([P, R_END])), (s_wq, wq), (s_wo, wo), (s_w1, w1), (s_w2, w2), (s_rw, rw),
                          (s_e1, ew1), (s_e2, ew2), (s_eb2, eb2)), s_wload)

            def f_step(place):
                b, r, _ = place
                if exists(place):
                    act.wait_ge(f_tr[0], at(f_tr, b))
                    nc.scalar.activation(xt0[:, r % 2, :], tr_ps[r % 2][:, 0:2 * P], ACT.Copy).then_inc(f_xt[0], 1)
                if exists(place, 2):
                    b, r, _ = back(place, 2)
                    act.wait_ge(f_qkb[0], at(f_qkb, b))
                    nc.scalar.activation(nrow[:, r, CQ:CQ + SM], qkb[:, r % 2, 0:SM], ACT.Tanh).then_inc(f_q[0], 1)
                    act.wait_ge(f_km[0], at(f_km, b))
                    nc.scalar.activation(km[:, r % 2, :], kb[:, r % 2, :], ACT.Relu, scale=-1.0).then_inc(f_kr[0], 1)
                    act.wait_ge(f_kr[0], at(f_kr, b))
                    nc.scalar.activation(km[:, r % 2, :], km[:, r % 2, :], ACT.Exp, scale=-1.0).then_inc(f_ke[0], 1)

            first_pass(act, f_step)

            counter = act.alloc_register("v_count_act")
            act.reg_mov(counter, 0)
            act.wait_ge(s_ctl, 16)

            def onehots(s, G, g):
                act.wait_ge(G["tr"][0], at(G["tr"], s, g + 1))
                nc.scalar.activation(onehot[:, g * GT:(g + 1) * GT, :], b_t[g % 2][:, :, :], ACT.Identity,
                                     bias=1.0, scale=1.0 / BIG).then_inc(G["oh"][0], 1)

            def weights(s, par, G, q, first=False):
                if q == 0:
                    act.wait_ge(G["eb"][0], at(G["eb"], s))
                    nc.scalar.activation(sm[:, par, 5:6], sm[:, par, 4:5], ACT.Exp).then_inc(G["es"][0], 1)
                if q >= RING:
                    act.wait_ge(G["wu"][0], at(G["wu"], s, q - RING + 1))
                elif not first:
                    act.wait_ge(G["wu"][0], at(G["wu"], s - 1, NP - RING + q + 1))
                for j in range(q * PT, (q + 1) * PT):
                    ins = nc.scalar.activation(wgt[:, j % (RING * PT), :], farm[:, par, j, :], ACT.Exp,
                                               bias=ebias[:, par, j:j + 1])
                ins.then_inc(G["w"][0], 1)

            def front_parts(f):
                return {f"e{g}": (lambda g=g: onehots(f, M, g)) for g in range(NG)}

            def weight_parts(s, par, first):
                return {f"w{q}": (lambda q=q: weights(s, par, M, q, first)) for q in range(NP)}

            flat2 = lambda t: t[:, :, :].rearrange("p a b -> p (a b)")

            def dense_parts(b):
                def evac(dst, src, ready, done):
                    act.wait_ge(ready[0], at(ready, b))
                    nc.scalar.activation(dst, src, ACT.Copy).then_inc(done[0], 1)

                def phi():
                    act.wait_ge(d_q[0], at(d_q, b))
                    for m in range(2):
                        ins = nc.scalar.activation(qm[:, m, :], b_d[1][:, m * P:(m + 1) * P], ACT.Relu,
                                                   bias=bqn[:, m:m + 1], scale=-1.0)
                    ins.then_inc(d_qm[0], 1)
                    act.wait_ge(d_qm[0], at(d_qm, b))
                    nc.scalar.activation(flat2(qm), flat2(qm), ACT.Exp, scale=-1.0).then_inc(d_qe[0], 1)

                def relu(half):
                    act.wait_ge(d_f1[0], at(d_f1, b, half + 1))
                    for m in range(4 * half, 4 * half + 4):
                        ins = nc.scalar.activation(hff[:, m, :], b_d[1 + half][:, m % 4 * P:(m % 4 + 1) * P], ACT.Relu,
                                                   bias=cv[:, V_FB1 + m:V_FB1 + m + 1])
                    ins.then_inc(d_h[0], 1)

                def router():
                    act.wait_ge(d_nm[0], at(d_nm, b))
                    nc.scalar.activation(rt[:, 0, :], b_d[0][:, 0:EXP], ACT.Exp, bias=rts[:, 0:1],
                                         accum_out=rts[:, 1:2]).then_inc(d_re[0], 1)

                def gelu(p):
                    act.wait_ge(d_eh[0], at(d_eh, b, p + 1))
                    for e in range(2):
                        for m in range(2):
                            c = V_EB1 + (2 * p + e) * 2 + m
                            ins = nc.scalar.activation(hex_[p][:, e, m, :],
                                                       b_d[1 + p % 2][:, (2 * e + m) * P:(2 * e + m + 1) * P],
                                                       ACT.Gelu, bias=cv[:, c:c + 1])
                    ins.then_inc(d_eg[0], 1)
                    if p == EXP // 2 - 1:
                        nc.scalar.activation(warm[:, :], identf[:, 0:1], ACT.Exp)

                turned = lambda ready, done: (lambda: evac(flat2(xt), b_d[0][:, 0:D], ready, done))
                return {
                    "xt": turned(d_t1, d_xt), "q": phi, "attT": turned(d_t2, d_attT), "x1T": turned(d_t3, d_x1T),
                    "f1a": lambda: relu(0), "f1b": lambda: relu(1), "xmT": turned(d_t4, d_xmT), "lg": router,
                    "h0": lambda: gelu(0), "h1": lambda: gelu(1), "h2": lambda: gelu(2), "h3": lambda: gelu(3),
                    "cT": lambda: evac(ct[:, :], b_c[0:EXP, 256:256 + P], d_ct, d_ctT),
                }

            def more(found, s, par):
                def body(k, c):
                    for g in range(NG):
                        onehots(k, V, g)
                    for q in range(NP):
                        weights(k, par, V, q, first=True)
                further_chunks(act, found[0], body, counter)

            def step(s, par, h, dense=True, late=True, after=True, masks_ahead=True):
                found = []
                in_order({"c": lambda: found.append(chunk_count(act, s))}, weight_parts(s, par, not dense), dense_parts(s - 1) if dense else {},
                         front_parts(s + 1) if after else {})
                more(found, s, par)

            pipeline(act, lambda s, par, h: in_order(front_parts(s)), step, lambda b, par, h: in_order(dense_parts(b)))

        @block.tensor
        def _(pe):
            pe.wait_ge(s_const, 1)
            pe.matmul(b_a[:, 0:2 * (P + 1)], zero[:, 0:P], zero, start=True, stop=False, skip_group_check=True)

            def f_transpose(place):
                b, r, _ = place
                pe.wait_ge(f_xn[0], at(f_xn, b))
                for c in range(2):
                    ins = pe.transpose(tr_ps[r % 2][:, c * P:(c + 1) * P], nrow[:, r, c * P:(c + 1) * P], identf[:, :])
                ins.then_inc(f_tr[0], 1)

            def f_products(place):
                b, r, _ = place
                pe.wait_ge(f_xt[0], at(f_xt, b))
                par = r % 2
                for c in range(2):
                    pe.matmul(kv_ps[par][:, :], xt0[:, par, c * P:(c + 1) * P], s_wkv[:, c, :], start=(c == 0), stop=(c == 1))
                for c in range(2):
                    ins = pe.matmul(qk_ps[par], xt0[:, par, c * P:(c + 1) * P], s_wqk[:, c, :], start=(c == 0), stop=(c == 1))
                ins.then_inc(f_kv[0], 1)

            def f_sum(place):
                b, r, _ = place
                n = LAST if isinstance(b, int) and b == NB - 1 else P
                pe.wait_ge(f_kphi[0], at(f_kphi, b))
                for c in range(2):
                    ins = pe.matmul(kva_ps[:, c, :], kphi[0:n, r % 2, c * P:(c + 1) * P], vaug[0:n, r % 2, c, :],
                                    start=False, stop=(n < P), skip_group_check=True)
                ins.then_inc(f_acc[0], 1)

            def f_step(place):
                for k, part in ((0, f_transpose), (3, f_sum), (1, f_products)):
                    if exists(place, k):
                        part(back(place, k))

            pe.wait_ge(s_fload, 16 * 4)
            first_pass(pe, f_step)
            pe.wait_ge(s_wload, 16 * 9)

            pe.wait_ge(s_kvm, 1)
            counter = pe.alloc_register("v_count_pe")
            pe.reg_mov(counter, 0)
            pe.wait_ge(s_ctl, 16)

            def turn_mask(s, par, G, g):
                pe.wait_ge(G["far"][0], at(G["far"], s, g + 1))
                if g >= 2:
                    pe.wait_ge(G["oh"][0], at(G["oh"], s, g - 1))
                for j in range(GT):
                    ins = pe.transpose(b_t[g % 2][:, j, :], farm[:, par, g * GT + j, :], identb[:, :])
                ins.then_inc(G["tr"][0], 1)

            def keys(s, par, G, g):
                pe.wait_ge(G["oh"][0], at(G["oh"], s, g + 1))
                if g >= 1:
                    pe.wait_ge(G["ku"][0], at(G["ku"], s, g))
                for j in range(GT):
                    for a in range(3):
                        ins = pe.matmul(b_s[:, j * SM:(j + 1) * SM], onehot[:, g * GT + j, :],
                                        kcur[:, par, a * SM:(a + 1) * SM], start=(a == 0), stop=(a == 2))
                ins.then_inc(G["ke"][0], 1)

            def turn_max(s, G):
                pe.wait_ge(G["mx"][0], at(G["mx"], s))
                pe.transpose(b_m[:, 0:P], mxr[:, :], identf[:, :]).then_inc(G["mt"][0], 1)

            def spread_max(s, G):
                pe.wait_ge(G["sh"][0], at(G["sh"], s))
                for j in range(CH):
                    ins = pe.matmul(b_m[:, P + 2 * j:P + 2 * j + 2], onehot[:, j, :], shift2[:, :], start=True, stop=True)
                ins.then_inc(G["me"][0], 1)

            def front_parts(f, par, h):
                def first_keys():
                    pe.wait_ge(M["key"][par], h * 16 + 16)
                    keys(f, par, M, 0)

                parts = {f"t{g}": (lambda g=g: turn_mask(f, par, M, g)) for g in range(NG)}
                parts.update({f"k{g}": (lambda g=g: keys(f, par, M, g)) for g in range(1, NG)})
                parts.update({"k0": first_keys, "mt": lambda: turn_max(f, M), "me": lambda: spread_max(f, M)})
                return parts

            def aggregate(s, par, G, q):
                pe.wait_ge(G["w"][0], at(G["w"], s, q + 1))
                for j in range(q * PT, (q + 1) * PT):
                    ins = pe.matmul(b_a[:, 0:AGG], wgt[:, j % (RING * PT), :], rows[:, par, j, 0:AGG],
                                    start=(j == 0), stop=(j == CH - 1))
                ins.then_inc(G["wu"][0], 1)

            def aggregate_parts(s, par, first, late):
                def first_group():
                    if not first:
                        pe.wait_ge(M["agg"][0], at(M["agg"], s - 1))
                    if late:
                        pe.wait_ge(d_eu[0], at(d_eu, s - 2, 3))
                    aggregate(s, par, M, 0)

                parts = {f"a{q}": (lambda q=q: aggregate(s, par, M, q)) for q in range(1, NP)}
                parts["a0"] = first_group
                return parts

            def expert_products(b, p):
                for e in range(2):
                    for m in range(2):
                        ins = pe.matmul(b_y[p][:, e * D:(e + 1) * D], hex_[p][:, e, m, :],
                                        s_e2[:, 2 * p + e, m, :], start=(m == 0), stop=(m == 1))
                ins.then_inc(d_ey[0], 1)

            def late_parts(b):
                def outputs(p):
                    if p == 2:
                        pe.wait_ge(d_eg[0], at(d_eg, b, p + 1))
                        pe.wait_ge(d_eu[0], at(d_eu, b, 2))
                    else:
                        pe.wait_ge(d_eg[0], at(d_eg, b, p + 1))
                    expert_products(b, p)

                return {"y2": lambda: outputs(2), "y3": lambda: outputs(3)}

            def dense_parts(b, par, h, merged, late):
                def transpose2(src, ready, done):
                    pe.wait_ge(*ready)
                    for c in range(2):
                        ins = pe.transpose(b_d[0][:, c * P:(c + 1) * P], src[:, c * P:(c + 1) * P], identf[:, :])
                    ins.then_inc(done[0], 1)

                def p_t1():
                    if not (isinstance(b, int) and b == 0):
                        pe.wait_ge(d_eu[0], at(d_eu, b - 1, 1))
                    transpose2(xd[:, par, 1, :], (d_x[par], h * 32 + 32), d_t1)

                def p_q():
                    pe.wait_ge(d_xt[0], at(d_xt, b))
                    for m in range(2):
                        for c in range(2):
                            ins = pe.matmul(b_d[1][:, m * P:(m + 1) * P], s_wq[:, c, m * P:(m + 1) * P], xt[:, c, :],
                                            start=(c == 0), stop=(c == 1))
                    ins.then_inc(d_q[0], 1)

                def p_att():
                    pe.wait_ge(d_qphi[0], at(d_qphi, b))
                    for c in range(2):
                        ins = pe.matmul(b_d[2][:, c * (P + 4):(c + 1) * (P + 4)], qm[:, c, :], kvm[:, c, :],
                                        start=True, stop=True)
                    ins.then_inc(d_at[0], 1)

                def p_t2():
                    if late:
                        pe.wait_ge(d_eu[0], at(d_eu, b - 1))
                    transpose2(att, (d_att[0], at(d_att, b)), d_t2)

                def p_o():
                    pe.wait_ge(d_attT[0], at(d_attT, b))
                    for c in range(2):
                        ins = pe.matmul(b_d[1][:, 0:D], xt[:, c, :], s_wo[:, c, :], start=(c == 0), stop=(c == 1))
                    ins.then_inc(d_o[0], 1)

                def p_t3():
                    transpose2(x1, (d_x1[0], at(d_x1, b)), d_t3)

                def p_f1(half):
                    if half == 0:
                        pe.wait_ge(d_x1T[0], at(d_x1T, b))
                    for m in range(4 * half, 4 * half + 4):
                        for c in range(2):
                            ins = pe.matmul(b_d[1 + half][:, m % 4 * P:(m % 4 + 1) * P], s_w1[:, c, m * P:(m + 1) * P],
                                            xt[:, c, :], start=(c == 0), stop=(c == 1))
                    ins.then_inc(d_f1[0], 1)

                def p_f2(half):
                    pe.wait_ge(d_h[0], at(d_h, b, half + 1))
                    for m in range(4 * half, 4 * half + 4):
                        ins = pe.matmul(b_d[0][:, 0:D], hff[:, m, :], s_w2[:, m, :], start=(m == 0), stop=(m == FC - 1))
                    if half == 1:
                        ins.then_inc(d_f2[0], 1)

                def p_t4():
                    transpose2(xm, (d_xm[0], at(d_xm, b)), d_t4)

                def p_logits():
                    pe.wait_ge(d_xmT[0], at(d_xmT, b))
                    for c in range(2):
                        ins = pe.matmul(b_d[0][:, 0:EXP], xt[:, c, :], s_rw[:, c, :], start=(c == 0), stop=(c == 1))
                    ins.then_inc(d_lg[0], 1)

                def hidden(p):
                    if p >= 2:
                        pe.wait_ge(d_eg[0], at(d_eg, b, p - 1))
                    for e in range(2):
                        for m in range(2):
                            for c in range(2):
                                ins = pe.matmul(b_d[1 + p % 2][:, (2 * e + m) * P:(2 * e + m + 1) * P],
                                                s_e1[:, 2 * p + e, c, m * P:(m + 1) * P], xt[:, c, :],
                                                start=(c == 0), stop=(c == 1))
                    ins.then_inc(d_eh[0], 1)

                def outputs(p):
                    pe.wait_ge(d_eg[0], at(d_eg, b, p + 1))
                    if p == 0:
                        pe.wait_ge(d_re[0], at(d_re, b))
                    else:
                        pe.wait_ge(M["agg"][0], at(M["agg"], merged))
                    expert_products(b, p)

                def p_ct():
                    pe.wait_ge(d_cb[0], at(d_cb, b))
                    pe.wait_ge(d_eg[0], at(d_eg, b, 3))
                    pe.transpose(b_c[0:EXP, 256:256 + P], rt[:, 1, :], identf[:, :]).then_inc(d_ct[0], 1)

                def p_b2():
                    pe.wait_ge(d_ctT[0], at(d_ctT, b))
                    pe.matmul(b_c[:, 0:D], ct[:, :], s_eb2[:, :], start=True, stop=True).then_inc(d_cb2[0], 1)

                parts = {f"h{p}": (lambda p=p: hidden(p)) for p in range(EXP // 2)}
                parts.update({f"y{p}": (lambda p=p: outputs(p)) for p in range(2)})
                parts.update({"xt": p_t1, "q": p_q, "att": p_att, "attT": p_t2, "o": p_o, "x1T": p_t3,
                              "f1a": lambda: p_f1(0), "f1b": lambda: p_f1(1), "f2a": lambda: p_f2(0), "f2b": lambda: p_f2(1), "xmT": p_t4, "lg": p_logits,
                              "cT": p_ct, "cb2": p_b2})
                return parts

            def more(found, s, par):
                def body(k, c):
                    for g in range(NG):
                        turn_mask(k, par, V, g)
                        if g >= 1:
                            keys(k, par, V, g - 1)
                    keys(k, par, V, NG - 1)
                    turn_max(k, V)
                    spread_max(k, V)
                    for q in range(NP):
                        aggregate(k, par, V, q)
                further_chunks(pe, found[0], body, counter)

            def step(s, par, h, dense=True, late=True, after=True, masks_ahead=True):
                found = []
                in_order({"c": lambda: found.append(chunk_count(pe, s))}, aggregate_parts(s, par, not dense, late), late_parts(s - 2) if late else {},
                         dense_parts(s - 1, 1 - par, h if par == 1 else h - 1, s, late) if dense else {},
                         front_parts(s + 1, 1 - par, h + 1 if par == 1 else h) if after else {})
                more(found, s, par)

            pipeline(pe, lambda s, par, h: in_order(front_parts(s, par, h)), step,
                     lambda b, par, h: in_order(late_parts(b - 1), dense_parts(b, par, h, b, True)))
            in_order(late_parts(NB - 1))

        @block.vector
        def _(dve):
            v = nc.vector
            _, _, link, _ = chain_of(dve, (s_set, 0), 0)
            v.memset(zero, 0.0).then_inc(s_const, 1)
            v.memset(vaug[:, :, :, P:P + 1], 1.0)
            v.memset(kvm[:, :, :], 0.0)
            v.memset(base[:, :], 0.0)

            def statistics(i):
                dve.wait_ge(s_xload[i], 16)
                for b in range(i * NB // XC, (i + 1) * NB // XC):
                    ins = v.bn_stats(st[:, b, :], xall[:, b, :])
                return ins

            dve.wait_ge(s_dn, 16)
            v.tensor_reduce(t_tmp[:, 0:TPP], dn[:, :, :], AX.X, ALU.max).then_inc(s_trng, 1)
            v.tensor_reduce(t_tmp[:, TPP:2 * TPP], dn[:, :, :], AX.X, ALU.min).then_inc(s_trng, 1)
            dve.wait_ge(s_pool, 4)
            v.tensor_copy(iota_b[:, :], iota_i[:, 0:P])
            v.tensor_copy(iota8[:, :], iota_i[:, 0:EXP])
            v.tensor_copy(identb[:, :], identf[:, :])
            v.tensor_copy(t_idx, iota_i[:, :])
            v.tensor_scalar(cols[:, 0:1], coli[:, 0:1], 1.0, None, ALU.mult)
            v.tensor_scalar(cols[:, 1:2], coli[:, 0:1], float(P - 1), None, ALU.add)
            link(v.tensor_scalar(chunk_steps[:, :], iota_i[:, 0:48], float(CH), float(CH), ALU.mult, ALU.add))
            for i in range(3):
                statistics(i)
            dve.wait_ge(s_rng_r, 32)
            link(v.tensor_scalar(t_tmp, t_idx, -1.0, float(NT), ALU.mult, ALU.add))
            link(v.scalar_tensor_tensor(t_tmp, t_max, cols[:, 0:1], t_tmp, ALU.is_ge, ALU.mult))
            link(v.tensor_reduce(cols[:, 2:3], t_tmp, AX.X, ALU.max))
            link(v.tensor_scalar(cols[:, 3:4], cols[:, 2:3], -1.0, float(NT), ALU.mult, ALU.add))
            link(v.tensor_scalar(t_tmp, t_idx, 1.0, None, ALU.add))
            link(v.scalar_tensor_tensor(t_tmp, t_min, cols[:, 1:2], t_tmp, ALU.is_le, ALU.mult))
            link(v.tensor_reduce(cols[:, 4:5], t_tmp, AX.X, ALU.max))
            link(v.tensor_scalar(cols[:, 3:4], cols[:, 3:4], float(EDGES // P), None, ALU.min))
            link(v.tensor_tensor(cols[:, 5:6], cols[:, 4:5], cols[:, 3:4], ALU.subtract))
            link(v.tensor_scalar(chunk_steps[:, :], chunk_steps[:, :], cols[:, 5:6], None, ALU.is_lt))
            link(v.tensor_reduce(cols[:, 6:7], chunk_steps[:, :], AX.X, ALU.add))
            v.tensor_copy(coli[:, 0:1], cols[:, 3:4])
            v.tensor_copy(coli[:, 1:2], cols[:, 6:7]).then_inc(s_blk, 1)

            link(v.memset(nrow[:, :, :], 0.0))
            v.memset(nrow[:, :, C1:C1 + 1], 1.0)
            for i in range(3, XC):
                ins = statistics(i)
            link(ins)
            mean, var, rstd, nmr, t1, t2 = [lnm[:, i, :] for i in range(6)]
            s_ = lambda i: st[:, :, i]
            v.tensor_tensor(t1, s_(1), s_(4), ALU.add)
            v.tensor_tensor(t2, s_(1), s_(4), ALU.subtract)
            link(v.tensor_tensor(var, s_(2), s_(5), ALU.add))
            v.tensor_scalar(mean, t1, 0.5, None, ALU.mult)
            link(v.tensor_tensor(t2, t2, t2, ALU.mult))
            link(v.tensor_scalar(t2, t2, 0.25, EPS, ALU.mult, ALU.add))
            link(v.scalar_tensor_tensor(var, var, 1.0 / D, t2, ALU.mult, ALU.add))

            def inv_sqrt(y, x, t):
                link(v.tensor_scalar(y.bitcast(I32), x.bitcast(I32), -0.5, float(0x5f3759df), ALU.mult, ALU.add))
                for _ in range(4):
                    link(v.tensor_tensor(t, y, y, ALU.mult))
                    link(v.tensor_tensor(t, t, x, ALU.mult))
                    link(v.tensor_scalar(t, t, -0.5, 1.5, ALU.mult, ALU.add))
                    link(v.tensor_tensor(y, y, t, ALU.mult))

            inv_sqrt(rstd, var, t1)
            link(v.scalar_tensor_tensor(nmr, mean, -1.0, rstd, ALU.mult, ALU.mult))
            dve.wait_ge(s_fload, 16 * 4)
            v.tensor_scalar(bqn[:, :], cv[:, V_BQ:V_BQ + 2], -1.0, None, ALU.mult)
            link(v.tensor_scalar(bq1[:, :], cv[:, V_BQ:V_BQ + 2], 1.0, None, ALU.add))

            def f_norm(place):
                b, r, q = place
                if not (isinstance(b, int) and b < 4):
                    dve.wait_ge(f_st[r], q * 32)
                v.tensor_scalar(nrow[:, r, 0:D], xall[:, b, :], rstd[:, bass.ds(b, 1)], nmr[:, bass.ds(b, 1)],
                                ALU.mult, ALU.add).then_inc(f_xn[0], 1)

            def f_rest(place):
                b, r, _ = place
                par = r % 2
                tick, wait, link, close = chain_of(dve, f_chain, b)
                dve.wait_ge(f_kv[0], at(f_kv, b))
                v.tensor_tensor(qkb[:, par, :], qk_ps[par], fv[:, R_BQK:R_BQK + 2 * SM], ALU.add).then_inc(f_qkb[0], 1)
                v.tensor_tensor(kb[:, par, :], kv_ps[par][:, 0:D], fv[:, R_BK:R_BK + D], ALU.add).then_inc(f_km[0], 1)
                dve.wait_ge(f_qkb[0], at(f_qkb, b))
                m = tick(v.tensor_scalar(kf, qkb[:, par, SM:2 * SM], 1.0 / 5.0, None, ALU.mult))
                wait(m)
                m = tick(v.tensor_copy(krow[:, r, 0:SM], kf))
                v.tensor_tensor(vaug[:, par, :, 0:P], kv_ps[par][:, D:2 * D].rearrange("p (c n) -> p c n", c=2),
                                fv[:, R_BV:R_BV + D].rearrange("p (c n) -> p c n", c=2), ALU.add)
                wait(m)
                link(v.tensor_tensor(kr[:, 0, :], kf, krow[:, r, 0:SM], ALU.subtract))
                link(v.tensor_copy(krow[:, r, SM:2 * SM], kr[:, 0, :]))
                link(v.tensor_tensor(kr[:, 1, :], kr[:, 0, :], krow[:, r, SM:2 * SM], ALU.subtract))
                v.tensor_copy(krow[:, r, 2 * SM:3 * SM], kr[:, 1, :])
                dve.wait_ge(f_q[0], at(f_q, b))
                link(v.tensor_tensor(qkp[:, :], nrow[:, r, CQ:CQ + SM], kf[:, :], ALU.mult))
                v.tensor_reduce(nrow[:, r, CW:CW + 1], qkp[:, :], AX.X, ALU.add).then_inc(f_row[0], 1)
                dve.wait_ge(f_ke[0], at(f_ke, b))
                v.scalar_tensor_tensor(kphi[:, par, :], kb[:, par, :], 1.0, km[:, par, :], ALU.add,
                                       ALU.max).then_inc(f_kphi[0], 1)
                close()

            def f_step(place):
                if exists(place):
                    f_norm(place)
                if exists(place, 2):
                    f_rest(back(place, 2))

            first_pass(dve, f_step)
            dve.wait_ge(s_wload, 16 * 9)

            dve.wait_ge(f_acc[0], at(f_acc, NB - 1))
            for c in range(2):
                for q in range(4):
                    r = slice(HD * q, HD * (q + 1))
                    v.tensor_copy(kvm[r, c, r], kva_ps[r, c, r])
                    ins = v.tensor_copy(kvm[r, c, P + q:P + q + 1], kva_ps[r, c, P:P + 1])
            ins.then_inc(s_kvm, 1)
            dve.wait_ge(s_kvm, 1)

            counter = dve.alloc_register("v_count_dve")
            dve.reg_mov(counter, 0)
            dve.wait_ge(s_ctl, 16)

            def masks(s, par, place, seen, G, replaced=None, groups=range(NG)):
                if groups[0] == 0:
                    _, _, link, close = chain_of(dve, G["loc"], s)
                    dve.wait_ge(G["idx"][place], seen)
                    if G is M and not (isinstance(s, int) and s == 0):
                        dve.wait_ge(M["far"][0], at(M["far"], s - 1))
                    b = 0 if G is M else 1
                    link(v.tensor_scalar(dloc[:, :], dst_i[:, place, :], base[:, b:b + 1], None, ALU.subtract))
                    link(v.tensor_scalar(base[:, b:b + 1], base[:, b:b + 1], float(P) if G is M else 0.0, None, ALU.add))
                    close()
                for g in groups:
                    if replaced is not None:
                        dve.wait_ge(M["w"][0], at(M["w"], replaced, (g * GT + GT + PT - 1) // PT))
                    for j in range(g * GT, (g + 1) * GT):
                        ins = one_mask(par, j)
                        if j == (g + 1) * GT - 1:
                            ins.then_inc(G["far"][0], 1)
                        yield

            def one_mask(par, j):
                return v.tensor_scalar(farm[:, par, j, :], iota_b[:, :], dloc[:, j:j + 1], -BIG, ALU.not_equal, ALU.mult)

            def finish(mask):
                for _ in mask:
                    pass

            def graph_front(s, par, place, h, G, start_cols, own_loaded=None):
                tick, wait, link, close = chain_of(dve, G["chain"], s)
                c = lambda i: sm[:, par, i:i + 1]

                def scores(g):
                    dve.wait_ge(G["ke"][0], at(G["ke"], s, g + 1))
                    dve.wait_ge(G["gat"][place][g], h * (GT * 16) + GT * 16)
                    v.tensor_tensor(prod, b_s[:, 0:GT * SM].rearrange("p (t k) -> p t k", t=GT),
                                    rows[:, par, g * GT:(g + 1) * GT, CQ:CQ + SM], ALU.mult).then_inc(G["ku"][0], 1)
                    dve.wait_ge(G["ku"][0], at(G["ku"], s, g + 1))
                    link(v.tensor_reduce(score[:, g * GT:(g + 1) * GT], prod, AX.X, ALU.add))
                    for j in range(g * GT, (g + 1) * GT):
                        k = j % GT
                        if g == 0:
                            ins = v.tensor_scalar(mx[:, k, :], farm[:, par, j, :], score[:, j:j + 1], None, ALU.add)
                        else:
                            ins = v.scalar_tensor_tensor(mx[:, k, :], farm[:, par, j, :], score[:, j:j + 1], mx[:, k, :],
                                                         ALU.add, ALU.max)
                    tick(ins)

                def greatest():
                    wait()
                    v.tensor_reduce(mxr[:, :], mx[:, :, :].rearrange("p k n -> p n k"), AX.X, ALU.max).then_inc(G["mx"][0], 1)

                def shift():
                    if own_loaded is not None:
                        dve.wait_ge(own_loaded, h * 16 + 16)
                    dve.wait_ge(G["mt"][0], at(G["mt"], s))
                    link(v.tensor_reduce(c(0), b_m[:, 0:P], AX.X, ALU.max))
                    link(v.tensor_tensor(c(1), c(0), start_cols, ALU.max))
                    link(v.tensor_copy(shift2[:, 0:1], c(1)))
                    link(v.tensor_tensor(c(2), c(1), shift2[:, 0:1], ALU.subtract))
                    v.tensor_copy(shift2[:, 1:2], c(2)).then_inc(G["sh"][0], 1)
                    dve.wait_ge(G["sh"][0], at(G["sh"], s))
                    link(v.tensor_tensor(c(3), shift2[:, 0:1], shift2[:, 1:2], ALU.add))
                    tick(v.tensor_tensor(c(4), start_cols, c(3), ALU.subtract))

                def bias():
                    dve.wait_ge(G["me"][0], at(G["me"], s))
                    spread = b_m[:, P:P + 2 * CH].rearrange("p (j a) -> p j a", a=2)
                    link(v.tensor_tensor(ebias[:, par, :], score[:, :], spread[:, :, 0], ALU.subtract))
                    v.tensor_tensor(ebias[:, par, :], ebias[:, par, :], spread[:, :, 1], ALU.subtract).then_inc(G["eb"][0], 1)
                    close()

                parts = {f"k{g}": (lambda g=g: scores(g)) for g in range(NG)}
                parts.update({"mx": greatest, "mt": shift, "me": bias})
                return parts

            def graph_merge(s, par, G, old):
                dve.wait_ge(G["wu"][0], at(G["wu"], s))
                dve.wait_ge(G["es"][0], at(G["es"], s))
                v.tensor_copy(sm[:, par, 6:7], sm[:, par, 3:4])
                v.scalar_tensor_tensor(acc[:, par, :], old, sm[:, par, 5:6], b_a[:, 0:AGG], ALU.mult,
                                       ALU.add).then_inc(G["agg"][0], 1)

            def front(s, par, h):
                return graph_front(s, par, par, h, M, own[:, par, CW:CW + 1], M["own"][par])

            def more(found, s, par, restore):
                def body(k, c):
                    finish(masks(k, par, 2, k * 32 + 32, V))
                    in_order(graph_front(k, par, 2, k, V, sm[:, par, 6:7]))
                    graph_merge(k, par, V, acc[:, par, :])
                    if restore:
                        dve.wait_ge(V["agg"][0], at(V["agg"], k))
                        v.tensor_scalar(dloc[:, :], dst_i[:, par, :], base[:, 1:2], -2.0 * P, ALU.subtract,
                                        ALU.add).then_inc(v_again[0], 1)
                        dve.wait_ge(v_again[0], at(v_again, k))
                        for j in range(CH):
                            one_mask(par, j)
                further_chunks(dve, found[0], body, counter)
                dve.wait_ge(M["agg"][0], at(M["agg"], s))
                v.tensor_scalar(base[:, 1:2], base[:, 1:2], float(P), None, ALU.add).then_inc(b_sig[0], 1)
                dve.wait_ge(b_sig[0], at(b_sig, s))

            def layer_norm(tick, wait, link, src, k, mid=None, g=None):
                s6, r, t = lns[:, k, 0:6], lns[:, k, 8:9], lns[:, k, 9:10]
                link(v.bn_stats(s6, src), hold=True)
                link(v.bn_aggr(lns[:, k, 6:8], s6))
                x = lns[:, k, 7:8]
                n = tick(v.tensor_scalar(x, x, 2.0 ** 26, EPS * 2.0 ** 26, ALU.mult, ALU.add))
                if mid is not None:
                    tick(v.scalar_tensor_tensor(mid, src, lns[:, k, 6:7], g, ALU.subtract, ALU.mult))
                wait(n)
                link(v.tensor_scalar(r.bitcast(I32), x.bitcast(I32), -0.5, float(0x5f3759df - 2 ** 31), ALU.mult, ALU.add))
                for factor in (1.0, 2.0, 16.0):
                    link(v.tensor_scalar(t, r, r, x, ALU.mult, ALU.mult))
                    link(v.scalar_tensor_tensor(r, t, -3.0 * factor * factor, r, ALU.add, ALU.mult))
                return lns[:, k, 6:7], r

            def add_experts(b, p, link):
                dve.wait_ge(d_ey[0], at(d_ey, b, p + 1))
                for e in range(2):
                    i = 2 * p + e
                    dst = res[:, :] if i == EXP - 1 else xr
                    ins = v.scalar_tensor_tensor(dst, b_y[p][:, e * D:(e + 1) * D], rt[:, 1, i:i + 1], xr, ALU.mult, ALU.add)
                    if e == 0:
                        link(ins)
                ins.then_inc(d_eu[0], 1)
                dve.wait_ge(d_eu[0], at(d_eu, b, p + 1))

            def late_parts(b):
                _, _, link, close = chain_of(dve, l_chain, b)

                def add_last():
                    if not (isinstance(b, int) and b == 0):
                        dve.wait_ge(d_out, b * 16)
                    add_experts(b, 3, link)
                    close()

                return {"s2": lambda: add_experts(b, 2, link), "s3": add_last}

            def dense_parts(b, par, h, rest, mask):
                tick, wait, link, close = chain_of(dve, d_chain, b, lambda: fence(dve))

                def link_mask(ins, hold=False):
                    tick(ins)
                    next(mask, None)
                    wait()
                    if hold:
                        fence(dve)

                def link_rest(ins, hold=False):
                    tick(ins)
                    next(rest, None)
                    wait()
                    if hold:
                        fence(dve)

                def q_phi():
                    dve.wait_ge(d_qe[0], at(d_qe, b))
                    for m in range(2):
                        ins = v.scalar_tensor_tensor(qm[:, m, :], b_d[1][:, m * P:(m + 1) * P], bq1[:, m:m + 1], qm[:, m, :],
                                                     ALU.add, ALU.max)
                    ins.then_inc(d_qphi[0], 1)

                def attention():
                    dve.wait_ge(d_at[0], at(d_at, b))
                    num = b_d[2][:, 0:2 * (P + 4)].rearrange("p (c n) -> p c n", c=2)
                    link(v.tensor_scalar(den[:, 0, :].rearrange("p (c h) -> p c h", c=2), num[:, :, P:P + 4], 1e-6,
                                         None, ALU.add))
                    link(v.reciprocal(den[:, 1, :], den[:, 0, :]))
                    for c in range(2):
                        ins = v.tensor_tensor(att[:, c * P:(c + 1) * P].rearrange("p (h d) -> p h d", h=4),
                                              num[:, c, 0:P].rearrange("p (h d) -> p h d", h=4),
                                              den[:, 1, 4 * c:4 * c + 4].unsqueeze(2).broadcast_to([P, 4, HD]), ALU.mult)
                    ins.then_inc(d_att[0], 1)
                    dve.wait_ge(d_x[par], h * 32 + 32)
                    tick(v.tensor_tensor(y1, xd[:, par, 1, :], rv[:, R_BO:R_BO + D], ALU.add))

                def norm_1():
                    dve.wait_ge(d_o[0], at(d_o, b))
                    link_rest(v.tensor_tensor(y1, b_d[1][:, 0:D], y1, ALU.add))
                    _, r = layer_norm(tick, wait, link_rest, y1, 0, x1, rv[:, R_G1:R_G1 + D])
                    v.scalar_tensor_tensor(x1, x1, r, rv[:, R_B1:R_B1 + D], ALU.mult, ALU.add).then_inc(d_x1[0], 1)
                    dve.wait_ge(d_x1[0], at(d_x1, b))
                    finish(rest)
                    tick(v.tensor_tensor(y1, x1, rv[:, R_F2:R_F2 + D], ALU.add))
                    link(v.reciprocal(rl[:, :], acc[:, par, D:D + 1]))
                    link(v.scalar_tensor_tensor(xr, acc[:, par, 0:D], rl[:, 0:1], xd[:, par, 0, :], ALU.mult, ALU.add))
                    tick(v.tensor_tensor(xr, xr, rv[:, R_B2:R_B2 + D], ALU.add))

                def norm_2_3():
                    dve.wait_ge(d_f2[0], at(d_f2, b))
                    link(v.tensor_tensor(y1, b_d[0][:, 0:D], y1, ALU.add))
                    _, r = layer_norm(tick, wait, link, y1, 1, x1, rv[:, R_G2:R_G2 + D])
                    link(v.scalar_tensor_tensor(xr, x1, r, xr, ALU.mult, ALU.add))
                    mean, r = layer_norm(tick, wait, link, xr, 2)
                    v.tensor_scalar(xm, xr, mean, r, ALU.subtract, ALU.mult).then_inc(d_xm[0], 1)
                    dve.wait_ge(d_xm[0], at(d_xm, b))
                    tick(v.tensor_tensor(xr, xr, xm, ALU.add))

                def logits():
                    dve.wait_ge(d_lg[0], at(d_lg, b))
                    v.tensor_reduce(rts[:, 0:1], b_d[0][:, 0:EXP], AX.X, ALU.max, negate=True).then_inc(d_nm[0], 1)

                def router():
                    dve.wait_ge(d_re[0], at(d_re, b))
                    link_mask(v.reciprocal(rts[:, 2:3], rts[:, 1:2]))
                    link_mask(v.tensor_scalar(rt[:, 2, :], rt[:, 0, :], rts[:, 2:3], None, ALU.mult), hold=True)
                    link_mask(v.max(rt[:, 3, :], rt[:, 2, :]), hold=True)
                    tick(v.max_index(ridx[:, :], rt[:, 3, :], rt[:, 2, :]))
                    link_mask(v.tensor_tensor(rts[:, 3:4], rt[:, 3, 0:1], rt[:, 3, 1:2], ALU.add))
                    link_mask(v.tensor_scalar(rts[:, 3:4], rts[:, 3:4], 1e-12, None, ALU.max))
                    link_mask(v.reciprocal(rts[:, 4:5], rts[:, 3:4]))
                    link_mask(v.tensor_scalar(rt[:, 3, 0:2], rt[:, 3, 0:2], rts[:, 4:5], None, ALU.mult))
                    link_mask(v.tensor_copy(rts[:, 5:7], ridx[:, 0:2]))
                    tick(v.tensor_scalar(rt[:, 0, :], iota8[:, :], rts[:, 5:6], rt[:, 3, 0:1], ALU.is_equal, ALU.mult))
                    link_mask(v.tensor_scalar(rt[:, 2, :], iota8[:, :], rts[:, 6:7], rt[:, 3, 1:2], ALU.is_equal, ALU.mult))
                    v.tensor_tensor(rt[:, 1, :], rt[:, 0, :], rt[:, 2, :], ALU.add).then_inc(d_cb[0], 1)
                    finish(mask)
                    dve.wait_ge(d_cb[0], at(d_cb, b))

                def add_early(p):
                    add_experts(b, p, link)
                    if p == 1:
                        close()

                def add_b2():
                    dve.wait_ge(d_cb2[0], at(d_cb2, b))
                    link(v.tensor_tensor(xr, b_c[:, 0:D], xr, ALU.add))

                parts = {f"s{p}": (lambda p=p: add_early(p)) for p in range(2)}
                parts.update({"qphi": q_phi, "att": attention, "o": norm_1, "f2b": norm_2_3, "lg": logits,
                              "rt": router, "cb2": add_b2})
                return parts

            def front_alone(s, par, h):
                finish(masks(0, 0, 0, 32, M))
                finish(masks(1, 1, 1, 32, M, None, range(NG - LATE)))
                in_order(front(s, par, h))

            def step(s, par, h, dense=True, late=True, after=True, masks_ahead=True):
                ahead = masks(s + 2, par, par, (h + 2) * 32, M, s, range(NG - LATE)) if masks_ahead else iter(())
                found = []

                rest = masks(s + 1, 1 - par, None, None, M, None, range(NG - LATE, NG)) if after else iter(())

                def some_masks():
                    for _ in range(2 * GT):
                        next(rest, None)

                extra = {"nb": some_masks, "c": lambda: found.append(chunk_count(dve, s))}
                merge = {"mg": lambda: graph_merge(s, par, M, own[:, par, 0:AGG])}
                scores = front(s + 1, 1 - par, h + 1 if par == 1 else h) if after else {}
                if dense:
                    in_order(dense_parts(s - 1, 1 - par, h if par == 1 else h - 1, rest, ahead), merge, scores,
                             late_parts(s - 2) if late else {}, extra)
                else:
                    finish(rest)
                    in_order(merge, scores, extra)
                    finish(ahead)
                more(found, s, par, masks_ahead)

            pipeline(dve, front_alone, step, lambda b, par, h: in_order(late_parts(b - 1), dense_parts(b, par, h, iter(()), iter(()))))
            in_order(late_parts(NB - 1))


def kernel(**inputs):
    import concourse.bacc as bacc
    from concourse.bass_utils import run_bass_kernel_spmd

    g = {k: np.asarray(a) for k, a in inputs.items()}
    halves = lambda w: np.ascontiguousarray(w.reshape(w.shape[0] // P, P, -1).transpose(1, 0, 2))
    column = lambda a: a.reshape(-1, P).T
    edges = np.full(NT * P - EDGES, FAR, g["dst"].dtype)
    dst = np.concatenate([g["dst"], edges])
    src = np.concatenate([g["src"], np.zeros_like(edges)])
    experts = lambda w: np.ascontiguousarray(w.reshape(EXP, 2, P, D).transpose(2, 0, 1, 3))
    arrays = {
        "xpad": np.concatenate([g["x"], np.zeros((NPAD - NODES, D), g["x"].dtype)]),
        "src_t": np.ascontiguousarray(src.reshape(NT, P).T),
        "dst_t": np.ascontiguousarray(dst.reshape(NT, P).T),
        "dst_n": dst.reshape(P, TPP, P),
        "rowvec": np.concatenate([g[k] for k in (
            "L0_mix_bo", "L0_mix_ln1_g", "L0_mix_ln1_b", "L0_mix_ln2_g", "L0_mix_ln2_b",
            "L0_mix_b2")])[None],
        "firstvec": np.concatenate([g[k] for k in ("L0_mix_bk", "L0_mix_bv", "L0_gnn_bq", "L0_gnn_bk")])[None],
        "colvec": np.ascontiguousarray(np.concatenate(
            [column(g["L0_mix_bq"]), column(g["L0_mix_b1"]), column(g["L0_ffn_b1"])], axis=1)),
        "wqk": halves(np.concatenate([g["L0_gnn_Wq"], g["L0_gnn_Wk"]], axis=1)),
        "wq": halves(g["L0_mix_Wq"]),
        "wkv": halves(np.concatenate([g["L0_mix_Wk"], g["L0_mix_Wv"]], axis=1)),
        "wo": halves(g["L0_mix_Wo"]),
        "w1": halves(g["L0_mix_W1"]),
        "w2": halves(g["L0_mix_W2"]),
        "rw": halves(np.ascontiguousarray(g["L0_ffn_router_w"].T)),
        "ew1": experts(g["L0_ffn_w1"]),
        "ew2": experts(g["L0_ffn_w2"]),
        "eb2": g["L0_ffn_b2"],
    }
    nc = bacc.Bacc("TRN2", target_bir_lowering=False, num_devices=1)
    args = [nc.dram_tensor(f"in_{k}", a.shape, mybir.dt.from_np(a.dtype), kind="ExternalInput").ap() for k, a in arrays.items()]
    out = nc.dram_tensor("out_0", (NPAD, D), F32, kind="ExternalOutput").ap()
    graph_block(nc, *args, out)
    r = run_bass_kernel_spmd(nc, [{f"in_{k}": a for k, a in arrays.items()}], core_ids=[0])
    return r.results[0]["out_0"][:NODES]
```
